# Optimizing a Trainium2 kernel written in Bass

```python
import numpy as np
import jax
import jax.numpy as jnp

def _softmax(x, axis=-1):
    return jax.nn.softmax(x, axis=axis)

def _gelu(x):
    return jax.nn.gelu(x, approximate=True)

def _silu(x):
    return jax.nn.silu(x)

def _sigmoid(x):
    return jax.nn.sigmoid(x)

def _layernorm(x, axis=-1, eps=1e-05):
    m = jnp.mean(x, axis=axis, keepdims=True)
    v = jnp.var(x, axis=axis, keepdims=True)
    return (x - m) / jnp.sqrt(v + eps)

def _scatter_add(tgt, idx, src, axis=0):
    return tgt.at[idx].add(src)

def _segment_sum(src, seg, n):
    return jax.ops.segment_sum(src, seg, n)
kernel_name = 'mk_hybrid_d1_jaxref_r8_d9deb3'

def setup_inputs(seed: int=0):
    np.random.seed(seed)
    _w = jnp.asarray

    def _L0_attn_a_setup():
        import jax, jax.numpy as jnp
        import numpy as np
        B, T, C, F = (8, 256, 128, 512)

        def _ln(x, g, b):
            m = jnp.mean(x, axis=-1, keepdims=True)
            v = jnp.mean((x - m) ** 2, axis=-1, keepdims=True)
            return (x - m) * jax.lax.rsqrt(v + 1e-05) * g + b

        def _shift(x):
            return jnp.pad(x, ((0, 0), (1, 0), (0, 0)))[:, :-1]

        def _wkv(w, u, k, v):
            kT = jnp.swapaxes(k, 0, 1)
            vT = jnp.swapaxes(v, 0, 1)
            b, c = (k.shape[0], k.shape[2])
            aa = jnp.zeros((b, c), k.dtype)
            bb = jnp.zeros((b, c), k.dtype)
            pp = jnp.full((b, c), -1e+38, k.dtype)

            def step(carry, kv_t):
                aa, bb, pp = carry
                kt, vt = kv_t
                ww = u + kt
                p = jnp.maximum(pp, ww)
                e1 = jnp.exp(pp - p)
                e2 = jnp.exp(ww - p)
                out = (e1 * aa + e2 * vt) / (e1 * bb + e2)
                ww2 = pp + w
                p2 = jnp.maximum(ww2, kt)
                e1 = jnp.exp(ww2 - p2)
                e2 = jnp.exp(kt - p2)
                return ((e1 * aa + e2 * vt, e1 * bb + e2, p2), out)
            _, outs = jax.lax.scan(step, (aa, bb, pp), (kT, vT))
            return jnp.swapaxes(outs, 0, 1)
        key = jax.random.key(seed)
        ks = jax.random.split(key, 16)
        s = 1.0 / np.sqrt(C)
        inp = {'x': jax.random.normal(ks[0], (B, T, C), jnp.float32), 'ln0_g': jnp.ones((C,), jnp.float32), 'ln0_b': jnp.zeros((C,), jnp.float32), 'ln1_g': jnp.ones((C,), jnp.float32), 'ln1_b': jnp.zeros((C,), jnp.float32), 'time_decay': jax.random.normal(ks[1], (C,), jnp.float32) * 0.5, 'time_first': jax.random.normal(ks[2], (C,), jnp.float32) * 0.5, 'tm_k': jax.random.uniform(ks[3], (C,), jnp.float32), 'tm_v': jax.random.uniform(ks[4], (C,), jnp.float32), 'tm_r': jax.random.uniform(ks[5], (C,), jnp.float32), 'Wk': jax.random.normal(ks[6], (C, C), jnp.float32) * s, 'Wv': jax.random.normal(ks[7], (C, C), jnp.float32) * s, 'Wr': jax.random.normal(ks[8], (C, C), jnp.float32) * s, 'Wo': jax.random.normal(ks[9], (C, C), jnp.float32) * s, 'cm_k': jax.random.uniform(ks[10], (C,), jnp.float32), 'cm_r': jax.random.uniform(ks[11], (C,), jnp.float32), 'Wck': jax.random.normal(ks[12], (C, F), jnp.float32) * s, 'Wcv': jax.random.normal(ks[13], (F, C), jnp.float32) * (1.0 / np.sqrt(F)), 'Wcr': jax.random.normal(ks[14], (C, C), jnp.float32) * s}
        return inp
    _L0_attn_a_in = _L0_attn_a_setup()

    def _L0_attn_b_setup():
        import jax, jax.numpy as jnp
        import numpy as np
        GAMMA_MIN, GAMMA_MAX = (0.15, 1.0)
        ALPHA_CAP = 1.0
        EPS_L2 = 1e-08
        EPS_RMS = 1e-06

        def _rmsnorm(x, w):
            return x * jax.lax.rsqrt(jnp.mean(x * x, axis=-1, keepdims=True) + EPS_RMS) * w

        def _l2norm(x):
            n = jnp.linalg.norm(x, axis=-1, keepdims=True)
            return x / jnp.maximum(n, EPS_L2)

        def _causal_conv(h, kernel):
            K = kernel.shape[0]
            S = h.shape[1]
            hp = jnp.pad(h, ((0, 0), (K - 1, 0), (0, 0)))
            out = jnp.zeros_like(h)
            for j in range(K):
                out = out + kernel[j] * hp[:, K - 1 - j:K - 1 - j + S, :]
            return out
        B, S, D, R, K = (8, 128, 128, 16, 4)
        key = jax.random.key(seed)
        ks = jax.random.split(key, 8)
        return {'h': jax.random.normal(ks[0], (B, S, D), dtype=jnp.float32), 'u': jax.random.normal(ks[1], (D, R), dtype=jnp.float32) * 0.05, 'v': jax.random.normal(ks[2], (D, R), dtype=jnp.float32) * 0.05, 'decay_logit': jnp.zeros((R,), jnp.float32), 'alpha_logit': jnp.zeros((R,), jnp.float32), 'k_base_gate_logit': jnp.float32(0.0), 'k_base_kernel': jax.random.normal(ks[3], (K,), dtype=jnp.float32) * 0.05, 'proj_w': jax.random.normal(ks[4], (D, D), dtype=jnp.float32) * 0.02, 'proj_b': jnp.zeros((D,), jnp.float32), 'norm1_w': jnp.ones((D,), jnp.float32), 'norm2_w': jnp.ones((D,), jnp.float32), 'mlp_w1': jax.random.normal(ks[5], (D, 4 * D), dtype=jnp.float32) * 0.02, 'mlp_b1': jnp.zeros((4 * D,), jnp.float32), 'mlp_w2': jax.random.normal(ks[6], (4 * D, D), dtype=jnp.float32) * 0.02, 'mlp_b2': jnp.zeros((D,), jnp.float32)}
    _L0_attn_b_in = _L0_attn_b_setup()

    def _L0_ffn_setup():
        import jax, jax.numpy as jnp
        import numpy as np
        B, S, D, DOUT, E = (2, 256, 128, 128, 8)
        DH = 4 * D
        key = jax.random.key(seed)
        ks = jax.random.split(key, 7)
        sc = lambda *sh: 1.0 / np.sqrt(sh[-2]) if len(sh) >= 2 else 0.02
        return {'x': jax.random.normal(ks[0], (B, S, D), jnp.float32), 'Wg': jax.random.normal(ks[1], (D, E), jnp.float32) / np.sqrt(D), 'bg': jnp.zeros((E,), jnp.float32), 'W1': jax.random.normal(ks[2], (E, D, DH), jnp.float32) / np.sqrt(D), 'b1': jax.random.normal(ks[3], (E, DH), jnp.float32) * 0.02, 'W2': jax.random.normal(ks[4], (E, DH, DOUT), jnp.float32) / np.sqrt(DH), 'b2': jax.random.normal(ks[5], (E, DOUT), jnp.float32) * 0.02}
    _L0_ffn_in = _L0_ffn_setup()
    _d = {'L0_attn_a_x': _L0_attn_a_in['x'], 'L0_attn_a_ln0_g': _L0_attn_a_in['ln0_g'], 'L0_attn_a_ln0_b': _L0_attn_a_in['ln0_b'], 'L0_attn_a_ln1_g': _L0_attn_a_in['ln1_g'], 'L0_attn_a_ln1_b': _L0_attn_a_in['ln1_b'], 'L0_attn_a_time_decay': _L0_attn_a_in['time_decay'], 'L0_attn_a_time_first': _L0_attn_a_in['time_first'], 'L0_attn_a_tm_k': _L0_attn_a_in['tm_k'], 'L0_attn_a_tm_v': _L0_attn_a_in['tm_v'], 'L0_attn_a_tm_r': _L0_attn_a_in['tm_r'], 'L0_attn_a_Wk': _L0_attn_a_in['Wk'], 'L0_attn_a_Wv': _L0_attn_a_in['Wv'], 'L0_attn_a_Wr': _L0_attn_a_in['Wr'], 'L0_attn_a_Wo': _L0_attn_a_in['Wo'], 'L0_attn_a_cm_k': _L0_attn_a_in['cm_k'], 'L0_attn_a_cm_r': _L0_attn_a_in['cm_r'], 'L0_attn_a_Wck': _L0_attn_a_in['Wck'], 'L0_attn_a_Wcv': _L0_attn_a_in['Wcv'], 'L0_attn_a_Wcr': _L0_attn_a_in['Wcr'], 'L0_attn_b_u': _L0_attn_b_in['u'], 'L0_attn_b_v': _L0_attn_b_in['v'], 'L0_attn_b_decay_logit': _L0_attn_b_in['decay_logit'], 'L0_attn_b_alpha_logit': _L0_attn_b_in['alpha_logit'], 'L0_attn_b_k_base_gate_logit': _L0_attn_b_in['k_base_gate_logit'], 'L0_attn_b_k_base_kernel': _L0_attn_b_in['k_base_kernel'], 'L0_attn_b_proj_w': _L0_attn_b_in['proj_w'], 'L0_attn_b_proj_b': _L0_attn_b_in['proj_b'], 'L0_attn_b_norm1_w': _L0_attn_b_in['norm1_w'], 'L0_attn_b_norm2_w': _L0_attn_b_in['norm2_w'], 'L0_attn_b_mlp_w1': _L0_attn_b_in['mlp_w1'], 'L0_attn_b_mlp_b1': _L0_attn_b_in['mlp_b1'], 'L0_attn_b_mlp_w2': _L0_attn_b_in['mlp_w2'], 'L0_attn_b_mlp_b2': _L0_attn_b_in['mlp_b2'], 'L0_ffn_Wg': _L0_ffn_in['Wg'], 'L0_ffn_bg': _L0_ffn_in['bg'], 'L0_ffn_W1': _L0_ffn_in['W1'], 'L0_ffn_b1': _L0_ffn_in['b1'], 'L0_ffn_W2': _L0_ffn_in['W2'], 'L0_ffn_b2': _L0_ffn_in['b2']}
    _x0 = _d['L0_attn_a_x']
    _d['L0_attn_a_x'] = jax.random.normal(jax.random.fold_in(jax.random.key(seed), 1), (4, 1024, 128), dtype=_x0.dtype)
    del _x0
    return _d

def reference(L0_attn_a_x, L0_attn_a_ln0_g, L0_attn_a_ln0_b, L0_attn_a_ln1_g, L0_attn_a_ln1_b, L0_attn_a_time_decay, L0_attn_a_time_first, L0_attn_a_tm_k, L0_attn_a_tm_v, L0_attn_a_tm_r, L0_attn_a_Wk, L0_attn_a_Wv, L0_attn_a_Wr, L0_attn_a_Wo, L0_attn_a_cm_k, L0_attn_a_cm_r, L0_attn_a_Wck, L0_attn_a_Wcv, L0_attn_a_Wcr, L0_attn_b_u, L0_attn_b_v, L0_attn_b_decay_logit, L0_attn_b_alpha_logit, L0_attn_b_k_base_gate_logit, L0_attn_b_k_base_kernel, L0_attn_b_proj_w, L0_attn_b_proj_b, L0_attn_b_norm1_w, L0_attn_b_norm2_w, L0_attn_b_mlp_w1, L0_attn_b_mlp_b1, L0_attn_b_mlp_w2, L0_attn_b_mlp_b2, L0_ffn_Wg, L0_ffn_bg, L0_ffn_W1, L0_ffn_b1, L0_ffn_W2, L0_ffn_b2):

    def _L0_attn_a_ref(x, ln0_g, ln0_b, ln1_g, ln1_b, time_decay, time_first, tm_k, tm_v, tm_r, Wk, Wv, Wr, Wo, cm_k, cm_r, Wck, Wcv, Wcr):
        import jax, jax.numpy as jnp
        import numpy as np
        B, T, C, F = (8, 256, 128, 512)

        def _ln(x, g, b):
            m = jnp.mean(x, axis=-1, keepdims=True)
            v = jnp.mean((x - m) ** 2, axis=-1, keepdims=True)
            return (x - m) * jax.lax.rsqrt(v + 1e-05) * g + b

        def _shift(x):
            return jnp.pad(x, ((0, 0), (1, 0), (0, 0)))[:, :-1]

        def _wkv(w, u, k, v):
            kT = jnp.swapaxes(k, 0, 1)
            vT = jnp.swapaxes(v, 0, 1)
            b, c = (k.shape[0], k.shape[2])
            aa = jnp.zeros((b, c), k.dtype)
            bb = jnp.zeros((b, c), k.dtype)
            pp = jnp.full((b, c), -1e+38, k.dtype)

            def step(carry, kv_t):
                aa, bb, pp = carry
                kt, vt = kv_t
                ww = u + kt
                p = jnp.maximum(pp, ww)
                e1 = jnp.exp(pp - p)
                e2 = jnp.exp(ww - p)
                out = (e1 * aa + e2 * vt) / (e1 * bb + e2)
                ww2 = pp + w
                p2 = jnp.maximum(ww2, kt)
                e1 = jnp.exp(ww2 - p2)
                e2 = jnp.exp(kt - p2)
                return ((e1 * aa + e2 * vt, e1 * bb + e2, p2), out)
            _, outs = jax.lax.scan(step, (aa, bb, pp), (kT, vT))
            return jnp.swapaxes(outs, 0, 1)
        xa = _ln(x, ln0_g, ln0_b)
        xs = _shift(xa)
        k = (xa * tm_k + xs * (1.0 - tm_k)) @ Wk
        v = (xa * tm_v + xs * (1.0 - tm_v)) @ Wv
        r = jax.nn.sigmoid((xa * tm_r + xs * (1.0 - tm_r)) @ Wr)
        w = -jnp.exp(time_decay)
        wkv = _wkv(w, time_first, k, v)
        x = x + r * wkv @ Wo
        xc = _ln(x, ln1_g, ln1_b)
        xs = _shift(xc)
        kk = (xc * cm_k + xs * (1.0 - cm_k)) @ Wck
        kv = jnp.square(jax.nn.relu(kk)) @ Wcv
        rr = jax.nn.sigmoid((xc * cm_r + xs * (1.0 - cm_r)) @ Wcr)
        return x + rr * kv

    def _L0_attn_b_ref(h, u, v, decay_logit, alpha_logit, k_base_gate_logit, k_base_kernel, proj_w, proj_b, norm1_w, norm2_w, mlp_w1, mlp_b1, mlp_w2, mlp_b2):
        import jax, jax.numpy as jnp
        import numpy as np
        GAMMA_MIN, GAMMA_MAX = (0.15, 1.0)
        ALPHA_CAP = 1.0
        EPS_L2 = 1e-08
        EPS_RMS = 1e-06

        def _rmsnorm(x, w):
            return x * jax.lax.rsqrt(jnp.mean(x * x, axis=-1, keepdims=True) + EPS_RMS) * w

        def _l2norm(x):
            n = jnp.linalg.norm(x, axis=-1, keepdims=True)
            return x / jnp.maximum(n, EPS_L2)

        def _causal_conv(h, kernel):
            K = kernel.shape[0]
            S = h.shape[1]
            hp = jnp.pad(h, ((0, 0), (K - 1, 0), (0, 0)))
            out = jnp.zeros_like(h)
            for j in range(K):
                out = out + kernel[j] * hp[:, K - 1 - j:K - 1 - j + S, :]
            return out
        B, S, D = h.shape
        R = u.shape[1]
        residual = h
        h_norm = _rmsnorm(h, norm1_w)
        gate = jax.nn.sigmoid(k_base_gate_logit)
        out = gate * _causal_conv(h_norm, k_base_kernel)
        alpha = ALPHA_CAP * jax.nn.sigmoid(alpha_logit)
        qk = h_norm @ jnp.concatenate((u, v), axis=1)
        q_raw, k_raw = (qk[..., :R], qk[..., R:])
        q = _l2norm(q_raw)
        k = _l2norm(k_raw)
        gamma = jnp.clip(jax.nn.sigmoid(decay_logit), GAMMA_MIN, GAMMA_MAX)
        pos = jnp.arange(S, dtype=h.dtype)
        diff = jnp.maximum(pos[:, None] - pos[None, :], 0.0)
        mask = jnp.tril(jnp.ones((S, S), dtype=h.dtype))
        w = gamma[:, None, None] ** diff * mask
        q_alpha = q * alpha
        A = jnp.einsum('bir,bjr,rij->bij', q_alpha, k, w)
        decay_out = jnp.einsum('bij,bjd->bid', A, h_norm)
        out = out + decay_out
        out = out @ proj_w.T + proj_b
        h2 = residual + out
        hn2 = _rmsnorm(h2, norm2_w)
        mlp_out = jax.nn.gelu(hn2 @ mlp_w1 + mlp_b1) @ mlp_w2 + mlp_b2
        return h2 + mlp_out

    def _L0_ffn_ref(x, Wg, bg, W1, b1, W2, b2):
        import jax, jax.numpy as jnp
        import numpy as np
        B, S, D, DOUT, E = (2, 256, 128, 128, 8)
        DH = 4 * D
        Bb, Ss, Dd = x.shape
        xt = x.reshape(-1, Dd)
        gates = jax.nn.softmax(xt @ Wg + bg, axis=-1)
        sel = jnp.argmax(gates, axis=-1)
        nE = W1.shape[0]
        out = jnp.zeros((xt.shape[0], W2.shape[-1]), x.dtype)
        for e in range(nE):
            h = jax.nn.gelu(xt @ W1[e] + b1[e], approximate=False)
            ye = h @ W2[e] + b2[e]
            out = jnp.where((sel == e)[:, None], ye, out)
        return out.reshape(Bb, Ss, -1)
    x = L0_attn_a_x
    x = x + _L0_attn_a_ref(_layernorm(x, axis=-1), L0_attn_a_ln0_g, L0_attn_a_ln0_b, L0_attn_a_ln1_g, L0_attn_a_ln1_b, L0_attn_a_time_decay, L0_attn_a_time_first, L0_attn_a_tm_k, L0_attn_a_tm_v, L0_attn_a_tm_r, L0_attn_a_Wk, L0_attn_a_Wv, L0_attn_a_Wr, L0_attn_a_Wo, L0_attn_a_cm_k, L0_attn_a_cm_r, L0_attn_a_Wck, L0_attn_a_Wcv, L0_attn_a_Wcr)
    x = x + _L0_ffn_ref(_layernorm(x, axis=-1), L0_ffn_Wg, L0_ffn_bg, L0_ffn_W1, L0_ffn_b1, L0_ffn_W2, L0_ffn_b2)
    x = x + _L0_attn_b_ref(_layernorm(x, axis=-1), L0_attn_b_u, L0_attn_b_v, L0_attn_b_decay_logit, L0_attn_b_alpha_logit, L0_attn_b_k_base_gate_logit, L0_attn_b_k_base_kernel, L0_attn_b_proj_w, L0_attn_b_proj_b, L0_attn_b_norm1_w, L0_attn_b_norm2_w, L0_attn_b_mlp_w1, L0_attn_b_mlp_b1, L0_attn_b_mlp_w2, L0_attn_b_mlp_b2)
    x = x + _L0_ffn_ref(_layernorm(x, axis=-1), L0_ffn_Wg, L0_ffn_bg, L0_ffn_W1, L0_ffn_b1, L0_ffn_W2, L0_ffn_b2)
    return x

_drawn_inputs = setup_inputs


def setup_inputs(seed=0):
    import zlib

    import numpy as np

    out = dict(_drawn_inputs(seed))
    spreads = {'L0_attn_a_ln0_g': (1.0, 0.2),
     'L0_attn_a_ln0_b': (0.0, 0.1),
     'L0_attn_a_ln1_g': (1.0, 0.2),
     'L0_attn_a_ln1_b': (0.0, 0.1),
     'L0_attn_b_decay_logit': (0.0, 0.8),
     'L0_attn_b_alpha_logit': (0.0, 0.8),
     'L0_attn_b_proj_b': (0.0, 0.1),
     'L0_attn_b_norm1_w': (1.0, 0.6),
     'L0_attn_b_norm2_w': (1.0, 0.6),
     'L0_attn_b_mlp_b1': (0.0, 0.321),
     'L0_attn_b_mlp_b2': (0.0, 0.1),
     'L0_ffn_bg': (0.0, 0.1)}
    factors = {'L0_attn_b_k_base_kernel': 3.658, 'L0_ffn_b1': 2.751}
    for name, (base, spread) in spreads.items():
        noise = np.random.default_rng([zlib.crc32(name.encode()), seed]).standard_normal(out[name].shape)
        drawn = base * np.exp(spread * noise) if base else spread * noise
        out[name] = jnp.asarray(drawn.astype(out[name].dtype))
    for name, factor in factors.items():
        out[name] = (out[name] * factor).astype(out[name].dtype)
    return out
```

```python
from contextlib import ExitStack

import concourse.bass as bass
from concourse import mybir

ALU = mybir.AluOpType
ACT = mybir.ActivationFunctionType
AX_X = mybir.AxisListType.X
F32 = mybir.dt.float32
I32 = mybir.dt.int32
U32 = mybir.dt.uint32

P = 128
ROW = P + 4
MEAN, RSTD, ID = P, P + 1, P + 2
NB = 4
TB = 8
NT = NB * TB
NE = 8
HC = 4
EPS = 1e-5
NS = (NT * P + NE * (P - 1)) // P
U = 3
assert NS % U == 0


class Chain:

    def __init__(self, engine, sem):
        self.engine, self.sem, self.base, self.n = engine, sem, 0, 0

    def __call__(self, ins):
        self.n += 1
        ins.then_inc(self.sem, 1)
        self.engine.wait_ge(self.sem, self.base + self.n)

    def loop(self, i, per_turn, start):
        self.base, self.n = start + i * per_turn, 0

    def leave(self, turns, per_turn, start):
        assert self.n == per_turn, (self.n, per_turn)
        self.base, self.n = start + turns * per_turn, 0


def build(nc, D, out, phases):
    with ExitStack() as ctx:
        def sb(name, shape, dt=F32):
            return ctx.enter_context(nc.sbuf_tensor(name, shape, dt))

        credits = []

        def sem(name, credit=0):
            handle = ctx.enter_context(nc.semaphore(name))
            if credit:
                credits.append((handle, credit))
            return handle

        sorted_rows = [nc.dram_tensor(f"sorted_rows{f}", [NS * P, ROW], F32, kind="Internal").ap() for f in range(2)]
        x2_rows = nc.dram_tensor("x2_rows", [NT * P, P], F32, kind="Internal").ap()

        W1 = sb("W1", [P, NE, HC * P])
        W2 = sb("W2", [P, NE, HC, P])
        B1 = sb("B1", [P, NE, HC])
        B2 = sb("B2", [P, NE, P])
        Wg = sb("Wg", [P, NE])
        bg = sb("bg", [P, NE])
        ident = sb("ident", [P, P])
        ones = sb("ones", [P, P])
        before = sb("before", [P, P])
        expert_m8 = sb("expert_m8", [P, NE])
        slot_no = sb("slot_no", [P, NS])
        not_first = sb("not_first", [P, NE, NT])
        minus_half = sb("minus_half", [P, 2 * TB])
        eps_ln = sb("eps_ln", [P, TB])
        eps_rms = sb("eps_rms", [P, TB])
        fill = sb("fill", [P, ROW])
        col = {n: sb("c_" + n, [P, 1]) for n in (
            "ln0_g", "ln0_b", "ln1_g", "ln1_b", "time_decay", "time_first", "tm_k", "tm_v", "tm_r", "cm_k", "cm_r",
            "norm1_w", "norm2_w")}
        rest = {n: sb("r_" + n, [P, 1]) for n in ("tm_k", "tm_v", "tm_r", "cm_k", "cm_r")}
        decay = sb("decay", [P, 1])
        cg = sb("cg", [P, 1])
        cb = sb("cb", [P, 1])
        W_now = {n: sb("now_" + n, [P, P]) for n in ("k", "v", "r", "cr")}
        W_shift = {n: sb("shift_" + n, [P, P]) for n in ("k", "v", "r", "cr")}
        Wo = sb("Wo", [P, P])
        Wck = sb("Wck", [P, HC * P])
        Wcv = sb("Wcv", [P, HC, P])
        R = 16
        BLK = 32
        NBLK = P // BLK
        uv = sb("uv", [P, 2 * R])
        projT = sb("projT", [P, P])
        pb = sb("pb", [P, P])
        M1 = sb("M1", [P, HC * P])
        M2 = sb("M2", [P, HC, P])
        mb1 = sb("mb1", [P, HC])
        mb2 = sb("mb2", [P, P])
        g128 = sb("g128", [64, 1])
        G = sb("G", [P, 3, NBLK, R])
        causal = sb("causal", [P, P])
        conv = sb("conv", [P, P])
        conv_prev = sb("conv_prev", [P, 4])

        Xrow = sb("Xrow", [P, NT, ROW])
        posi = [sb(f"posi{f}", [P, NT], U32) for f in range(2)]
        texp = [sb(f"texp{f}", [P, NS], I32) for f in range(2)]

        ARENA = 31000
        arena = sb("arena", [P, ARENA])
        sizes = {}

        class Scratch:
            def __init__(self, name):
                self.name, self.at = name, 0

            def __call__(self, *dims, parts=P):
                n = 1
                for d in dims:
                    n *= d
                ap = arena[0:parts, self.at:self.at + n]
                self.at += n
                assert self.at <= ARENA, (self.name, self.at)
                if len(dims) > 1:
                    names = ["a", "b", "c", "d"][:len(dims)]
                    ap = ap.rearrange(f"p ({' '.join(names)}) -> p {' '.join(names)}", **dict(zip(names, dims)))
                return ap

        fs = Scratch("ffn")
        x_rows = fs(NS, ROW)
        y_rows = fs(NS, P)
        z8 = fs(TB, P)
        z8T = fs(TB * P)
        bst = fs(TB, 6)
        sm = fs(12, TB)
        lg = fs(NT, NE)
        eq = fs(NT, NE)
        top = fs(NT)
        oh = fs(NE, NT)
        run = fs(NE, NT)
        pos3 = fs(NE, NT)
        nti = fs(NE).bitcast(I32)
        ntf = fs(NE)
        endt = fs(NE)
        baset = fs(NE)
        posf = fs(NT)
        cmp_ = fs(NS, NE)
        texf = fs(NS)
        zs = [fs(P) for u in range(U)]
        zsT = [fs(P) for u in range(U)]
        w1cur = [fs(HC * P) for u in range(U)]
        hT = [fs(HC, P) for u in range(U)]

        bs = Scratch("attn_b")
        setup = sb("setup", [P, 1500])
        setup_at = [0]

        def su(*dims, parts=P):
            n = 1
            for d in dims:
                n *= d
            ap = setup[0:parts, setup_at[0]:setup_at[0] + n]
            setup_at[0] += n
            if len(dims) > 1:
                names = ["a", "b", "c"][:len(dims)]
                ap = ap.rearrange(f"p ({' '.join(names)}) -> p {' '.join(names)}", **dict(zip(names, dims)))
            return ap

        proj_in = su(P)
        dl = su(3, R)
        dcol = su(2, parts=64)
        cst = su(8)
        hundred28 = su(1, parts=64)
        expo = su(3, NBLK, R)
        gmask = su(3, NBLK, R)
        dist = su(P)
        ctmp = su(P)
        gam = su(3, NBLK, R)
        hn = bs(TB, P)
        hnT = bs(TB * P)
        qks = bs(TB, 2, R)
        sq = bs(TB, 2, R)
        n2 = bs(TB, 2)
        rn = bs(TB, 2)
        KQ = bs(TB, 2 * NBLK * R)
        kd = bs(TB, NBLK * R)
        kT = bs(TB * P, parts=64)
        qT = bs(TB * P, parts=64)
        AT = bs(TB, P)
        state = bs(TB, P, parts=64)
        oT = bs(TB * P)
        h2 = bs(TB, P)
        h2n = bs(TB, P)
        xh = bs(TB, P)
        h2T = bs(TB * P)
        hmT = bs(2, HC, 4 * P)
        bstb = bs(TB, 6)
        smb = bs(14, TB)

        as_ = Scratch("attn_a")
        L = TB * P
        wraw = as_(4, P)
        a8 = as_(TB, P)
        Y = as_(NT, P)
        xa = as_(1 + L)
        p_ = as_(1 + L)
        aa = as_(1 + L)
        bb = as_(1 + L)
        E1 = as_(L)
        E2 = as_(L)
        E3 = as_(L)
        E4 = as_(L)
        vs = as_(L)
        av = as_(L)
        num = as_(L)
        den = as_(L)
        y0 = as_(L)
        th = as_(L)
        rw = as_(L)
        x1 = as_(TB, P)
        x1n = as_(TB, P)
        xc = as_(1 + L)
        ca = as_(L)
        mk = as_(L)
        kkr = [as_(512) for _ in range(2)]
        kk2 = as_(HC, 512)
        th2 = as_(L)
        bsta = as_(TB, 6)
        sma = as_(14, TB)
        smx = as_(14, TB)

        ps = [ctx.enter_context(nc.psum_tensor(f"ps{i}", [P, 512], F32)) for i in range(8)]

        w_loaded = sem("w_loaded")
        w_loaded2 = sem("w_loaded2")
        x_loaded = [sem(f"x_loaded{b}") for b in range(NB)]
        consts = sem("consts")
        pool_own = sem("pool_own")
        tables = sem("tables")
        filled = sem("filled")
        credit = sem("credit")
        dve_own = sem("dve_own")
        act_own = sem("act_own")
        act_setup = sem("act_setup")
        gpow = sem("gpow")
        gexp = sem("gexp")
        proj_turned = sem("proj_turned")
        proj_ready = sem("proj_ready")
        out_written = sem("out_written")
        CR = {"zt_copied": 2, "logits_done": 1, "h_psum": U, "zsT_psum": U, "h_ready": U, "y_psum": U, "y_ready": 2,
              "zt_psum": 1}
        S = [{n: sem(f"{n}{f}", CR.get(n, 0)) for n in (
            "ve_ready", "rstd_ready", "z_ready", "zt_psum", "zt_copied", "logits_done",
            "onehot_ready", "ranks_done", "pos_ready", "rows_scattered", "zs_ready", "zsT_psum",
            "zsT_ready", "w1_ready", "h_psum", "h_ready", "y_psum", "y_ready",
            "y_scattered")} for f in range(2)]
        V = {n: sem(n + "_b", c) for n, c in (
            ("var_ready", 0), ("scale_ready", 0), ("hn_ready", 0), ("t1_psum", 0), ("hnT_ready", 0),
            ("qk_psum", 0), ("qk_copied", 0), ("n2_ready", 0), ("rn_ready", 0), ("kq_ready", 0),
            ("t2_psum", 0), ("kqT_ready", 0), ("u_psum", 0), ("state_ready", 0), ("at_psum", 0), ("at_ready", 0),
            ("o_psum", 1), ("oT_ready", 0), ("proj_psum", 0), ("h2_ready", 0), ("ms_ready", 0), ("s2_ready", 0),
            ("h2n_ready", 0), ("t3_psum", 1), ("h2T_ready", 0), ("xh_ready", 0),
            ("up_psum", 0), ("hm_ready", 2), ("down_psum", 2), ("x3_ready", 1), ("x3_half", 1))}
        x2_loaded = [sem(f"x2_loaded{b}") for b in range(NB)]
        A = {n: sem(n + "_a", c) for n, c in (
            ("var0_ready", 0), ("scale0_ready", 0), ("a8_ready", 0), ("t0_psum", 1), ("xa_ready", 0),
            ("k_psum", 0), ("v_psum", 0), ("r_psum", 0), ("v_copied", 0), ("r_tanh", 0), ("kv_used", 1),
            ("d12_ready", 0), ("s_ready", 0), ("e12_ready", 0), ("e34_ready", 0), ("av_ready", 0), ("e4v_ready", 0),
            ("scan_ready", 0), ("n1_ready", 0), ("num_ready", 0), ("den_ready", 0), ("y0_ready", 0), ("qt_ready", 0), ("rw_ready", 0),
            ("wo_psum", 1), ("x1_ready", 0), ("var1_ready", 0), ("scale1_ready", 0), ("x1n_ready", 0),
            ("t1_psum", 0), ("xc_ready", 0), ("mk_ready", 0), ("cr_psum", 0), ("ck_psum", 2), ("relu_ready", 2),
            ("kk_ready", 2), ("cv_psum", 2), ("th2_ready", 1), ("xx_ready", 0), ("x1_done", 1))}
        loads = [[sem(f"slot_load{f}_{u}") for u in range(U)] for f in range(2)]

        block = ctx.enter_context(nc.Block())

        vec = "(p a) -> p a"
        first_loads = [(col[n][:], D["attn_a_" + n].rearrange(vec, a=1)) for n in (
            "ln0_g", "ln0_b", "ln1_g", "ln1_b", "time_decay", "time_first", "tm_k", "tm_v", "tm_r", "cm_k", "cm_r")]
        first_loads += [(wraw[:, j, :], D["attn_a_" + n]) for j, n in enumerate(("Wk", "Wv", "Wr", "Wcr"))]
        first_loads += [
            (Wo[:], D["attn_a_Wo"]),
            (Wck[:], D["attn_a_Wck"]),
            (Wcv[:], D["attn_a_Wcv"].rearrange("(k p) c -> p k c", p=P)),
        ]
        second_loads = [(col[n][:], D["attn_b_" + n].rearrange(vec, a=1)) for n in ("norm1_w", "norm2_w")]
        second_loads += [
            (uv[:, 0:R], D["attn_b_u"]),
            (uv[:, R:2 * R], D["attn_b_v"]),
            (proj_in, D["attn_b_proj_w"]),
            (pb[:], D["attn_b_proj_b"].partition_broadcast(P)),
            (M1[:], D["attn_b_mlp_w1"]),
            (M2[:], D["attn_b_mlp_w2"].rearrange("(k p) c -> p k c", p=P)),
            (mb1[:], D["attn_b_mlp_b1"].rearrange("(k p) -> p k", p=P)),
            (mb2[:], D["attn_b_mlp_b2"].partition_broadcast(P)),
            (dl[:, 0, :], D["attn_b_decay_logit"].partition_broadcast(P)),
            (dl[:, 1, :], D["attn_b_alpha_logit"].partition_broadcast(P)),
            (cst[:, 0:4], D["attn_b_k_base_kernel"].partition_broadcast(P)),
            (cst[:, 4:5], D["attn_b_k_base_gate_logit"].partition_broadcast(P)),
        ]
        second_loads += [(dcol[R * g:R * g + R, 0:1], D["attn_b_decay_logit"].rearrange(vec, a=1)) for g in range(NBLK)]
        second_loads += [
            (Wg[:], D["ffn_Wg"]),
            (bg[:], D["ffn_bg"].partition_broadcast(P)),
            (B1[:], D["ffn_b1"].rearrange("e (k p) -> p e k", p=P)),
            (B2[:], D["ffn_b2"].partition_broadcast(P)),
            (W1[:], D["ffn_W1"].rearrange("e c h -> c e h")),
            (W2[:], D["ffn_W2"].rearrange("e (k p) d -> p e k d", p=P)),
        ]
        W_FIRST, W_SECOND = 16 * len(first_loads), 16 * len(second_loads)

        Y_BANK = [6, 7, 6]
        Y_BACK = 2
        last = {0: x2_rows, 1: out}
        if "B" not in phases:
            last[0] = out

        @block.sync
        def _(sp):
            for handle, count in credits:
                sp.sem_inc(handle, count)
            x_view = D["attn_a_x"].rearrange("b (t p) c -> b p t c", p=P)
            with nc.allow_non_contiguous_dma(reason="vectors onto partitions"):
                sp.dma_start(Xrow[:, 0:TB, 0:P], x_view[0]).then_inc(x_loaded[0], 16)
                for dst, src in first_loads:
                    sp.dma_start(dst, src).then_inc(w_loaded, 16)
                for b in range(1, NB):
                    sp.dma_start(Xrow[:, b * TB:(b + 1) * TB, 0:P], x_view[b]).then_inc(x_loaded[b], 16)
                for dst, src in second_loads:
                    sp.dma_start(dst, src).then_inc(w_loaded2, 16)
            sp.wait_ge(consts, 1)
            for f in range(2):
                sp.dma_start(sorted_rows[f].rearrange("(s p) w -> p s w", p=P),
                             fill[:].unsqueeze(1).to_broadcast([P, NS, ROW])).then_inc(filled, 16)

            def slot_loads(f):
                sp.wait_ge(S[f]["rows_scattered"], 16 * NT)
                view = sorted_rows[f].rearrange("(s p) w -> s p w", p=P)
                for u in range(U):
                    sp.dma_start(x_rows[:, u, :], view[u]).then_inc(loads[f][u], 16)
                with sp.Fori(1, NS // U) as i:
                    for u in range(U):
                        sp.wait_ge(loads[f][u], 16 * i)
                        s = i * U + u
                        sp.dma_start(x_rows[:, bass.ds(s, 1), :], view[bass.ds(s, 1)].rearrange("a p w -> p a w")).then_inc(loads[f][u], 16)

            def write_rows(done, n):
                sp.wait_ge(done, n)
                sp.dma_start(out.rearrange("(t p) c -> p t c", p=P), Xrow[:, :, 0:P]).then_inc(out_written, 16)
                sp.wait_ge(out_written, 16)

            if phases == "A":
                write_rows(A["x1_done"], NB + 1)
            if "F" in phases:
                slot_loads(0)
                sp.wait_ge(S[0]["y_scattered"], 16 * NS)
            if "B" in phases:
                for b in range(NB):
                    sp.wait_ge(x_loaded[b], 16)
                    sp.dma_start(Xrow[:, b * TB:(b + 1) * TB, 0:P],
                                 (x2_rows if "F" in phases else D["attn_a_x"].rearrange("b t c -> (b t) c")).rearrange("(b t p) c -> b p t c", p=P, t=TB)[b]).then_inc(x2_loaded[b], 16)
                if "G" not in phases:
                    write_rows(V["x3_half"], 2 * NB + 1)
            if "G" in phases:
                slot_loads(1)
                sp.wait_ge(S[1]["y_scattered"], 16 * NS)

        @block.gpsimd
        def _(pool):
            own = Chain(pool, pool_own)
            nc.gpsimd.memset(ident[:], 0.0)
            nc.gpsimd.memset(ones[:], 1.0)
            nc.gpsimd.memset(minus_half[:], -0.5)
            nc.gpsimd.memset(eps_ln[:], EPS)
            nc.gpsimd.memset(eps_rms[:], 1e-6)
            nc.gpsimd.memset(not_first[:], 1.0)
            nc.gpsimd.memset(hundred28[:], float(P))
            own(nc.gpsimd.memset(fill[:], 0.0))
            nc.gpsimd.memset(fill[:, ID:ID + 1].bitcast(I32), NT * P).then_inc(consts, 1)
            nc.gpsimd.affine_select(out=ident[:], in_=ident[:], compare_op=ALU.not_equal, fill=1.0, base=0,
                                    pattern=[[-1, P]], channel_multiplier=1).then_inc(consts, 1)
            for line in (xa, p_, aa, bb, xc):
                nc.gpsimd.memset(line[:, 0:1], -1e38 if line is p_ else 0.0)
            nc.gpsimd.affine_select(out=before[:], in_=ones[:], compare_op=ALU.is_gt, fill=0.0, base=0,
                                    pattern=[[1, P]], channel_multiplier=-1)
            nc.gpsimd.affine_select(out=causal[:], in_=ones[:], compare_op=ALU.is_ge, fill=0.0, base=0,
                                    pattern=[[1, P]], channel_multiplier=-1)
            nc.gpsimd.iota(expert_m8[:], [[1, NE]], base=-NE, channel_multiplier=0, allow_small_or_imprecise_dtypes=True)
            nc.gpsimd.iota(slot_no[:], [[1, NS]], base=0, channel_multiplier=0, allow_small_or_imprecise_dtypes=True)
            nc.gpsimd.iota(dist, [[1, P]], base=0, channel_multiplier=-1, allow_small_or_imprecise_dtypes=True)
            nc.gpsimd.iota(expo[:, 0], [[BLK, NBLK], [0, R]], base=0, channel_multiplier=-1, allow_small_or_imprecise_dtypes=True)
            nc.gpsimd.iota(expo[:, 1], [[-BLK, NBLK], [0, R]], base=0, channel_multiplier=1, allow_small_or_imprecise_dtypes=True)
            nc.gpsimd.iota(expo[:, 2], [[BLK, NBLK], [0, R]], base=P, channel_multiplier=-1, allow_small_or_imprecise_dtypes=True)
            nc.gpsimd.iota(Xrow[:, :, ID:ID + 1].rearrange("p t w -> p (t w)").bitcast(I32), [[P, NT]], base=0, channel_multiplier=1)
            nc.gpsimd.memset(Xrow[:, :, ID + 1:ROW], 0.0)
            nc.gpsimd.memset(not_first[:, :, 0:1], 0.0).then_inc(consts, 1)

            def rstd_chain(var, sems, n, sm_, second):
                pool.wait_ge(sems[0], n)
                own(nc.gpsimd.tensor_tensor(sm_[:, 7, :], var, eps_ln[:], ALU.add))
                ins = nc.gpsimd.tensor_tensor(sm_[:, 5, :], sm_[:, 7, :], minus_half[:, 0:TB], ALU.pow)
                if second is not None:
                    own(ins)
                    own(nc.gpsimd.tensor_tensor(sm_[:, 8, :], sm_[:, 5, :], sm_[:, 5, :], ALU.mult))
                    own(nc.gpsimd.tensor_tensor(sm_[:, 8, :], sm_[:, 8, :], var, ALU.mult))
                    own(nc.gpsimd.tensor_tensor(sm_[:, 8, :], sm_[:, 8, :], second[:], ALU.add))
                    own(nc.gpsimd.tensor_tensor(sm_[:, 9, :], sm_[:, 8, :], minus_half[:, 0:TB], ALU.pow))
                    own(nc.gpsimd.tensor_tensor(sm_[:, 7, :], sm_[:, 8, :], sm_[:, 9, :], ALU.mult))
                    ins = nc.gpsimd.tensor_tensor(sm_[:, 6, :], sm_[:, 5, :], sm_[:, 9, :], ALU.mult)
                ins.then_inc(sems[1], 1)

            def a_products(b, h):
                c = slice(512 * h, 512 * h + 512)
                pool.wait_ge(A["e12_ready"], 2 * b + h + 1)
                pool.wait_ge(A["v_copied"], b + 1)
                nc.gpsimd.tensor_tensor(av[:, c], E2[:, c], vs[:, c], ALU.mult).then_inc(A["av_ready"], 1)
                pool.wait_ge(A["e34_ready"], 2 * b + h + 1)
                own(nc.gpsimd.tensor_tensor(num[:, c], E4[:, c], vs[:, c], ALU.mult))

            def a_numerator(b, h):
                c = slice(512 * h, 512 * h + 512)
                pool.wait_ge(A["scan_ready"], 2 * b + h + 1)
                own(nc.gpsimd.tensor_tensor(av[:, c], E3[:, c], aa[:, c], ALU.mult))
                own(nc.gpsimd.tensor_tensor(num[:, c], num[:, c], av[:, c], ALU.add))

            def a_quotient(b):
                pool.wait_ge(A["y0_ready"], b + 1)
                nc.gpsimd.tensor_tensor(num, num, y0, ALU.mult)
                nc.gpsimd.tensor_tensor(den, den, y0, ALU.mult).then_inc(A["qt_ready"], 1)

            def a_squares(b, half):
                for k in range(HC):
                    pool.wait_ge(A["relu_ready"], b * (2 * HC) + half * HC + k + 1 + 2)
                    if k == 0:
                        pool.wait_ge(A["cv_psum"], 2 * b + half + 2)
                    nc.gpsimd.tensor_tensor(kk2[:, k, :], kkr[k % 2], kkr[k % 2], ALU.mult).then_inc(A["kk_ready"], 1)

            def a_streams(b):
                nc.gpsimd.tensor_tensor(x1, Xrow[:, bass.ts(b, TB), 0:P], x1, ALU.add).then_inc(A["xx_ready"], 1)

            def rstd0(b):
                rstd_chain(sma[:, 4, :], (A["var0_ready"], A["scale0_ready"]), b + 1, sma, eps_ln)

            def rstd1(b):
                rstd_chain(smx[:, 4, :], (A["var1_ready"], A["scale1_ready"]), b + 1, smx, None)

            if "A" in phases:
                rstd0(0)
                for h in range(2):
                    a_products(0, h)
                for h in range(2):
                    a_numerator(0, h)
                a_quotient(0)
                start = own.base + own.n
                K = 7 + 1 + 2 * 3
                with pool.Fori(1, NB) as b:
                    own.loop(b - 1, K, start)
                    rstd0(b)
                    rstd1(b - 1)
                    a_products(b, 0)
                    a_squares(b - 1, 0)
                    a_products(b, 1)
                    a_numerator(b, 0)
                    a_squares(b - 1, 1)
                    a_numerator(b, 1)
                    a_quotient(b)
                    a_streams(b - 1)
                own.leave(NB - 1, K, start)
                rstd1(NB - 1)
                a_squares(NB - 1, 0)
                a_squares(NB - 1, 1)
                a_streams(NB - 1)

            def ffn_pool(f, target):
                s_ = S[f]
                with pool.Fori(0, NB) as b:
                    pool.wait_ge(s_["ve_ready"], b + 1)
                    nc.gpsimd.tensor_tensor(Xrow[:, bass.ts(b, TB), RSTD:RSTD + 1].rearrange("p t w -> p (t w)"), sm[:, 5, :], minus_half[:, 0:TB], ALU.pow).then_inc(s_["rstd_ready"], 1)
                pool.wait_ge(filled, 32)
                pool.wait_ge(s_["pos_ready"], 1)
                for t in range(NT):
                    nc.gpsimd.indirect_dma_start(
                        out=sorted_rows[f], out_offset=bass.IndirectOffsetOnAxis(posi[f][:, t:t + 1], 0),
                        in_=Xrow[:, t, :], in_offset=None).then_inc(s_["rows_scattered"], 16)

                for s in range(NS):
                    pool.wait_ge(s_["y_ready"], s + 1 + 2)
                    nc.gpsimd.indirect_dma_start(
                        out=target, out_offset=bass.IndirectOffsetOnAxis(x_rows[:, s, ID:ID + 1].bitcast(U32), 0),
                        in_=y_rows[:, s, :], in_offset=None, bounds_check=NT * P - 1,
                        oob_is_err=False).then_inc(s_["y_scattered"], 16)
                pool.wait_ge(s_["y_scattered"], 16 * NS)

            def b_tables():
                pool.wait_ge(gexp, 1)
                nc.gpsimd.tensor_tensor(G[:].rearrange("p a b r -> p (a b r)"), gam.rearrange("p a b r -> p (a b r)"), expo.rearrange("p a b r -> p (a b r)"), ALU.pow)
                nc.gpsimd.tensor_tensor(g128[:], dcol[:, 1:2], hundred28, ALU.pow).then_inc(gpow, 1)

            def b_front(b):
                rstd_chain(smb[:, 4, :], (V["var_ready"], V["scale_ready"]), b + 1, smb, eps_rms)
                pool.wait_ge(V["n2_ready"], b + 1)
                nc.gpsimd.tensor_tensor(rn.rearrange("p t s -> p (t s)"), n2.rearrange("p t s -> p (t s)"), minus_half[:], ALU.pow).then_inc(V["rn_ready"], 1)
                pool.wait_ge(V["ms_ready"], b + 1)
                pool.wait_ge(V["x3_half"], 2 * b + 1)
                nc.gpsimd.tensor_tensor(smb[:, 12, :], smb[:, 11, :], minus_half[:, 0:TB], ALU.pow).then_inc(V["s2_ready"], 1)
                own(nc.gpsimd.tensor_tensor(xh, Xrow[:, bass.ts(b, TB), 0:P], h2, ALU.add))
                nc.gpsimd.tensor_tensor(xh, xh, mb2[:].unsqueeze(1).to_broadcast([P, TB, P]), ALU.add).then_inc(V["xh_ready"], 1)

            if "B" in phases:
                b_tables()
            if "F" in phases:
                ffn_pool(0, last[0])
            if "B" in phases:
                start = own.base + own.n
                with pool.Fori(0, NB) as b:
                    own.loop(b, 8, start)
                    b_front(b)
                own.leave(NB, 8, start)
            if "G" in phases:
                ffn_pool(1, out)

        @block.vector
        def _(dve):
            own = Chain(dve, dve_own)

            def stats(src, bst, sm):
                for t in range(TB):
                    ins = nc.vector.bn_stats(bst[:, t, :], src(t))
                own(ins)

                def part(k):
                    return bst[:, :, k:k + 1].rearrange("p t w -> p (t w)")
                nc.vector.tensor_tensor(sm[:, 1, :], part(1), part(4), ALU.add)
                nc.vector.tensor_tensor(sm[:, 2, :], part(4), part(1), ALU.subtract)
                own(nc.vector.tensor_tensor(sm[:, 3, :], part(2), part(5), ALU.add))
                nc.vector.tensor_scalar(sm[:, 0, :], sm[:, 1, :], 0.5, None, ALU.mult)
                own(nc.vector.scalar_tensor_tensor(sm[:, 2, :], sm[:, 2, :], 0.25 * P, sm[:, 2, :], ALU.mult, ALU.mult))
                own(nc.vector.tensor_tensor(sm[:, 3, :], sm[:, 2, :], sm[:, 3, :], ALU.add))
                return nc.vector.tensor_scalar(sm[:, 4, :], sm[:, 3, :], 1.0 / P, None, ALU.mult)
            STATS = 4

            def x_tile(b, t, width=P):
                return Xrow[:, bass.ds(b * TB + t, 1), 0:width].rearrange("p a c -> p (a c)")

            def a_tables():
                dve.wait_ge(w_loaded, W_FIRST)
                for n in rest:
                    ins = nc.vector.tensor_scalar(rest[n][:], col[n][:], -1.0, 1.0, ALU.mult, ALU.add)
                own(ins)
                for j, (n, m) in enumerate((("k", "tm_k"), ("v", "tm_v"), ("r", "tm_r"), ("cr", "cm_r"))):
                    nc.vector.tensor_scalar(W_now[n][:], wraw[:, j, :], col[m][:], None, ALU.mult)
                    nc.vector.tensor_scalar(W_shift[n][:], wraw[:, j, :], rest[m][:], None, ALU.mult)
                nc.vector.tensor_scalar(Wo[:], Wo[:], -0.5, None, ALU.mult)
                nc.vector.tensor_tensor(cg[:], col["cm_k"][:], col["ln1_g"][:], ALU.mult)
                nc.vector.tensor_tensor(cb[:], col["cm_k"][:], col["ln1_b"][:], ALU.mult)
                dve.wait_ge(act_setup, 1)
                nc.vector.tensor_scalar(decay[:], decay[:], -1.0, None, ALU.mult).then_inc(tables, 1)
                dve.wait_ge(tables, 1)

            def a_front(b):
                stats(lambda t: x_tile(b, t), bsta, sma).then_inc(A["var0_ready"], 1)
                dve.wait_ge(A["scale0_ready"], b + 1)
                dve.wait_ge(A["t0_psum"], b + 1)
                for t in range(TB):
                    ins = nc.vector.tensor_scalar(a8[:, t, :], x_tile(b, t), sma[:, 0, t:t + 1], sma[:, 6, t:t + 1], ALU.subtract, ALU.mult)
                ins.then_inc(A["a8_ready"], 1)
                for t in range(TB):
                    ins = nc.vector.tensor_scalar(Y[:, bass.ds(b * TB + t, 1), :].rearrange("p a c -> p (a c)"), x_tile(b, t), sma[:, 0, t:t + 1], sma[:, 5, t:t + 1], ALU.subtract, ALU.mult)
                own(ins)
            FRONT = STATS + 1

            def a_wkv(b):
                for h in range(2):
                    c, c1 = slice(512 * h, 512 * h + 512), slice(512 * h + 1, 512 * h + 513)
                    kp = ps[2 + h][:]
                    dve.wait_ge(A["k_psum"], 2 * b + h + 1)
                    own(nc.vector.tensor_tensor_scan(p_[:, c1], decay[:].to_broadcast([P, 512]), kp, p_[:, 512 * h:512 * h + 1], ALU.add, ALU.max))
                    nc.vector.tensor_tensor(E2[:, c], kp, p_[:, c1], ALU.subtract)
                    nc.vector.scalar_tensor_tensor(E1[:, c], p_[:, c], decay[:], p_[:, c1], ALU.add, ALU.subtract).then_inc(A["d12_ready"], 1)
                    nc.vector.scalar_tensor_tensor(E3[:, c], kp, col["time_first"][:], p_[:, c], ALU.add, ALU.subtract).then_inc(A["s_ready"], 1)
                for h in range(2):
                    c, c1 = slice(512 * h, 512 * h + 512), slice(512 * h + 1, 512 * h + 513)
                    dve.wait_ge(A["e12_ready"], 2 * b + h + 1)
                    nc.vector.tensor_tensor_scan(bb[:, c1], E1[:, c], E2[:, c], bb[:, 512 * h:512 * h + 1] if h else 0.0, ALU.mult, ALU.add)
                    dve.wait_ge(A["av_ready"], 2 * b + h + 1)
                    nc.vector.tensor_tensor_scan(aa[:, c1], E1[:, c], av[:, c], aa[:, 512 * h:512 * h + 1] if h else 0.0, ALU.mult, ALU.add).then_inc(A["scan_ready"], 1)
                    dve.wait_ge(A["scan_ready"], 2 * b + h + 1)
                    dve.wait_ge(A["e34_ready"], 2 * b + h + 1)
                    own(nc.vector.tensor_tensor(den[:, c], E3[:, c], bb[:, c], ALU.mult))
                    nc.vector.tensor_tensor(den[:, c], den[:, c], E4[:, c], ALU.add).then_inc(A["den_ready"], 1)
                dve.wait_ge(A["qt_ready"], b + 1)
                dve.wait_ge(A["r_tanh"], b + 1)
                own(nc.vector.scalar_tensor_tensor(th, th, 1.0, num, ALU.add, ALU.mult))
                nc.vector.scalar_tensor_tensor(rw, den, -2.0, th, ALU.add, ALU.mult).then_inc(A["rw_ready"], 1)
            WKV = 2 + 2 + 1

            def a_back(b):
                dve.wait_ge(A["x1_done"], b + 1)
                for h in range(2):
                    dve.wait_ge(A["wo_psum"], 2 * b + h + 1 + 1)
                    ins = nc.vector.tensor_tensor(x1[:, 4 * h:4 * h + 4, :], ps[6 + h][:].rearrange("p (t c) -> p t c", c=P),
                                                  Y[:, bass.ds(b * TB + 4 * h, 4), :], ALU.add)
                own(ins)
                stats(lambda t: x1[:, t, :], bsta, smx).then_inc(A["var1_ready"], 1)
                dve.wait_ge(A["scale1_ready"], b + 1)
                for t in range(TB):
                    ins = nc.vector.tensor_scalar(x1n[:, t, :], x1[:, t, :], smx[:, 0, t:t + 1], smx[:, 5, t:t + 1], ALU.subtract, ALU.mult)
                ins.then_inc(A["x1n_ready"], 1)
                dve.wait_ge(A["xc_ready"], b + 1)
                nc.vector.scalar_tensor_tensor(mk, xc[:, 0:L], rest["cm_k"][:], ca, ALU.mult, ALU.add).then_inc(A["mk_ready"], 1)
            BACK = 1 + STATS

            def a_final(b):
                dve.wait_ge(A["th2_ready"], b + 2)
                dve.wait_ge(A["xx_ready"], b + 1)
                for h in range(2):
                    dve.wait_ge(A["cv_psum"], 2 * b + h + 1 + 2)
                    t4 = th2[:, 512 * h:512 * h + 512]
                    own(nc.vector.scalar_tensor_tensor(t4, t4, 1.0, ps[h][:], ALU.add, ALU.mult))
                    ins = nc.vector.scalar_tensor_tensor(Xrow[:, bass.ds(b * TB + 4 * h, 4), 0:P], t4.rearrange("p (t c) -> p t c", c=P), 0.5, x1[:, 4 * h:4 * h + 4, :], ALU.mult, ALU.add)
                ins.then_inc(A["x1_done"], 1)
            FINAL = 2

            def attn_a():
                dve.wait_ge(x_loaded[0], 16)
                a_front(0)
                a_tables()
                a_wkv(0)
                for b in range(1, NB):
                    dve.wait_ge(x_loaded[b], 16)
                start = own.base + own.n
                K = FRONT + BACK + WKV + FINAL
                with dve.Fori(1, NB) as b:
                    own.loop(b - 1, K, start)
                    a_front(b)
                    a_back(b - 1)
                    a_wkv(b)
                    a_final(b - 1)
                own.leave(NB - 1, K, start)
                a_back(NB - 1)
                a_final(NB - 1)
                dve.wait_ge(A["x1_done"], NB + 1)

            def gate_loop(f):
                s_ = S[f]
                start = own.base + own.n
                K = STATS + 2
                with dve.Fori(0, NB) as b:
                    own.loop(b, K, start)
                    own(stats(lambda t: x_tile(b, t), bst, sm))
                    own(nc.vector.tensor_copy(Xrow[:, bass.ts(b, TB), MEAN:MEAN + 1].rearrange("p t w -> p (t w)"), sm[:, 0, :]))
                    nc.vector.tensor_scalar(sm[:, 5, :], sm[:, 4, :], EPS, None, ALU.add).then_inc(s_["ve_ready"], 1)
                    dve.wait_ge(s_["rstd_ready"], b + 1)
                    dve.wait_ge(s_["zt_psum"], b + 1)
                    for t in range(TB):
                        row = x_tile(b, t, ROW)
                        ins = nc.vector.tensor_scalar(z8[:, t, :], row[:, 0:P], row[:, MEAN:MEAN + 1], row[:, RSTD:RSTD + 1], ALU.subtract, ALU.mult)
                    ins.then_inc(s_["z_ready"], 1)
                own.leave(NB, K, start)

            def flat(ap):
                return ap.rearrange("p e t -> p (e t)")

            def route(f):
                s_ = S[f]
                dve.wait_ge(s_["logits_done"], NB + 1)
                own(nc.vector.tensor_tensor(lg, ps[2][:, 0:NT * NE].rearrange("p (t e) -> p t e", e=NE), bg[:].unsqueeze(1).to_broadcast([P, NT, NE]), ALU.add))
                own(nc.vector.tensor_reduce(top, lg, AX_X, ALU.max))
                own(nc.vector.tensor_tensor(eq, lg, top.unsqueeze(2).to_broadcast([P, NT, NE]), ALU.is_ge))
                own(nc.vector.tensor_tensor(eq, eq, expert_m8[:].unsqueeze(1).to_broadcast([P, NT, NE]), ALU.mult))
                own(nc.vector.tensor_reduce(top, eq, AX_X, ALU.min))
                nc.vector.tensor_tensor(oh, expert_m8[:].unsqueeze(2).to_broadcast([P, NE, NT]), top.unsqueeze(1).to_broadcast([P, NE, NT]), ALU.is_equal).then_inc(s_["onehot_ready"], 1)
                dve.wait_ge(s_["ranks_done"], 1)
                tot = ps[4][:, 0:NE * NT]
                own(nc.vector.tensor_tensor_scan(flat(run), flat(not_first[:]), tot, 0.0, ALU.mult, ALU.add))
                own(nc.vector.tensor_scalar(ntf, flat(run[:, :, NT - 1:NT]), float(P - 1), None, ALU.add))
                own(nc.vector.tensor_copy(nti, ntf))
                own(nc.vector.tensor_scalar(nti, nti, 7, None, ALU.arith_shift_right))
                own(nc.vector.tensor_copy(ntf, nti))
                own(nc.vector.tensor_tensor_scan(endt, ones[:, 0:NE], ntf, 0.0, ALU.mult, ALU.add))
                own(nc.vector.tensor_tensor(baset, endt, ntf, ALU.subtract))
                own(nc.vector.tensor_tensor(flat(run), flat(run), tot, ALU.subtract))
                own(nc.vector.tensor_tensor(flat(run), flat(run), ps[3][:, 0:NE * NT], ALU.add))
                own(nc.vector.scalar_tensor_tensor(run, baset.unsqueeze(2).to_broadcast([P, NE, NT]), float(P), run, ALU.mult, ALU.add))
                own(nc.vector.tensor_tensor(pos3, run, oh, ALU.mult))
                own(nc.vector.tensor_reduce(posf, pos3.rearrange("p e t -> p t e"), AX_X, ALU.add))
                nc.vector.tensor_copy(posi[f][:], posf).then_inc(s_["pos_ready"], 1)
                own(nc.vector.tensor_tensor(cmp_, endt.unsqueeze(1).to_broadcast([P, NS, NE]), slot_no[:].unsqueeze(2).to_broadcast([P, NS, NE]), ALU.is_le))
                own(nc.vector.tensor_reduce(texf, cmp_, AX_X, ALU.add))
                own(nc.vector.tensor_scalar(texf, texf, float(NE - 1), None, ALU.min))
                nc.vector.tensor_copy(texp[f][:], texf).then_inc(s_["pos_ready"], 1)
                dve.wait_ge(s_["pos_ready"], 2)

            def experts(f):
                s_ = S[f]

                def finish(u, g):
                    dve.wait_ge(s_["y_psum"], g + 1 + U)
                    y = y_rows[:, bass.ds(g, 1), :].rearrange("p a c -> p (a c)")
                    x = x_rows[:, bass.ds(g, 1), 0:P].rearrange("p a c -> p (a c)")
                    own(nc.vector.tensor_tensor(y, ps[Y_BANK[u]][:, 0:P], x, ALU.add))
                    e = dve.value_load(texp[f][0:1, bass.ds(g, 1)], min_val=0, max_val=NE - 1)
                    b2 = B2[:, bass.ds(e, 1), :].rearrange("p a c -> p (a c)")
                    nc.vector.tensor_tensor(y, y, b2, ALU.add).then_inc(s_["y_ready"], 1)

                def turn(i, first):
                    for u in range(U):
                        g = i * U + u
                        dve.wait_ge(loads[f][u], 16 * i + 16)
                        dve.wait_ge(s_["zsT_psum"], g + 1)
                        dve.wait_ge(s_["h_psum"], g + 1)
                        row = x_rows[:, bass.ds(g, 1), :].rearrange("p a c -> p (a c)")
                        nc.vector.tensor_scalar(zs[u], row[:, 0:P], row[:, MEAN:MEAN + 1], row[:, RSTD:RSTD + 1], ALU.subtract, ALU.mult).then_inc(s_["zs_ready"], 1)
                        e = dve.value_load(texp[f][0:1, bass.ds(g, 1)], min_val=0, max_val=NE - 1)
                        nc.vector.tensor_copy(w1cur[u], W1[:, bass.ds(e, 1), :].rearrange("p a c -> p (a c)")).then_inc(s_["w1_ready"], 1)
                        if not first:
                            finish(u, g - U)
                        dve.wait_ge(s_["zsT_psum"], g + 1 + U)
                        nc.vector.tensor_copy(zsT[u], ps[u][:, 0:P]).then_inc(s_["zsT_ready"], 1)

                turn(0, True)
                start = own.base + own.n
                with dve.Fori(1, NS // U) as i:
                    own.loop(i - 1, U, start)
                    turn(i, False)
                own.leave(NS // U - 1, U, start)
                for u in range(U):
                    finish(u, NS - U + u)
                own(nc.vector.tensor_copy(posf[:, 0:1], posf[:, 1:2]))

            def b_tables():
                dve.wait_ge(w_loaded2, W_SECOND)
                nc.vector.tensor_scalar(uv[:], uv[:], col["norm1_w"][:], None, ALU.mult)
                nc.vector.tensor_scalar(M1[:], M1[:], col["norm2_w"][:], None, ALU.mult)
                dve.wait_ge(act_setup, 5)
                nc.vector.tensor_scalar(cst[:, 4:5], cst[:, 4:5], 0.5, 0.5, ALU.mult, ALU.add)
                nc.vector.tensor_scalar(dcol[:, 0:1], dcol[:, 0:1], 0.5, 0.5, ALU.mult, ALU.add)
                own(nc.vector.tensor_scalar(dl[:, 0:2], dl[:, 0:2], 0.5, 0.5, ALU.mult, ALU.add))
                nc.vector.tensor_scalar(dcol[:, 1:2], dcol[:, 0:1], 0.15, 1.0, ALU.max, ALU.min)
                nc.vector.tensor_scalar(cst[:, 0:4], cst[:, 0:4], cst[:, 4:5], None, ALU.mult)
                own(nc.vector.tensor_scalar(dl[:, 2], dl[:, 0], 0.15, 1.0, ALU.max, ALU.min))
                g2 = dl[:, 2].unsqueeze(1).to_broadcast([P, 3 * NBLK, R])
                own(nc.vector.tensor_copy(gam.rearrange("p a b r -> p (a b) r"), g2))
                nc.vector.tensor_scalar(gmask[:, 0], expo[:, 0], 0.5 - BLK, None, ALU.is_gt)
                nc.vector.tensor_scalar(gmask[:, 2], expo[:, 1], BLK - 0.5, None, ALU.is_lt)
                own(nc.vector.tensor_scalar(gmask[:, 1], expo[:, 1], -0.5, None, ALU.is_gt))
                own(nc.vector.tensor_tensor(gmask[:, 1], gmask[:, 1], gmask[:, 2], ALU.mult))
                own(nc.vector.tensor_tensor(gmask[:, 1], gmask[:, 1], dl[:, 1].unsqueeze(1).to_broadcast([P, NBLK, R]), ALU.mult))
                nc.vector.tensor_scalar(expo[:, 0], expo[:, 0], float(-BLK), None, ALU.max)
                nc.vector.tensor_scalar(expo[:, 1], expo[:, 1], 0.0, None, ALU.max).then_inc(gexp, 1)
                nc.vector.tensor_scalar(conv[:], dist, 0.0, cst[:, 0:1], ALU.is_equal, ALU.mult)
                own(nc.vector.tensor_scalar(conv_prev[:], dist[:, 0:4], float(1 - P), cst[:, 1:2], ALU.is_equal, ALU.mult))
                for m in range(1, 4):
                    own(nc.vector.tensor_scalar(ctmp, dist, float(m), cst[:, m:m + 1], ALU.is_equal, ALU.mult))
                    own(nc.vector.tensor_tensor(conv[:], conv[:], ctmp, ALU.add))
                    if m > 1:
                        own(nc.vector.tensor_scalar(ctmp[:, 0:4], dist[:, 0:4], float(m - P), cst[:, m:m + 1], ALU.is_equal, ALU.mult))
                        own(nc.vector.tensor_tensor(conv_prev[:], conv_prev[:], ctmp[:, 0:4], ALU.add))
                dve.wait_ge(gpow, 1)
                own(nc.vector.tensor_tensor(G[:, 0:2].rearrange("p a b r -> p (a b r)"), G[:, 0:2].rearrange("p a b r -> p (a b r)"), gmask[:, 0:2].rearrange("p a b r -> p (a b r)"), ALU.mult))

            def b_front(b):
                stats(lambda t: x_tile(b, t), bstb, smb).then_inc(V["var_ready"], 1)
                dve.wait_ge(V["scale_ready"], b + 1)
                dve.wait_ge(V["t3_psum"], b + 1)
                for t in range(TB):
                    ins = nc.vector.tensor_scalar(hn[:, t, :], x_tile(b, t), smb[:, 0, t:t + 1], smb[:, 6, t:t + 1], ALU.subtract, ALU.mult)
                ins.then_inc(V["hn_ready"], 1)
                dve.wait_ge(V["qk_copied"], b + 1)
                own(nc.vector.tensor_tensor(sq, qks, qks, ALU.mult))
                own(nc.vector.tensor_reduce(n2, sq, AX_X, ALU.add))
                nc.vector.tensor_scalar(n2, n2, 1e-16, None, ALU.max).then_inc(V["n2_ready"], 1)
                dve.wait_ge(V["rn_ready"], b + 1)
                own(nc.vector.tensor_tensor(sq, qks, rn.unsqueeze(3).to_broadcast([P, TB, 2, R]), ALU.mult))
                for dst, qk, table in ((KQ[:, :, 0:64], 1, 0), (KQ[:, :, 64:128], 0, 1), (kd, 1, 2)):
                    ins = nc.vector.tensor_tensor(dst.rearrange("p t (b r) -> p t b r", r=R),
                                                  sq[:, :, qk, :].unsqueeze(2).to_broadcast([P, TB, NBLK, R]),
                                                  G[:, table].unsqueeze(1).to_broadcast([P, TB, NBLK, R]), ALU.mult)
                ins.then_inc(V["kq_ready"], 1)
                for t in range(TB - 1):
                    src = ps[3 + t // 4][0:64, (t % 4) * P:(t % 4 + 1) * P]
                    if t % 4 == 0:
                        dve.wait_ge(V["u_psum"], 2 * b + t // 4 + 1)
                    if t == 0:
                        ins = nc.vector.tensor_copy(state[:, 1, :], src)
                    else:
                        ins = nc.vector.scalar_tensor_tensor(state[:, t + 1, :], state[:, t, :], g128[:], src, ALU.mult, ALU.add)
                    if t == 3 or t == TB - 2:
                        ins.then_inc(V["state_ready"], 1)
                        dve.wait_ge(V["state_ready"], 2 * b + (1 if t == 3 else 2))
                    else:
                        own(ins)
                for h in range(2):
                    dve.wait_ge(V["at_psum"], 2 * b + h + 1)
                    at = AT[:, 4 * h:4 * h + 4, :]
                    own(nc.vector.tensor_tensor(at, ps[2 + h][:].rearrange("p (t c) -> p t c", c=P), causal[:].unsqueeze(1).to_broadcast([P, 4, P]), ALU.mult))
                    nc.vector.tensor_tensor(at, at, conv[:].unsqueeze(1).to_broadcast([P, 4, P]), ALU.add).then_inc(V["at_ready"], 1)
                for h in range(2):
                    dve.wait_ge(V["proj_psum"], 2 * b + h + 1)
                    hh = h2[:, 4 * h:4 * h + 4, :]
                    own(nc.vector.tensor_tensor(hh, ps[4 if h == 0 else 2][:].rearrange("p (t c) -> p t c", c=P), pb[:].unsqueeze(1).to_broadcast([P, 4, P]), ALU.add))
                    for t in range(4 * h, 4 * h + 4):
                        ins = nc.vector.scalar_tensor_tensor(h2[:, t, :], hn[:, t, :], smb[:, 7, t:t + 1], h2[:, t, :], ALU.mult, ALU.add)
                own(ins)
                own(stats(lambda t: h2[:, t, :], bstb, smb))
                own(nc.vector.tensor_tensor(smb[:, 10, :], smb[:, 0, :], smb[:, 0, :], ALU.mult))
                nc.vector.scalar_tensor_tensor(smb[:, 11, :], smb[:, 4, :], 1e-6, smb[:, 10, :], ALU.add, ALU.add).then_inc(V["ms_ready"], 1)
                dve.wait_ge(V["s2_ready"], b + 1)
                for t in range(TB):
                    ins = nc.vector.tensor_scalar(h2n[:, t, :], h2[:, t, :], smb[:, 12, t:t + 1], None, ALU.mult)
                ins.then_inc(V["h2n_ready"], 1)
            BFRONT = STATS + 3 + 5 + 2 + 3 + (STATS + 1) + 1

            def b_final(b):
                dve.wait_ge(V["xh_ready"], b + 1)
                for h in range(2):
                    dve.wait_ge(V["down_psum"], 2 * b + h + 1 + 2)
                    x = Xrow[:, bass.ds(b * TB + 4 * h, 4), 0:P]
                    ins = nc.vector.tensor_tensor(x, ps[7][:].rearrange("p (t c) -> p t c", c=P), xh[:, 4 * h:4 * h + 4, :], ALU.add)
                    ins.then_inc(V["x3_half"], 1)

            dve.wait_ge(consts, 3)
            if "A" in phases:
                attn_a()
            if "B" in phases:
                b_tables()
            if "F" in phases:
                dve.wait_ge(w_loaded2, W_SECOND)
                gate_loop(0)
                route(0)
                experts(0)
            if "B" in phases:
                for b in range(NB):
                    dve.wait_ge(x2_loaded[b], 16)
                start = own.base + own.n
                K = BFRONT
                with dve.Fori(0, NB) as b:
                    own.loop(b, K, start)
                    b_front(b)
                    b_final(b)
                own.leave(NB, K, start)
                dve.wait_ge(V["x3_half"], 2 * NB + 1)
            if "G" in phases:
                gate_loop(1)
                route(1)
                experts(1)

        @block.scalar
        def _(act):
            own = Chain(act, act_own)

            def setup_act():
                act.wait_ge(w_loaded, W_FIRST)
                nc.scalar.activation(decay[:], col["time_decay"][:], ACT.Exp).then_inc(act_setup, 1)

            def setup_act2():
                act.wait_ge(w_loaded2, W_SECOND)
                for ap in (dl[:, 0], dl[:, 1], dcol[:, 0:1], cst[:, 4:5]):
                    nc.scalar.activation(ap, ap, ACT.Tanh, scale=0.5).then_inc(act_setup, 1)
                act.wait_ge(proj_turned, 1)
                nc.scalar.activation(projT[:], ps[2][:, 0:P], ACT.Copy, scale=col["norm1_w"][:]).then_inc(proj_ready, 1)

            def a_front(b):
                act.wait_ge(A["t0_psum"], b + 1 + 1)
                for h in range(2):
                    ins = nc.scalar.activation(xa[:, 1 + 512 * h:513 + 512 * h], ps[h][:], ACT.Identity, bias=col["ln0_b"][:], scale=col["ln0_g"][:])
                ins.then_inc(A["xa_ready"], 1)

            def a_kvr(b):
                for h in range(2):
                    act.wait_ge(A["v_psum"], 2 * b + h + 1)
                    ins = nc.scalar.copy(vs[:, 512 * h:512 * h + 512], ps[4 + h][:])
                ins.then_inc(A["v_copied"], 1)
                for h in range(2):
                    act.wait_ge(A["r_psum"], 2 * b + h + 1)
                    ins = nc.scalar.activation(th[:, 512 * h:512 * h + 512], ps[h][:], ACT.Tanh, scale=0.5)
                ins.then_inc(A["r_tanh"], 1)

            def a_exps(b, h):
                c = slice(512 * h, 512 * h + 512)
                act.wait_ge(A["d12_ready"], 2 * b + h + 1)
                nc.scalar.activation(E1[:, c], E1[:, c], ACT.Exp)
                nc.scalar.activation(E2[:, c], E2[:, c], ACT.Exp).then_inc(A["e12_ready"], 1)
                act.wait_ge(A["s_ready"], 2 * b + h + 1)
                own(nc.scalar.activation(E4[:, c], E3[:, c], ACT.Relu, scale=-1.0))
                own(nc.scalar.activation(E3[:, c], E3[:, c], ACT.Relu))
                nc.scalar.activation(E4[:, c], E4[:, c], ACT.Exp, scale=-1.0)
                nc.scalar.activation(E3[:, c], E3[:, c], ACT.Exp, scale=-1.0).then_inc(A["e34_ready"], 1)

            def a_guess(b):
                act.wait_ge(A["den_ready"], 2 * b + 2)
                own(nc.scalar.activation(y0, den, ACT.Ln))
                nc.scalar.activation(y0, y0, ACT.Exp, scale=-1.0).then_inc(A["y0_ready"], 1)
            A_WKV = 5

            def a_back1(b):
                act.wait_ge(A["t1_psum"], b + 1)
                for h in range(2):
                    c = slice(512 * h, 512 * h + 512)
                    nc.scalar.activation(xc[:, 1 + 512 * h:513 + 512 * h], ps[h][:], ACT.Identity, bias=col["ln1_b"][:], scale=col["ln1_g"][:])
                    ins = nc.scalar.activation(ca[:, c], ps[h][:], ACT.Identity, bias=cb[:], scale=cg[:])
                ins.then_inc(A["xc_ready"], 1)

            def a_relu(b, half):
                for k in range(HC):
                    n = b * (2 * HC) + half * HC + k
                    act.wait_ge(A["ck_psum"], n + 1 + 2)
                    act.wait_ge(A["kk_ready"], n + 1)
                    nc.scalar.activation(kkr[k % 2], ps[4 + k % 2][:], ACT.Relu).then_inc(A["relu_ready"], 1)

            def a_gate(b):
                for h in range(2):
                    act.wait_ge(A["cr_psum"], 2 * b + h + 1)
                    ins = nc.scalar.activation(th2[:, 512 * h:512 * h + 512], ps[6 + h][:], ACT.Tanh, scale=0.5)
                ins.then_inc(A["th2_ready"], 1)

            setup_act()
            if "A" in phases:
                act.wait_ge(tables, 1)
                a_front(0)
                a_kvr(0)
                a_exps(0, 0)
                a_exps(0, 1)
                a_guess(0)
                start = own.base + own.n
                with act.Fori(1, NB) as b:
                    own.loop(b - 1, A_WKV, start)
                    a_front(b)
                    a_kvr(b)
                    a_back1(b - 1)
                    a_gate(b - 1)
                    a_exps(b, 0)
                    a_relu(b - 1, 0)
                    a_exps(b, 1)
                    a_relu(b - 1, 1)
                    a_guess(b)
                own.leave(NB - 1, A_WKV, start)
                a_back1(NB - 1)
                a_gate(NB - 1)
                a_relu(NB - 1, 0)
                a_relu(NB - 1, 1)

            def ffn_act(f):
                s_ = S[f]
                with act.Fori(0, NB) as b:
                    act.wait_ge(s_["zt_psum"], b + 1 + 1)
                    act.wait_ge(s_["logits_done"], b + 1)
                    nc.scalar.copy(z8T[:, 0:512], ps[0][:]).then_inc(s_["zt_copied"], 1)
                    nc.scalar.copy(z8T[:, 512:1024], ps[1][:]).then_inc(s_["zt_copied"], 1)
                act.wait_ge(s_["pos_ready"], 2)

                with act.Fori(0, NS // U) as i:
                    for u in range(U):
                        g = i * U + u
                        e = act.value_load(texp[f][0:1, bass.ds(g, 1)], min_val=0, max_val=NE - 1)
                        act.wait_ge(s_["h_psum"], g + 1 + U)
                        act.wait_ge(s_["y_psum"], g + 1)
                        for k in range(HC):
                            b1 = B1[:, bass.ds(e, 1), k:k + 1].rearrange("p a c -> p (a c)")
                            ins = nc.scalar.activation(hT[u][:, k, :], ps[3 + u][:, k * P:(k + 1) * P], ACT.Gelu, bias=b1)
                        ins.then_inc(s_["h_ready"], 1)

            def b_front(b):
                act.wait_ge(V["t1_psum"], b + 1)
                for h in range(2):
                    ins = nc.scalar.copy(hnT[:, 512 * h:512 * h + 512], ps[h][:])
                ins.then_inc(V["hnT_ready"], 1)
                act.wait_ge(V["qk_psum"], b + 1)
                nc.scalar.copy(qks.rearrange("p t s r -> p (t s r)"), ps[2][:, 0:TB * 2 * R]).then_inc(V["qk_copied"], 1)
                act.wait_ge(V["t2_psum"], b + 1)
                for h in range(2):
                    nc.scalar.copy(kT[:, 512 * h:512 * h + 512], ps[h][0:64, :])
                    ins = nc.scalar.copy(qT[:, 512 * h:512 * h + 512], ps[h][64:128, :])
                ins.then_inc(V["kqT_ready"], 1)
                for h in range(2):
                    act.wait_ge(V["o_psum"], 2 * b + h + 1 + 1)
                    nc.scalar.copy(oT[:, 512 * h:512 * h + 512], ps[h][:]).then_inc(V["oT_ready"], 1)
                act.wait_ge(V["t3_psum"], b + 1 + 1)
                for h in range(2):
                    ins = nc.scalar.copy(h2T[:, 512 * h:512 * h + 512], ps[h][:])
                ins.then_inc(V["h2T_ready"], 1)

            def b_mlp(b):
                for h in range(2):
                    act.wait_ge(V["down_psum"], 2 * b + h + 1)
                    for k in range(HC):
                        act.wait_ge(V["up_psum"], 2 * HC * b + HC * h + k + 1)
                        nc.scalar.activation(hmT[:, h, k, :], ps[5 + k % 2][:], ACT.Gelu_apprx_tanh, bias=mb1[:, k:k + 1]).then_inc(V["hm_ready"], 1)

            if "B" in phases:
                setup_act2()
            if "F" in phases:
                ffn_act(0)
            if "B" in phases:
                with act.Fori(0, NB) as b:
                    b_front(b)
                    b_mlp(b)
            if "G" in phases:
                ffn_act(1)

        @block.tensor
        def _(pe):
            def tiles_turned(src, n=TB):
                for t in range(n):
                    ins = nc.tensor.transpose(ps[t // 4][:, (t % 4) * P:(t % 4 + 1) * P], src[:, t, :], ident[:])
                return ins

            def a_wo(b):
                pe.wait_ge(A["rw_ready"], b + 1)
                pe.wait_ge(A["th2_ready"], b + 1)
                for h in range(2):
                    for t in range(4):
                        at = (4 * h + t) * P
                        ins = nc.tensor.matmul(ps[6 + h][:, t * P:(t + 1) * P], rw[:, at:at + P], Wo[:], start=True, stop=True)
                    ins.then_inc(A["wo_psum"], 1)

            def a_front(b, first=False):
                pe.wait_ge(A["a8_ready"], b + 1)
                if not first:
                    pe.wait_ge(A["x1_done"], b)
                    pe.wait_ge(A["s_ready"], 2 * b)
                    pe.wait_ge(A["relu_ready"], 2 * HC * (b - 1) + 2)
                tiles_turned(a8).then_inc(A["t0_psum"], 1)
                pe.wait_ge(A["xa_ready"], b + 1)
                for n, bank, done in (("k", 2, A["k_psum"]), ("v", 4, A["v_psum"]), ("r", 0, A["r_psum"])):
                    for h in range(2):
                        nc.tensor.matmul(ps[bank + h][:], W_now[n][:], xa[:, 1 + 512 * h:513 + 512 * h], start=True, stop=False)
                        nc.tensor.matmul(ps[bank + h][:], W_shift[n][:], xa[:, 512 * h:512 + 512 * h], start=False, stop=True).then_inc(done, 1)

            def a_back(b, started):
                pe.wait_ge(A["r_tanh"], started)
                pe.wait_ge(A["v_copied"], started)
                pe.wait_ge(A["x1n_ready"], b + 1)
                tiles_turned(x1n).then_inc(A["t1_psum"], 1)
                pe.wait_ge(A["xc_ready"], b + 1)
                for h in range(2):
                    for t in range(4):
                        at = (4 * h + t) * P
                        nc.tensor.matmul(ps[6 + h][:, t * P:(t + 1) * P], xc[:, 1 + at:1 + at + P], W_now["cr"][:], start=True, stop=False)
                        ins = nc.tensor.matmul(ps[6 + h][:, t * P:(t + 1) * P], xc[:, at:at + P], W_shift["cr"][:], start=False, stop=True)
                    ins.then_inc(A["cr_psum"], 1)
                pe.wait_ge(A["mk_ready"], b + 1)
                for h in range(2):
                    for k in range(HC):
                        n = 2 * HC * b + HC * h + k
                        pe.wait_ge(A["relu_ready"], n + 1)
                        nc.tensor.matmul(ps[4 + k % 2][:], Wck[:, k * P:(k + 1) * P], mk[:, 512 * h:512 * h + 512], start=True, stop=True).then_inc(A["ck_psum"], 1)
                    pe.wait_ge(A["kk_ready"], 2 * HC * b + HC * h + HC + 2)
                    for t in range(4):
                        for k in range(HC):
                            ins = nc.tensor.matmul(ps[h][:, t * P:(t + 1) * P], kk2[:, k, t * P:(t + 1) * P], Wcv[:, k, :], start=(k == 0), stop=(k == HC - 1))
                    ins.then_inc(A["cv_psum"], 1)

            def ffn_pe(f):
                s_ = S[f]
                with pe.Fori(0, NB) as b:
                    pe.wait_ge(s_["z_ready"], b + 1)
                    pe.wait_ge(s_["zt_copied"], 2 * b + 2)
                    tiles_turned(z8).then_inc(s_["zt_psum"], 1)
                    pe.wait_ge(s_["zt_copied"], 2 * b + 2 + 2)
                    for t in range(TB):
                        ins = nc.tensor.matmul(ps[2][:, bass.ds(b * (TB * NE) + t * NE, NE)], z8T[:, t * P:(t + 1) * P], Wg[:], start=True, stop=True)
                    ins.then_inc(s_["logits_done"], 1)
                pe.wait_ge(s_["onehot_ready"], 1)
                nc.tensor.matmul(ps[3][:, 0:NE * NT], before[:], oh.rearrange("p e t -> p (e t)"), start=True, stop=True)
                nc.tensor.matmul(ps[4][:, 0:NE * NT], ones[:], oh.rearrange("p e t -> p (e t)"), start=True, stop=True).then_inc(s_["ranks_done"], 1)
                pe.wait_ge(s_["pos_ready"], 2)

                def turn_z(u, g):
                    pe.wait_ge(s_["zs_ready"], g + 1)
                    nc.tensor.transpose(ps[u][:, 0:P], zs[u], ident[:]).then_inc(s_["zsT_psum"], 1)

                def up(u, g):
                    pe.wait_ge(s_["zsT_ready"], g + 1)
                    pe.wait_ge(s_["w1_ready"], g + 1)
                    pe.wait_ge(s_["h_ready"], g + 1)
                    for k in range(HC):
                        ins = nc.tensor.matmul(ps[3 + u][:, k * P:(k + 1) * P], w1cur[u][:, k * P:(k + 1) * P], zsT[u], start=True, stop=True)
                    ins.then_inc(s_["h_psum"], 1)

                def down(u, g):
                    e = pe.value_load(texp[f][0:1, bass.ds(g, 1)], min_val=0, max_val=NE - 1)
                    pe.wait_ge(s_["h_ready"], g + 1 + U)
                    pe.wait_ge(s_["y_ready"], g + (2 if u == 0 else 1))
                    for k in range(HC):
                        ins = nc.tensor.matmul(ps[Y_BANK[u]][:, 0:P], hT[u][:, k, :],
                                               W2[:, bass.ds(e, 1), k, :].rearrange("p a c -> p (a c)"), start=(k == 0), stop=(k == HC - 1))
                    ins.then_inc(s_["y_psum"], 1)

                def turn(i, first):
                    for u in range(U):
                        g = i * U + u
                        turn_z(u, g)
                        if not (first and u < 1):
                            up((u - 1) % U, g - 1)
                        if not (first and u < 2):
                            down((u - 2) % U, g - 2)

                turn(0, True)
                with pe.Fori(1, NS // U) as i:
                    turn(i, False)
                up(U - 1, NS - 1)
                down(U - 2, NS - 2)
                down(U - 1, NS - 1)

            def b_front(b):
                pe.wait_ge(V["hn_ready"], b + 1)
                tiles_turned(hn).then_inc(V["t1_psum"], 1)
                pe.wait_ge(V["hnT_ready"], b + 1)
                for t in range(TB):
                    ins = nc.tensor.matmul(ps[2][:, t * 2 * R:(t + 1) * 2 * R], hnT[:, t * P:(t + 1) * P], uv[:], start=True, stop=True)
                ins.then_inc(V["qk_psum"], 1)
                pe.wait_ge(V["kq_ready"], b + 1)
                tiles_turned(KQ).then_inc(V["t2_psum"], 1)
                for t in range(TB - 1):
                    ins = nc.tensor.matmul(ps[3 + t // 4][0:64, (t % 4) * P:(t % 4 + 1) * P], kd[:, t, :], hn[:, t, :], start=True, stop=True)
                    if t % 4 == 3 or t == TB - 2:
                        ins.then_inc(V["u_psum"], 1)
                pe.wait_ge(V["kqT_ready"], b + 1)
                for h in range(2):
                    if h == 1:
                        pe.wait_ge(V["state_ready"], 2 * b + 1)
                    for t in range(4):
                        at = slice((4 * h + t) * P, (4 * h + t + 1) * P)
                        ins = nc.tensor.matmul(ps[2 + h][:, t * P:(t + 1) * P], kT[:, at], qT[:, at], start=True, stop=True)
                    ins.then_inc(V["at_psum"], 1)
                pe.wait_ge(V["state_ready"], 2 * b + 2)
                for h in range(2):
                    pe.wait_ge(V["at_ready"], 2 * b + h + 1)
                    for t in range(4):
                        c = 4 * h + t
                        o = ps[h][:, t * P:(t + 1) * P]
                        ins = nc.tensor.matmul(o, hn[:, c, :], AT[:, c, :], start=True, stop=(c == 0))
                        if c:
                            nc.tensor.matmul(ps[h][:, t * P:t * P + 4], hn[:, c - 1, :], conv_prev[:], start=False, stop=False)
                            ins = nc.tensor.matmul(o, state[:, c, :], qT[:, c * P:(c + 1) * P], start=False, stop=True)
                    ins.then_inc(V["o_psum"], 1)
                for h in range(2):
                    pe.wait_ge(V["oT_ready"], 2 * b + h + 1)
                    for t in range(4):
                        at = (4 * h + t) * P
                        ins = nc.tensor.matmul(ps[4 if h == 0 else 2][:, t * P:(t + 1) * P], oT[:, at:at + P], projT[:], start=True, stop=True)
                    ins.then_inc(V["proj_psum"], 1)
                pe.wait_ge(V["h2n_ready"], b + 1)
                tiles_turned(h2n).then_inc(V["t3_psum"], 1)

            def b_mlp(b):
                pe.wait_ge(V["h2T_ready"], b + 1)
                for h in range(2):
                    for k in range(HC):
                        pe.wait_ge(V["hm_ready"], 2 * HC * b + HC * h + k + 1)
                        nc.tensor.matmul(ps[5 + k % 2][:], M1[:, k * P:(k + 1) * P], h2T[:, 512 * h:512 * h + 512], start=True, stop=True).then_inc(V["up_psum"], 1)
                for h in range(2):
                    pe.wait_ge(V["hm_ready"], 2 * HC * b + HC * h + HC + 2)
                    pe.wait_ge(V["x3_half"], 2 * b + h + 1)
                    for t in range(4):
                        for k in range(HC):
                            ins = nc.tensor.matmul(ps[7][:, t * P:(t + 1) * P], hmT[:, h, k, t * P:(t + 1) * P], M2[:, k, :], start=(k == 0), stop=(k == HC - 1))
                    ins.then_inc(V["down_psum"], 1)

            pe.wait_ge(consts, 3)
            if "A" in phases:
                pe.wait_ge(tables, 1)
                a_front(0, first=True)
                with pe.Fori(1, NB) as b:
                    a_wo(b - 1)
                    a_front(b)
                    a_back(b - 1, b + 1)
                a_wo(NB - 1)
                a_back(NB - 1, NB)
            if "B" in phases:
                pe.wait_ge(w_loaded2, W_SECOND)
                nc.tensor.transpose(ps[2][:, 0:P], proj_in, ident[:]).then_inc(proj_turned, 1)
                pe.wait_ge(proj_ready, 1)
            if "F" in phases:
                pe.wait_ge(w_loaded2, W_SECOND)
                ffn_pe(0)
            if "B" in phases:
                with pe.Fori(0, NB) as b:
                    b_front(b)
                    b_mlp(b)
            if "G" in phases:
                ffn_pe(1)


_INS = [
    'L0_attn_a_x', 'L0_attn_a_ln0_g', 'L0_attn_a_ln0_b', 'L0_attn_a_ln1_g', 'L0_attn_a_ln1_b', 'L0_attn_a_time_decay',
    'L0_attn_a_time_first', 'L0_attn_a_tm_k', 'L0_attn_a_tm_v', 'L0_attn_a_tm_r', 'L0_attn_a_Wk', 'L0_attn_a_Wv',
    'L0_attn_a_Wr', 'L0_attn_a_Wo', 'L0_attn_a_cm_k', 'L0_attn_a_cm_r', 'L0_attn_a_Wck', 'L0_attn_a_Wcv',
    'L0_attn_a_Wcr', 'L0_attn_b_u', 'L0_attn_b_v', 'L0_attn_b_decay_logit', 'L0_attn_b_alpha_logit',
    'L0_attn_b_k_base_gate_logit', 'L0_attn_b_k_base_kernel', 'L0_attn_b_proj_w', 'L0_attn_b_proj_b',
    'L0_attn_b_norm1_w', 'L0_attn_b_norm2_w', 'L0_attn_b_mlp_w1', 'L0_attn_b_mlp_b1', 'L0_attn_b_mlp_w2',
    'L0_attn_b_mlp_b2', 'L0_ffn_Wg', 'L0_ffn_bg', 'L0_ffn_W1', 'L0_ffn_b1', 'L0_ffn_W2', 'L0_ffn_b2',
]
PHASES = "AFBG"


def kernel(**inputs):
    import numpy as _np
    import concourse.bacc as _bacc
    from concourse import mybir as _mybir
    from concourse.bass_utils import run_bass_kernel_spmd as _run

    nc = _bacc.Bacc("TRN2", target_bir_lowering=False, num_devices=1)
    arrays, aps = {}, {}
    for name in _INS:
        arr = _np.ascontiguousarray(inputs[name])
        shape = arr.shape if arr.ndim and inputs[name].ndim else (1,)
        arrays[f"in_{name}_dram"] = arr.reshape(shape)
        aps[name[3:]] = nc.dram_tensor(f"in_{name}_dram", shape, _mybir.dt.from_np(arr.dtype), kind="ExternalInput").ap()
    out = nc.dram_tensor("out_0_dram", (NT * P, P), F32, kind="ExternalOutput").ap()
    build(nc, aps, out, PHASES)
    r = _run(nc, [arrays], core_ids=[0])
    return r.results[0]["out_0_dram"].reshape(NB, TB * P, P)
```

```python
from contextlib import ExitStack

import concourse.bass as bass
from concourse import mybir

ALU = mybir.AluOpType
ACT = mybir.ActivationFunctionType
AX_X = mybir.AxisListType.X
F32 = mybir.dt.float32
I32 = mybir.dt.int32
U32 = mybir.dt.uint32

P = 128
ROW = P + 4
MEAN, RSTD, ID = P, P + 1, P + 2
NB = 4
TB = 8
NT = NB * TB
NE = 8
HC = 4
EPS = 1e-5
NS = (NT * P + NE * (P - 1)) // P
U = 3
assert NS % U == 0


class Chain:

    def __init__(self, engine, sem):
        self.engine, self.sem, self.base, self.n = engine, sem, 0, 0

    def __call__(self, ins):
        self.n += 1
        ins.then_inc(self.sem, 1)
        self.engine.wait_ge(self.sem, self.base + self.n)

    def loop(self, i, per_turn, start):
        self.base, self.n = start + i * per_turn, 0

    def leave(self, turns, per_turn, start):
        assert self.n == per_turn, (self.n, per_turn)
        self.base, self.n = start + turns * per_turn, 0


def build(nc, D, out, phases):
    with ExitStack() as ctx:
        def sb(name, shape, dt=F32):
            return ctx.enter_context(nc.sbuf_tensor(name, shape, dt))

        credits = []

        def sem(name, credit=0):
            handle = ctx.enter_context(nc.semaphore(name))
            if credit:
                credits.append((handle, credit))
            return handle

        sorted_rows = [nc.dram_tensor(f"sorted_rows{f}", [NS * P, ROW], F32, kind="Internal").ap() for f in range(2)]
        x2_rows = nc.dram_tensor("x2_rows", [NT * P, P], F32, kind="Internal").ap()

        W1 = sb("W1", [P, NE, HC * P + HC])
        W2 = sb("W2", [P, NE, HC, P])
        B2 = sb("B2", [1, NE, P])
        Wg = sb("Wg", [P, NE])
        bg = sb("bg", [P, NE])
        ident = sb("ident", [P, P])
        ones = sb("ones", [P, P])
        before = sb("before", [P, P])
        expert_m8 = sb("expert_m8", [P, NE])
        slot_no = sb("slot_no", [P, NS])
        not_first = sb("not_first", [P, NE, NT])
        minus_half = sb("minus_half", [P, 2 * TB])
        eps_ln = sb("eps_ln", [P, TB])
        eps_rms = sb("eps_rms", [P, TB])
        fill = sb("fill", [P, ROW])
        col = {n: sb("c_" + n, [P, 1]) for n in (
            "ln0_g", "ln0_b", "ln1_g", "ln1_b", "time_decay", "time_first", "tm_k", "tm_v", "tm_r", "cm_k", "cm_r",
            "norm1_w", "norm2_w")}
        rest = {n: sb("r_" + n, [P, 1]) for n in ("tm_k", "tm_v", "tm_r", "cm_k", "cm_r")}
        gelu_dummy = sb("gelu_dummy", [1, 1])
        decay = sb("decay", [P, 1])
        cg = sb("cg", [P, 1])
        cb = sb("cb", [P, 1])
        W_now = {n: sb("now_" + n, [P, P]) for n in ("k", "v", "r", "cr")}
        W_shift = {n: sb("shift_" + n, [P, P]) for n in ("k", "v", "r", "cr")}
        Wo = sb("Wo", [P, P])
        Wck = sb("Wck", [P, HC * P])
        Wcv = sb("Wcv", [P, HC, P])
        R = 16
        BLK = 32
        NBLK = P // BLK
        uv = sb("uv", [P, 2 * R])
        projT = sb("projT", [P, P])
        pb = sb("pb", [P, P])
        M1 = sb("M1", [P, HC * P])
        M2 = sb("M2", [P, HC, P])
        mb1 = sb("mb1", [P, HC])
        mb2 = sb("mb2", [P, P])
        g128 = sb("g128", [64, 1])
        G = sb("G", [P, 3, NBLK, R])
        causal = sb("causal", [P, P])
        conv = sb("conv", [P, P])
        conv_prev = sb("conv_prev", [P, 4])

        Xrow = sb("Xrow", [P, NT, ROW])
        posi = [sb(f"posi{f}", [P, NT], U32) for f in range(2)]
        texp = [sb(f"texp{f}", [P, NS], I32) for f in range(2)]

        ARENA = 32540
        arena = sb("arena", [P, ARENA])
        sizes = {}

        class Scratch:
            def __init__(self, name):
                self.name, self.at = name, 0

            def __call__(self, *dims, parts=P):
                n = 1
                for d in dims:
                    n *= d
                ap = arena[0:parts, self.at:self.at + n]
                self.at += n
                assert self.at <= ARENA, (self.name, self.at)
                if len(dims) > 1:
                    names = ["a", "b", "c", "d"][:len(dims)]
                    ap = ap.rearrange(f"p ({' '.join(names)}) -> p {' '.join(names)}", **dict(zip(names, dims)))
                return ap

        fs = Scratch("ffn")
        x_rows = fs(NS, ROW)
        y_rows = fs(NS, P)
        z8 = fs(TB, P)
        z8T = fs(TB * P)
        bst = fs(TB, 6)
        sm = fs(12, TB)
        lg = fs(NT, NE)
        eq = fs(NT, NE)
        top = fs(NT)
        oh = fs(NE, NT)
        run = fs(NE, NT)
        pos3 = fs(NE, NT)
        nti = fs(NE).bitcast(I32)
        ntf = fs(NE)
        endt = fs(NE)
        baset = fs(NE)
        posf = fs(NT)
        cmp_ = fs(NS, NE)
        texf = fs(NS)
        zs = [fs(P) for u in range(U)]
        zsT = [fs(P) for u in range(U)]
        w1cur = [fs(HC * P) for u in range(U)]
        hT = [fs(HC, P) for u in range(U)]

        bs = Scratch("attn_b")
        setup = sb("setup", [P, 1500])
        setup_at = [0]

        def su(*dims, parts=P):
            n = 1
            for d in dims:
                n *= d
            ap = setup[0:parts, setup_at[0]:setup_at[0] + n]
            setup_at[0] += n
            if len(dims) > 1:
                names = ["a", "b", "c"][:len(dims)]
                ap = ap.rearrange(f"p ({' '.join(names)}) -> p {' '.join(names)}", **dict(zip(names, dims)))
            return ap

        proj_in = su(P)
        dl = su(3, R)
        dcol = su(2, parts=64)
        cst = su(8)
        hundred28 = su(1, parts=64)
        expo = su(3, NBLK, R)
        gmask = su(3, NBLK, R)
        dist = su(P)
        ctmp = su(P)
        gam = su(3, NBLK, R)
        hna = bs(TB, P)
        hn = bs(TB, P)
        hnT = bs(TB * P)
        qks = bs(TB, 2, R)
        sq = bs(TB, 2, R)
        n2 = bs(TB, 2)
        rn = bs(TB, 2)
        KQ = bs(TB, 2 * NBLK * R)
        kd = bs(TB, NBLK * R)
        kT = bs(TB * P, parts=64)
        qT = bs(TB * P, parts=64)
        AT = bs(TB, P)
        state = bs(TB, P, parts=64)
        oT = bs(TB * P)
        h2 = bs(TB, P)
        h2n = bs(TB, P)
        xh = bs(TB, P)
        h2T = bs(TB * P)
        hmT = bs(2, HC, 4 * P)
        bstb = bs(TB, 6)
        smb = bs(14, TB)
        smc = bs(14, TB)

        as_ = Scratch("attn_a")
        L = TB * P
        wraw = as_(4, P)
        a8 = as_(TB, P)
        Y = as_(NT, P)
        xa = as_(1 + L)
        p_ = as_(1 + L)
        aa = as_(1 + L)
        bb = as_(1 + L)
        E1 = as_(L)
        E2 = as_(L)
        E3 = as_(L)
        E4 = as_(L)
        vs = as_(L)
        av = as_(L)
        num = as_(L)
        den = as_(L)
        y0 = as_(L)
        th = as_(L)
        rw = as_(L)
        x1 = as_(TB, P)
        x1n = as_(TB, P)
        xc = as_(1 + L)
        ca = as_(L)
        mk = as_(L)
        kkr = [as_(512) for _ in range(2)]
        kk2 = as_(2, HC, 512)
        th2 = as_(L)
        bsta = as_(TB, 6)
        sma = as_(14, TB)
        smx = as_(14, TB)

        ps = [ctx.enter_context(nc.psum_tensor(f"ps{i}", [P, 512], F32)) for i in range(8)]

        w_loaded = sem("w_loaded")
        w_loaded2 = sem("w_loaded2")
        x_loaded = [sem(f"x_loaded{b}") for b in range(NB)]
        consts = sem("consts")
        pool_own = sem("pool_own")
        tables = sem("tables")
        filled = sem("filled")
        credit = sem("credit")
        dve_own = sem("dve_own")
        act_own = sem("act_own")
        act_setup = sem("act_setup")
        gpow = sem("gpow")
        gexp = sem("gexp")
        proj_turned = sem("proj_turned")
        proj_ready = sem("proj_ready")
        out_written = sem("out_written")
        CR = {"zt_copied": 2, "logits_done": 1, "h_psum": U, "zsT_psum": U, "h_ready": U, "y_psum": U, "y_ready": 2,
              "zt_psum": 1}
        S = [{n: sem(f"{n}{f}", CR.get(n, 0)) for n in (
            "ve_ready", "rstd_ready", "z_ready", "zt_psum", "zt_copied", "logits_done",
            "onehot_ready", "ranks_done", "pos_ready", "rows_scattered", "zs_ready", "zsT_psum",
            "zsT_ready", "h_psum", "h_ready", "y_psum", "y_ready",
            "y_scattered")} for f in range(2)]
        V = {n: sem(n + "_b", c) for n, c in (
            ("var_ready", 0), ("scale_ready", 0), ("hn_ready", 0), ("hn_held", 0), ("t1_psum", 0), ("hnT_ready", 0),
            ("qk_psum", 0), ("qk_copied", 0), ("n2_ready", 0), ("rn_ready", 0), ("kq_ready", 0),
            ("t2_psum", 0), ("kqT_ready", 0), ("u_psum", 0), ("state_ready", 0), ("at_psum", 0), ("at_ready", 0),
            ("o_psum", 1), ("oT_ready", 0), ("proj_psum", 0), ("h2_ready", 0), ("ms_ready", 0), ("s2_ready", 0),
            ("h2n_ready", 0), ("t3_psum", 1), ("h2T_ready", 0), ("xh_ready", 0),
            ("up_psum", 0), ("hm_ready", 2), ("down_psum", 2), ("x3_ready", 1), ("x3_half", 1))}
        x2_loaded = [sem(f"x2_loaded{b}") for b in range(NB)]
        A = {n: sem(n + "_a", c) for n, c in (
            ("var0_ready", 0), ("scale0_ready", 0), ("a8_ready", 0), ("t0_psum", 1), ("xa_ready", 0),
            ("k_psum", 0), ("v_psum", 0), ("r_psum", 0), ("v_copied", 0), ("r_tanh", 0), ("kv_used", 1),
            ("d12_ready", 0), ("s_ready", 0), ("e12_ready", 0), ("e34_ready", 0), ("av_ready", 0), ("e4v_ready", 0),
            ("scan_ready", 0), ("n1_ready", 0), ("num_ready", 0), ("den_ready", 0), ("y0_ready", 0), ("qt_ready", 0), ("rw_ready", 0),
            ("wo_psum", 1), ("x1_ready", 0), ("var1_ready", 0), ("scale1_ready", 0), ("x1n_ready", 0),
            ("t1_psum", 0), ("xc_ready", 0), ("ca_ready", 0), ("mk_ready", 0), ("cr_psum", 0), ("ck_psum", 2), ("relu_ready", 2),
            ("kk_ready", 2), ("cv_psum", 2), ("th2_ready", 1), ("xx_ready", 0), ("x1_done", 1))}
        w_loads = [[sem(f"tile_weights{f}_{u}") for u in range(U)] for f in range(2)]
        loads = [sem(f"rows_loaded{f}") for f in range(2)]

        block = ctx.enter_context(nc.Block())

        vec = "(p a) -> p a"
        first_loads = [(col[n][:], D["attn_a_" + n].rearrange(vec, a=1)) for n in (
            "ln0_g", "ln0_b", "ln1_g", "ln1_b", "time_decay", "time_first", "tm_k", "tm_v", "tm_r", "cm_k", "cm_r")]
        first_loads += [(wraw[:, j, :], D["attn_a_" + n]) for j, n in enumerate(("Wk", "Wv", "Wr", "Wcr"))]
        first_loads += [
            (Wo[:], D["attn_a_Wo"]),
            (Wck[:], D["attn_a_Wck"]),
            (Wcv[:], D["attn_a_Wcv"].rearrange("(k p) c -> p k c", p=P)),
        ]
        second_loads = [(col[n][:], D["attn_b_" + n].rearrange(vec, a=1)) for n in ("norm1_w", "norm2_w")]
        second_loads += [
            (uv[:, 0:R], D["attn_b_u"]),
            (uv[:, R:2 * R], D["attn_b_v"]),
            (proj_in, D["attn_b_proj_w"]),
            (pb[:], D["attn_b_proj_b"].partition_broadcast(P)),
            (M1[:], D["attn_b_mlp_w1"]),
            (M2[:], D["attn_b_mlp_w2"].rearrange("(k p) c -> p k c", p=P)),
            (mb1[:], D["attn_b_mlp_b1"].rearrange("(k p) -> p k", p=P)),
            (mb2[:], D["attn_b_mlp_b2"].partition_broadcast(P)),
            (dl[:, 0, :], D["attn_b_decay_logit"].partition_broadcast(P)),
            (dl[:, 1, :], D["attn_b_alpha_logit"].partition_broadcast(P)),
            (cst[:, 0:4], D["attn_b_k_base_kernel"].partition_broadcast(P)),
            (cst[:, 4:5], D["attn_b_k_base_gate_logit"].partition_broadcast(P)),
        ]
        second_loads += [(dcol[R * g:R * g + R, 0:1], D["attn_b_decay_logit"].rearrange(vec, a=1)) for g in range(NBLK)]
        second_loads += [
            (Wg[:], D["ffn_Wg"]),
            (bg[:], D["ffn_bg"].partition_broadcast(P)),
            *((W1[:, e, HC * P:], D["ffn_b1"][e].rearrange("(k p) -> p k", p=P)) for e in range(NE)),
            (B2[:], D["ffn_b2"].unsqueeze(0)),
            (W1[:, :, 0:HC * P], D["ffn_W1"].rearrange("e c h -> c e h")),
            (W2[:], D["ffn_W2"].rearrange("e (k p) d -> p e k d", p=P)),
        ]
        W_FIRST, W_SECOND = 16 * len(first_loads), 16 * len(second_loads)

        Y_BANK = [6, 7, 6]
        Y_BACK = 2
        last = {0: x2_rows, 1: out}
        if "B" not in phases:
            last[0] = out

        @block.sync
        def _(sp):
            for handle, count in credits:
                sp.sem_inc(handle, count)
            x_view = D["attn_a_x"].rearrange("b (t p) c -> b p t c", p=P)
            with nc.allow_non_contiguous_dma(reason="vectors onto partitions"):
                sp.dma_start(Xrow[:, 0:TB, 0:P], x_view[0]).then_inc(x_loaded[0], 16)
                for dst, src in first_loads:
                    sp.dma_start(dst, src).then_inc(w_loaded, 16)
                for b in range(1, NB):
                    sp.dma_start(Xrow[:, b * TB:(b + 1) * TB, 0:P], x_view[b]).then_inc(x_loaded[b], 16)
                for dst, src in second_loads:
                    sp.dma_start(dst, src).then_inc(w_loaded2, 16)
            sp.wait_ge(consts, 1)
            for f in range(2):
                sp.dma_start(sorted_rows[f].rearrange("(s p) w -> p s w", p=P),
                             fill[:].unsqueeze(1).to_broadcast([P, NS, ROW])).then_inc(filled, 16)

            def slot_loads(f):
                view = sorted_rows[f].rearrange("(s p) w -> s p w", p=P)

                def rows(i):
                    sp.dma_start(x_rows[:, bass.ds(i * U, U), :], view[bass.ds(i * U, U)].rearrange("a p w -> p a w")).then_inc(loads[f], 16)

                def weights(u, i):
                    g = i * U + u
                    e = sp.value_load(texp[f][0:1, bass.ds(g, 1)], min_val=0, max_val=NE - 1)
                    sp.wait_ge(S[f]["h_psum"], g + 1)
                    sp.dma_start(w1cur[u], W1[:, bass.ds(e, 1), 0:HC * P].rearrange("p a c -> p (a c)")).then_inc(w_loads[f][u], 16)

                sp.wait_ge(S[f]["pos_ready"], 2)
                for u in range(U):
                    weights(u, 0)
                sp.wait_ge(S[f]["rows_scattered"], 16 * NT)
                rows(0)
                sp.wait_ge(loads[f], 16)
                rows(1)
                with sp.Fori(1, NS // U - 1) as i:
                    sp.wait_ge(loads[f], 16 * i + 16)
                    rows(i + 1)
                    for u in range(U):
                        sp.wait_ge(w_loads[f][u], 16 * i)
                        weights(u, i)
                for u in range(U):
                    sp.wait_ge(w_loads[f][u], 16 * (NS // U - 1))
                    weights(u, NS // U - 1)

            def write_rows(done, n):
                sp.wait_ge(w_loaded2, W_SECOND)
                sp.wait_ge(done, n)
                sp.dma_start(out.rearrange("(t p) c -> p t c", p=P), Xrow[:, :, 0:P]).then_inc(out_written, 16)
                sp.wait_ge(out_written, 16)

            if phases == "A":
                write_rows(A["x1_done"], NB + 1)
            if "F" in phases:
                slot_loads(0)
                sp.wait_ge(S[0]["y_scattered"], 16 * NS)
            if "B" in phases:
                for b in range(NB):
                    sp.wait_ge(x_loaded[b], 16)
                    sp.dma_start(Xrow[:, b * TB:(b + 1) * TB, 0:P],
                                 (x2_rows if "F" in phases else D["attn_a_x"].rearrange("b t c -> (b t) c")).rearrange("(b t p) c -> b p t c", p=P, t=TB)[b]).then_inc(x2_loaded[b], 16)
                if "G" not in phases:
                    write_rows(V["x3_half"], 2 * NB + 1)
            if "G" in phases:
                slot_loads(1)
                sp.wait_ge(S[1]["y_scattered"], 16 * NS)

        @block.gpsimd
        def _(pool):
            own = Chain(pool, pool_own)
            nc.gpsimd.memset(ident[:], 0.0)
            nc.gpsimd.memset(ones[:], 1.0)
            nc.gpsimd.memset(minus_half[:], -0.5)
            nc.gpsimd.memset(eps_ln[:], EPS)
            nc.gpsimd.memset(eps_rms[:], 1e-6)
            nc.gpsimd.memset(not_first[:], 1.0)
            nc.gpsimd.memset(hundred28[:], float(P))
            own(nc.gpsimd.memset(fill[:], 0.0))
            nc.gpsimd.memset(fill[:, ID:ID + 1].bitcast(I32), NT * P).then_inc(consts, 1)
            nc.gpsimd.affine_select(out=ident[:], in_=ident[:], compare_op=ALU.not_equal, fill=1.0, base=0,
                                    pattern=[[-1, P]], channel_multiplier=1).then_inc(consts, 1)
            for line in (xa, p_, aa, bb, xc):
                nc.gpsimd.memset(line[:, 0:1], -1e38 if line is p_ else 0.0)
            nc.gpsimd.affine_select(out=before[:], in_=ones[:], compare_op=ALU.is_gt, fill=0.0, base=0,
                                    pattern=[[1, P]], channel_multiplier=-1)
            nc.gpsimd.affine_select(out=causal[:], in_=ones[:], compare_op=ALU.is_ge, fill=0.0, base=0,
                                    pattern=[[1, P]], channel_multiplier=-1)
            nc.gpsimd.iota(expert_m8[:], [[1, NE]], base=-NE, channel_multiplier=0, allow_small_or_imprecise_dtypes=True)
            nc.gpsimd.iota(slot_no[:], [[1, NS]], base=0, channel_multiplier=0, allow_small_or_imprecise_dtypes=True)
            nc.gpsimd.iota(dist, [[1, P]], base=0, channel_multiplier=-1, allow_small_or_imprecise_dtypes=True)
            nc.gpsimd.iota(expo[:, 0], [[BLK, NBLK], [0, R]], base=0, channel_multiplier=-1, allow_small_or_imprecise_dtypes=True)
            nc.gpsimd.iota(expo[:, 1], [[-BLK, NBLK], [0, R]], base=0, channel_multiplier=1, allow_small_or_imprecise_dtypes=True)
            nc.gpsimd.iota(expo[:, 2], [[BLK, NBLK], [0, R]], base=P, channel_multiplier=-1, allow_small_or_imprecise_dtypes=True)
            nc.gpsimd.iota(Xrow[:, :, ID:ID + 1].rearrange("p t w -> p (t w)").bitcast(I32), [[P, NT]], base=0, channel_multiplier=1)
            nc.gpsimd.memset(Xrow[:, :, ID + 1:ROW], 0.0)
            nc.gpsimd.memset(not_first[:, :, 0:1], 0.0).then_inc(consts, 1)

            def rstd_chain(var, sems, n, sm_, second):
                pool.wait_ge(sems[0], n)
                own(nc.gpsimd.tensor_tensor(sm_[:, 7, :], var, eps_ln[:], ALU.add))
                ins = nc.gpsimd.tensor_tensor(sm_[:, 5, :], sm_[:, 7, :], minus_half[:, 0:TB], ALU.pow)
                if second is not None:
                    own(ins)
                    own(nc.gpsimd.tensor_tensor(sm_[:, 8, :], sm_[:, 5, :], sm_[:, 5, :], ALU.mult))
                    own(nc.gpsimd.tensor_tensor(sm_[:, 8, :], sm_[:, 8, :], var, ALU.mult))
                    own(nc.gpsimd.tensor_tensor(sm_[:, 8, :], sm_[:, 8, :], second[:], ALU.add))
                    own(nc.gpsimd.tensor_tensor(sm_[:, 9, :], sm_[:, 8, :], minus_half[:, 0:TB], ALU.pow))
                    own(nc.gpsimd.tensor_tensor(sm_[:, 7, :], sm_[:, 8, :], sm_[:, 9, :], ALU.mult))
                    ins = nc.gpsimd.tensor_tensor(sm_[:, 6, :], sm_[:, 5, :], sm_[:, 9, :], ALU.mult)
                ins.then_inc(sems[1], 1)

            def a_products(b, h):
                c = slice(512 * h, 512 * h + 512)
                pool.wait_ge(A["e12_ready"], 2 * b + h + 1)
                pool.wait_ge(A["v_copied"], b + 1)
                nc.gpsimd.tensor_tensor(av[:, c], E2[:, c], vs[:, c], ALU.mult).then_inc(A["av_ready"], 1)
                pool.wait_ge(A["e34_ready"], 2 * b + h + 1)
                own(nc.gpsimd.tensor_tensor(num[:, c], E4[:, c], vs[:, c], ALU.mult))

            def a_numerator(b, h):
                c = slice(512 * h, 512 * h + 512)
                pool.wait_ge(A["scan_ready"], 2 * b + h + 1)
                own(nc.gpsimd.tensor_tensor(av[:, c], E3[:, c], aa[:, c], ALU.mult))
                own(nc.gpsimd.tensor_tensor(num[:, c], num[:, c], av[:, c], ALU.add))

            def a_quotient(b):
                pool.wait_ge(A["y0_ready"], b + 1)
                nc.gpsimd.tensor_tensor(num, num, y0, ALU.mult)
                nc.gpsimd.tensor_tensor(den, den, y0, ALU.mult).then_inc(A["qt_ready"], 1)

            def a_streams(b):
                nc.gpsimd.tensor_tensor(x1, Xrow[:, bass.ts(b, TB), 0:P], x1, ALU.add).then_inc(A["xx_ready"], 1)

            def rstd0(b):
                rstd_chain(sma[:, 4, :], (A["var0_ready"], A["scale0_ready"]), b + 1, sma, eps_ln)

            def rstd1(b):
                rstd_chain(smx[:, 4, :], (A["var1_ready"], A["scale1_ready"]), b + 1, smx, None)

            if "A" in phases:
                def a_body(b, behind=True, ahead=True):
                    if behind:
                        rstd1(b - 1)
                    if ahead:
                        rstd0(b + 1)
                    a_products(b, 0)
                    a_products(b, 1)
                    if behind:
                        pool.wait_ge(A["x1n_ready"], b)
                    a_numerator(b, 0)
                    a_numerator(b, 1)
                    if behind:
                        a_streams(b - 1)
                    a_quotient(b)

                rstd0(0)
                a_body(0, behind=False)
                start = own.base + own.n
                K = 7 + 1 + 2 * 3
                with pool.Fori(1, NB - 1) as b:
                    own.loop(b - 1, K, start)
                    a_body(b)
                own.leave(NB - 2, K, start)
                a_body(NB - 1, ahead=False)
                rstd1(NB - 1)
                pool.wait_ge(A["x1n_ready"], NB)
                a_streams(NB - 1)

            def b_tables():
                pool.wait_ge(gexp, 1)
                nc.gpsimd.tensor_tensor(G[:].rearrange("p a b r -> p (a b r)"), gam.rearrange("p a b r -> p (a b r)"), expo.rearrange("p a b r -> p (a b r)"), ALU.pow)
                nc.gpsimd.tensor_tensor(g128[:], dcol[:, 1:2], hundred28, ALU.pow).then_inc(gpow, 1)

            def ffn_pool(f, target):
                s_ = S[f]
                with pool.Fori(0, NB) as b:
                    pool.wait_ge(s_["ve_ready"], b + 1)
                    nc.gpsimd.tensor_tensor(Xrow[:, bass.ts(b, TB), RSTD:RSTD + 1].rearrange("p t w -> p (t w)"), sm[:, 5, :], minus_half[:, 0:TB], ALU.pow).then_inc(s_["rstd_ready"], 1)
                pool.wait_ge(filled, 32)
                pool.wait_ge(s_["pos_ready"], 1)
                for t in range(NT):
                    nc.gpsimd.indirect_dma_start(
                        out=sorted_rows[f], out_offset=bass.IndirectOffsetOnAxis(posi[f][:, t:t + 1], 0),
                        in_=Xrow[:, t, :], in_offset=None).then_inc(s_["rows_scattered"], 16)

                if f == 0 and "B" in phases:
                    b_tables()
                for s in range(NS):
                    pool.wait_ge(s_["y_ready"], s + 1 + 2)
                    nc.gpsimd.indirect_dma_start(
                        out=target, out_offset=bass.IndirectOffsetOnAxis(x_rows[:, s, ID:ID + 1].bitcast(U32), 0),
                        in_=y_rows[:, s, :], in_offset=None, bounds_check=NT * P - 1,
                        oob_is_err=False).then_inc(s_["y_scattered"], 16)
                pool.wait_ge(s_["y_scattered"], 16 * NS)

            def b_rstd(b):
                rstd_chain(smb[:, 4, :], (V["var_ready"], V["scale_ready"]), b + 1, smb, eps_rms)

            def b_unit(b):
                pool.wait_ge(V["n2_ready"], b + 1)
                nc.gpsimd.tensor_tensor(rn.rearrange("p t s -> p (t s)"), n2.rearrange("p t s -> p (t s)"), minus_half[:], ALU.pow).then_inc(V["rn_ready"], 1)

            def b_norm2(b):
                pool.wait_ge(V["ms_ready"], b + 1)
                nc.gpsimd.tensor_tensor(smc[:, 12, :], smc[:, 11, :], minus_half[:, 0:TB], ALU.pow).then_inc(V["s2_ready"], 1)

            def b_residual(b):
                pool.wait_ge(V["x3_half"], 2 * b + 1)
                own(nc.gpsimd.tensor_tensor(xh, Xrow[:, bass.ts(b, TB), 0:P], h2, ALU.add))
                nc.gpsimd.tensor_tensor(xh, xh, mb2[:].unsqueeze(1).to_broadcast([P, TB, P]), ALU.add).then_inc(V["xh_ready"], 1)

            def b_body(b, ahead=True):
                if ahead:
                    b_rstd(b + 1)
                b_norm2(b)
                if ahead:
                    b_unit(b + 1)
                b_residual(b)

            if phases == "B":
                b_tables()
            if "F" in phases:
                ffn_pool(0, last[0])
            if "B" in phases:
                b_rstd(0)
                b_unit(0)
                b_body(0)
                start = own.base + own.n
                with pool.Fori(1, NB - 1) as b:
                    own.loop(b - 1, 8, start)
                    b_body(b)
                own.leave(NB - 2, 8, start)
                b_body(NB - 1, ahead=False)
            if "G" in phases:
                ffn_pool(1, out)

        @block.vector
        def _(dve):
            own = Chain(dve, dve_own)

            def stats(src, bst, sm):
                for t in range(TB):
                    ins = nc.vector.bn_stats(bst[:, t, :], src(t))
                own(ins)

                def part(k):
                    return bst[:, :, k:k + 1].rearrange("p t w -> p (t w)")
                nc.vector.tensor_tensor(sm[:, 1, :], part(1), part(4), ALU.add)
                nc.vector.tensor_tensor(sm[:, 2, :], part(4), part(1), ALU.subtract)
                own(nc.vector.tensor_tensor(sm[:, 3, :], part(2), part(5), ALU.add))
                nc.vector.tensor_scalar(sm[:, 0, :], sm[:, 1, :], 0.5, None, ALU.mult)
                own(nc.vector.scalar_tensor_tensor(sm[:, 2, :], sm[:, 2, :], 0.25 * P, sm[:, 2, :], ALU.mult, ALU.mult))
                own(nc.vector.tensor_tensor(sm[:, 3, :], sm[:, 2, :], sm[:, 3, :], ALU.add))
                return nc.vector.tensor_scalar(sm[:, 4, :], sm[:, 3, :], 1.0 / P, None, ALU.mult)
            STATS = 4

            def x_tile(b, t, width=P):
                return Xrow[:, bass.ds(b * TB + t, 1), 0:width].rearrange("p a c -> p (a c)")

            def a_tables():
                dve.wait_ge(w_loaded, W_FIRST)
                for n in rest:
                    ins = nc.vector.tensor_scalar(rest[n][:], col[n][:], -1.0, 1.0, ALU.mult, ALU.add)
                own(ins)
                for j, (n, m) in enumerate((("k", "tm_k"), ("v", "tm_v"), ("r", "tm_r"), ("cr", "cm_r"))):
                    nc.vector.tensor_scalar(W_now[n][:], wraw[:, j, :], col[m][:], None, ALU.mult)
                    nc.vector.tensor_scalar(W_shift[n][:], wraw[:, j, :], rest[m][:], None, ALU.mult)
                nc.vector.tensor_scalar(Wo[:], Wo[:], -0.5, None, ALU.mult)
                nc.vector.tensor_tensor(cg[:], col["cm_k"][:], col["ln1_g"][:], ALU.mult)
                nc.vector.tensor_tensor(cb[:], col["cm_k"][:], col["ln1_b"][:], ALU.mult)
                dve.wait_ge(act_setup, 1)
                nc.vector.tensor_scalar(decay[:], decay[:], -1.0, None, ALU.mult).then_inc(tables, 1)
                dve.wait_ge(tables, 1)

            def a_stats(b):
                stats(lambda t: x_tile(b, t), bsta, sma).then_inc(A["var0_ready"], 1)

            def a_norm0(b):
                dve.wait_ge(A["scale0_ready"], b + 1)
                dve.wait_ge(A["t0_psum"], b + 1)
                for t in range(TB):
                    ins = nc.vector.tensor_scalar(a8[:, t, :], x_tile(b, t), sma[:, 0, t:t + 1], sma[:, 6, t:t + 1], ALU.subtract, ALU.mult)
                ins.then_inc(A["a8_ready"], 1)

            def a_residual(b):
                for t in range(TB):
                    ins = nc.vector.tensor_scalar(Y[:, bass.ds(b * TB + t, 1), :].rearrange("p a c -> p (a c)"), x_tile(b, t), sma[:, 0, t:t + 1], sma[:, 5, t:t + 1], ALU.subtract, ALU.mult)
                own(ins)

            def a_exponents(b):
                for h in range(2):
                    c, c1 = slice(512 * h, 512 * h + 512), slice(512 * h + 1, 512 * h + 513)
                    kp = ps[2 + h][:]
                    dve.wait_ge(A["k_psum"], 2 * b + h + 1)
                    own(nc.vector.tensor_tensor_scan(p_[:, c1], decay[:].to_broadcast([P, 512]), kp, p_[:, 512 * h:512 * h + 1], ALU.add, ALU.max))
                    nc.vector.tensor_tensor(E2[:, c], kp, p_[:, c1], ALU.subtract)
                    nc.vector.scalar_tensor_tensor(E1[:, c], p_[:, c], decay[:], p_[:, c1], ALU.add, ALU.subtract).then_inc(A["d12_ready"], 1)
                    nc.vector.scalar_tensor_tensor(E3[:, c], kp, col["time_first"][:], p_[:, c], ALU.add, ALU.subtract).then_inc(A["s_ready"], 1)

            def a_scans(b, h):
                c, c1 = slice(512 * h, 512 * h + 512), slice(512 * h + 1, 512 * h + 513)
                dve.wait_ge(A["e12_ready"], 2 * b + h + 1)
                nc.vector.tensor_tensor_scan(bb[:, c1], E1[:, c], E2[:, c], bb[:, 512 * h:512 * h + 1] if h else 0.0, ALU.mult, ALU.add)
                dve.wait_ge(A["av_ready"], 2 * b + h + 1)
                nc.vector.tensor_tensor_scan(aa[:, c1], E1[:, c], av[:, c], aa[:, 512 * h:512 * h + 1] if h else 0.0, ALU.mult, ALU.add).then_inc(A["scan_ready"], 1)
                dve.wait_ge(A["scan_ready"], 2 * b + h + 1)
                dve.wait_ge(A["e34_ready"], 2 * b + h + 1)
                own(nc.vector.tensor_tensor(den[:, c], E3[:, c], bb[:, c], ALU.mult))
                nc.vector.tensor_tensor(den[:, c], den[:, c], E4[:, c], ALU.add).then_inc(A["den_ready"], 1)

            def a_rw(b):
                dve.wait_ge(A["qt_ready"], b + 1)
                dve.wait_ge(A["r_tanh"], b + 1)
                own(nc.vector.scalar_tensor_tensor(th, th, 1.0, num, ALU.add, ALU.mult))
                nc.vector.scalar_tensor_tensor(rw, den, -2.0, th, ALU.add, ALU.mult).then_inc(A["rw_ready"], 1)

            def a_x1(b):
                dve.wait_ge(A["x1_done"], b + 1)
                for h in range(2):
                    dve.wait_ge(A["wo_psum"], 2 * b + h + 1 + 1)
                    ins = nc.vector.tensor_tensor(x1[:, 4 * h:4 * h + 4, :], ps[6 + h][:].rearrange("p (t c) -> p t c", c=P),
                                                  Y[:, bass.ds(b * TB + 4 * h, 4), :], ALU.add)
                own(ins)
                stats(lambda t: x1[:, t, :], bsta, smx).then_inc(A["var1_ready"], 1)

            def a_norm1(b):
                dve.wait_ge(A["scale1_ready"], b + 1)
                for t in range(TB):
                    ins = nc.vector.tensor_scalar(x1n[:, t, :], x1[:, t, :], smx[:, 0, t:t + 1], smx[:, 5, t:t + 1], ALU.subtract, ALU.mult)
                ins.then_inc(A["x1n_ready"], 1)

            def a_mix(b):
                dve.wait_ge(A["ca_ready"], b + 1)
                nc.vector.scalar_tensor_tensor(mk, xc[:, 0:L], rest["cm_k"][:], ca, ALU.mult, ALU.add).then_inc(A["mk_ready"], 1)

            def a_final(b):
                dve.wait_ge(A["th2_ready"], b + 2)
                dve.wait_ge(A["xx_ready"], b + 1)
                for h in range(2):
                    dve.wait_ge(A["cv_psum"], 2 * b + h + 1 + 2)
                    t4 = th2[:, 512 * h:512 * h + 512]
                    own(nc.vector.scalar_tensor_tensor(t4, t4, 1.0, ps[2 + h][:], ALU.add, ALU.mult))
                    ins = nc.vector.scalar_tensor_tensor(Xrow[:, bass.ds(b * TB + 4 * h, 4), 0:P], t4.rearrange("p (t c) -> p t c", c=P), 0.5, x1[:, 4 * h:4 * h + 4, :], ALU.mult, ALU.add)
                ins.then_inc(A["x1_done"], 1)

            def a_body(b, behind=True, ahead=True):
                if behind:
                    a_x1(b - 1)
                if ahead:
                    a_stats(b + 1)
                a_exponents(b)
                if behind:
                    a_norm1(b - 1)
                a_scans(b, 0)
                a_scans(b, 1)
                if behind:
                    a_mix(b - 1)
                if ahead:
                    a_norm0(b + 1)
                    a_residual(b + 1)
                a_rw(b)
                if behind:
                    a_final(b - 1)

            def attn_a():
                dve.wait_ge(x_loaded[0], 16)
                a_stats(0)
                a_norm0(0)
                a_residual(0)
                a_tables()
                for b in range(1, NB):
                    dve.wait_ge(x_loaded[b], 16)
                a_body(0, behind=False)
                start = own.base + own.n
                K = 1 + 2 * STATS + 2 + 2 + 1 + 1 + 2
                with dve.Fori(1, NB - 1) as b:
                    own.loop(b - 1, K, start)
                    a_body(b)
                own.leave(NB - 2, K, start)
                a_body(NB - 1, ahead=False)
                a_x1(NB - 1)
                a_norm1(NB - 1)
                a_mix(NB - 1)
                a_final(NB - 1)
                dve.wait_ge(A["x1_done"], NB + 1)

            def gate_loop(f):
                s_ = S[f]
                start = own.base + own.n
                K = STATS + 2
                with dve.Fori(0, NB) as b:
                    own.loop(b, K, start)
                    own(stats(lambda t: x_tile(b, t), bst, sm))
                    own(nc.vector.tensor_copy(Xrow[:, bass.ts(b, TB), MEAN:MEAN + 1].rearrange("p t w -> p (t w)"), sm[:, 0, :]))
                    nc.vector.tensor_scalar(sm[:, 5, :], sm[:, 4, :], EPS, None, ALU.add).then_inc(s_["ve_ready"], 1)
                    dve.wait_ge(s_["rstd_ready"], b + 1)
                    dve.wait_ge(s_["zt_psum"], b + 1)
                    for t in range(TB):
                        row = x_tile(b, t, ROW)
                        ins = nc.vector.tensor_scalar(z8[:, t, :], row[:, 0:P], row[:, MEAN:MEAN + 1], row[:, RSTD:RSTD + 1], ALU.subtract, ALU.mult)
                    ins.then_inc(s_["z_ready"], 1)
                own.leave(NB, K, start)

            def flat(ap):
                return ap.rearrange("p e t -> p (e t)")

            def route(f):
                s_ = S[f]
                dve.wait_ge(s_["logits_done"], NB + 1)
                own(nc.vector.tensor_tensor(lg, ps[2][:, 0:NT * NE].rearrange("p (t e) -> p t e", e=NE), bg[:].unsqueeze(1).to_broadcast([P, NT, NE]), ALU.add))
                own(nc.vector.tensor_reduce(top, lg, AX_X, ALU.max))
                own(nc.vector.tensor_tensor(eq, lg, top.unsqueeze(2).to_broadcast([P, NT, NE]), ALU.is_ge))
                own(nc.vector.tensor_tensor(eq, eq, expert_m8[:].unsqueeze(1).to_broadcast([P, NT, NE]), ALU.mult))
                own(nc.vector.tensor_reduce(top, eq, AX_X, ALU.min))
                nc.vector.tensor_tensor(oh, expert_m8[:].unsqueeze(2).to_broadcast([P, NE, NT]), top.unsqueeze(1).to_broadcast([P, NE, NT]), ALU.is_equal).then_inc(s_["onehot_ready"], 1)
                dve.wait_ge(s_["ranks_done"], 1)
                tot = ps[4][:, 0:NE * NT]
                own(nc.vector.tensor_tensor_scan(flat(run), flat(not_first[:]), tot, 0.0, ALU.mult, ALU.add))
                own(nc.vector.tensor_scalar(ntf, flat(run[:, :, NT - 1:NT]), float(P - 1), None, ALU.add))
                own(nc.vector.tensor_copy(nti, ntf))
                own(nc.vector.tensor_scalar(nti, nti, 7, None, ALU.arith_shift_right))
                own(nc.vector.tensor_copy(ntf, nti))
                own(nc.vector.tensor_tensor_scan(endt, ones[:, 0:NE], ntf, 0.0, ALU.mult, ALU.add))
                own(nc.vector.tensor_tensor(baset, endt, ntf, ALU.subtract))
                own(nc.vector.tensor_tensor(flat(run), flat(run), tot, ALU.subtract))
                own(nc.vector.tensor_tensor(flat(run), flat(run), ps[3][:, 0:NE * NT], ALU.add))
                own(nc.vector.scalar_tensor_tensor(run, baset.unsqueeze(2).to_broadcast([P, NE, NT]), float(P), run, ALU.mult, ALU.add))
                own(nc.vector.tensor_tensor(pos3, run, oh, ALU.mult))
                own(nc.vector.tensor_reduce(posf, pos3.rearrange("p e t -> p t e"), AX_X, ALU.add))
                nc.vector.tensor_copy(posi[f][:], posf).then_inc(s_["pos_ready"], 1)
                own(nc.vector.tensor_tensor(cmp_, endt.unsqueeze(1).to_broadcast([P, NS, NE]), slot_no[:].unsqueeze(2).to_broadcast([P, NS, NE]), ALU.is_le))
                own(nc.vector.tensor_reduce(texf, cmp_, AX_X, ALU.add))
                own(nc.vector.tensor_scalar(texf, texf, float(NE - 1), None, ALU.min))
                nc.vector.tensor_copy(texp[f][:], texf).then_inc(s_["pos_ready"], 1)
                dve.wait_ge(s_["pos_ready"], 2)

            def experts(f):
                s_ = S[f]

                def finish(u, g):
                    y = y_rows[:, bass.ds(g, 1), :].rearrange("p a c -> p (a c)")
                    x = x_rows[:, bass.ds(g, 1), 0:P].rearrange("p a c -> p (a c)")
                    dve.wait_ge(s_["y_psum"], g + 1 + U)
                    nc.vector.tensor_tensor(y, ps[Y_BANK[u]][:, 0:P], x, ALU.add).then_inc(s_["y_ready"], 1)

                def turn(i, first):
                    for u in range(U):
                        g = i * U + u
                        if u == 0:
                            dve.wait_ge(loads[f], 16 * i + 16)
                        dve.wait_ge(s_["zsT_psum"], g + 1)
                        row = x_rows[:, bass.ds(g, 1), :].rearrange("p a c -> p (a c)")
                        nc.vector.tensor_scalar(zs[u], row[:, 0:P], row[:, MEAN:MEAN + 1], row[:, RSTD:RSTD + 1], ALU.subtract, ALU.mult).then_inc(s_["zs_ready"], 1)
                        dve.wait_ge(s_["h_psum"], g + 1)
                        dve.wait_ge(s_["zsT_psum"], g + 1 + U)
                        nc.vector.tensor_copy(zsT[u], ps[u][:, 0:P]).then_inc(s_["zsT_ready"], 1)
                        if not first:
                            finish(u, g - U)

                turn(0, True)
                with dve.Fori(1, NS // U) as i:
                    turn(i, False)
                for u in range(U):
                    finish(u, NS - U + u)
                own(nc.vector.tensor_copy(posf[:, 0:1], posf[:, 1:2]))

            def b_tables():
                dve.wait_ge(w_loaded2, W_SECOND)
                nc.vector.tensor_scalar(uv[:], uv[:], col["norm1_w"][:], None, ALU.mult)
                nc.vector.tensor_scalar(M1[:], M1[:], col["norm2_w"][:], None, ALU.mult)
                dve.wait_ge(act_setup, 5)
                nc.vector.tensor_scalar(cst[:, 4:5], cst[:, 4:5], 0.5, 0.5, ALU.mult, ALU.add)
                nc.vector.tensor_scalar(dcol[:, 0:1], dcol[:, 0:1], 0.5, 0.5, ALU.mult, ALU.add)
                own(nc.vector.tensor_scalar(dl[:, 0:2], dl[:, 0:2], 0.5, 0.5, ALU.mult, ALU.add))
                nc.vector.tensor_scalar(dcol[:, 1:2], dcol[:, 0:1], 0.15, 1.0, ALU.max, ALU.min)
                nc.vector.tensor_scalar(cst[:, 0:4], cst[:, 0:4], cst[:, 4:5], None, ALU.mult)
                own(nc.vector.tensor_scalar(dl[:, 2], dl[:, 0], 0.15, 1.0, ALU.max, ALU.min))
                g2 = dl[:, 2].unsqueeze(1).to_broadcast([P, 3 * NBLK, R])
                own(nc.vector.tensor_copy(gam.rearrange("p a b r -> p (a b) r"), g2))
                nc.vector.tensor_scalar(gmask[:, 0], expo[:, 0], 0.5 - BLK, None, ALU.is_gt)
                nc.vector.tensor_scalar(gmask[:, 2], expo[:, 1], BLK - 0.5, None, ALU.is_lt)
                own(nc.vector.tensor_scalar(gmask[:, 1], expo[:, 1], -0.5, None, ALU.is_gt))
                own(nc.vector.tensor_tensor(gmask[:, 1], gmask[:, 1], gmask[:, 2], ALU.mult))
                own(nc.vector.tensor_tensor(gmask[:, 1], gmask[:, 1], dl[:, 1].unsqueeze(1).to_broadcast([P, NBLK, R]), ALU.mult))
                nc.vector.tensor_scalar(expo[:, 0], expo[:, 0], float(-BLK), None, ALU.max)
                nc.vector.tensor_scalar(expo[:, 1], expo[:, 1], 0.0, None, ALU.max).then_inc(gexp, 1)
                nc.vector.tensor_scalar(conv[:], dist, 0.0, cst[:, 0:1], ALU.is_equal, ALU.mult)
                own(nc.vector.tensor_scalar(conv_prev[:], dist[:, 0:4], float(1 - P), cst[:, 1:2], ALU.is_equal, ALU.mult))
                for m in range(1, 4):
                    own(nc.vector.tensor_scalar(ctmp, dist, float(m), cst[:, m:m + 1], ALU.is_equal, ALU.mult))
                    own(nc.vector.tensor_tensor(conv[:], conv[:], ctmp, ALU.add))
                    if m > 1:
                        own(nc.vector.tensor_scalar(ctmp[:, 0:4], dist[:, 0:4], float(m - P), cst[:, m:m + 1], ALU.is_equal, ALU.mult))
                        own(nc.vector.tensor_tensor(conv_prev[:], conv_prev[:], ctmp[:, 0:4], ALU.add))

            def b_masks():
                dve.wait_ge(gpow, 1)
                own(nc.vector.tensor_tensor(G[:, 0:2].rearrange("p a b r -> p (a b r)"), G[:, 0:2].rearrange("p a b r -> p (a b r)"), gmask[:, 0:2].rearrange("p a b r -> p (a b r)"), ALU.mult))

            def b_stats(b):
                stats(lambda t: x_tile(b, t), bstb, smb).then_inc(V["var_ready"], 1)

            def b_norm1(b, first=False):
                dve.wait_ge(V["scale_ready"], b + 1)
                if not first:
                    dve.wait_ge(V["hn_held"], b)
                for t in range(TB):
                    ins = nc.vector.tensor_scalar(hna[:, t, :], x_tile(b, t), smb[:, 0, t:t + 1], smb[:, 6, t:t + 1], ALU.subtract, ALU.mult)
                ins.then_inc(V["hn_ready"], 1)

            def b_lengths(b):
                dve.wait_ge(V["qk_copied"], b + 1)
                own(nc.vector.tensor_tensor(sq, qks, qks, ALU.mult))
                own(nc.vector.tensor_reduce(n2, sq, AX_X, ALU.add))
                nc.vector.tensor_scalar(n2, n2, 1e-16, None, ALU.max).then_inc(V["n2_ready"], 1)

            def b_decayed(b):
                dve.wait_ge(V["rn_ready"], b + 1)
                own(nc.vector.tensor_tensor(sq, qks, rn.unsqueeze(3).to_broadcast([P, TB, 2, R]), ALU.mult))
                for dst, qk, table in ((KQ[:, :, 0:64], 1, 0), (KQ[:, :, 64:128], 0, 1), (kd, 1, 2)):
                    ins = nc.vector.tensor_tensor(dst.rearrange("p t (b r) -> p t b r", r=R),
                                                  sq[:, :, qk, :].unsqueeze(2).to_broadcast([P, TB, NBLK, R]),
                                                  G[:, table].unsqueeze(1).to_broadcast([P, TB, NBLK, R]), ALU.mult)
                ins.then_inc(V["kq_ready"], 1)
                own(nc.vector.tensor_copy(smc[:, 7, :], smb[:, 7, :]))

            def b_scores(b):
                for t in range(TB - 1):
                    src = ps[3 + t // 4][0:64, (t % 4) * P:(t % 4 + 1) * P]
                    if t % 4 == 0:
                        dve.wait_ge(V["u_psum"], 2 * b + t // 4 + 1)
                    if t == 0:
                        ins = nc.vector.tensor_copy(state[:, 1, :], src)
                    else:
                        ins = nc.vector.scalar_tensor_tensor(state[:, t + 1, :], state[:, t, :], g128[:], src, ALU.mult, ALU.add)
                    if t == 3 or t == TB - 2:
                        ins.then_inc(V["state_ready"], 1)
                        dve.wait_ge(V["state_ready"], 2 * b + (1 if t == 3 else 2))
                    else:
                        own(ins)
                for h in range(2):
                    dve.wait_ge(V["at_psum"], 2 * b + h + 1)
                    at = AT[:, 4 * h:4 * h + 4, :]
                    own(nc.vector.tensor_tensor(at, ps[2 + h][:].rearrange("p (t c) -> p t c", c=P), causal[:].unsqueeze(1).to_broadcast([P, 4, P]), ALU.mult))
                    nc.vector.tensor_tensor(at, at, conv[:].unsqueeze(1).to_broadcast([P, 4, P]), ALU.add).then_inc(V["at_ready"], 1)

            def b_h2(b, first):
                if not first:
                    dve.wait_ge(V["xh_ready"], b)
                for h in range(2):
                    dve.wait_ge(V["proj_psum"], 2 * b + h + 1)
                    hh = h2[:, 4 * h:4 * h + 4, :]
                    own(nc.vector.tensor_tensor(hh, ps[4 if h == 0 else 2][:].rearrange("p (t c) -> p t c", c=P), pb[:].unsqueeze(1).to_broadcast([P, 4, P]), ALU.add))
                    for t in range(4 * h, 4 * h + 4):
                        ins = nc.vector.scalar_tensor_tensor(h2[:, t, :], hn[:, t, :], smc[:, 7, t:t + 1], h2[:, t, :], ALU.mult, ALU.add)
                own(ins)
                own(stats(lambda t: h2[:, t, :], bstb, smc))
                own(nc.vector.tensor_tensor(smc[:, 10, :], smc[:, 0, :], smc[:, 0, :], ALU.mult))
                nc.vector.scalar_tensor_tensor(smc[:, 11, :], smc[:, 4, :], 1e-6, smc[:, 10, :], ALU.add, ALU.add).then_inc(V["ms_ready"], 1)

            def b_norm2(b):
                dve.wait_ge(V["s2_ready"], b + 1)
                dve.wait_ge(V["t3_psum"], b + 1)
                for t in range(TB):
                    ins = nc.vector.tensor_scalar(h2n[:, t, :], h2[:, t, :], smc[:, 12, t:t + 1], None, ALU.mult)
                ins.then_inc(V["h2n_ready"], 1)

            def b_final(b, h):
                if h == 0:
                    dve.wait_ge(V["xh_ready"], b + 1)
                dve.wait_ge(V["down_psum"], 2 * b + h + 1 + 2)
                x = Xrow[:, bass.ds(b * TB + 4 * h, 4), 0:P]
                ins = nc.vector.tensor_tensor(x, ps[7][:].rearrange("p (t c) -> p t c", c=P), xh[:, 4 * h:4 * h + 4, :], ALU.add)
                ins.then_inc(V["x3_half"], 1)

            def b_body(b, behind=True, ahead=True):
                b_decayed(b)
                if ahead:
                    b_stats(b + 1)
                b_scores(b)
                if ahead:
                    b_norm1(b + 1)
                b_h2(b, first=not behind)
                if behind:
                    b_final(b - 1, 0)
                if ahead:
                    b_lengths(b + 1)
                b_norm2(b)
                if behind:
                    b_final(b - 1, 1)

            dve.wait_ge(consts, 3)
            if "A" in phases:
                attn_a()
            if "F" in phases:
                dve.wait_ge(w_loaded2, W_SECOND)
                gate_loop(0)
                route(0)
                if "B" in phases:
                    b_tables()
                experts(0)
            if "B" in phases:
                if "F" not in phases:
                    b_tables()
                b_masks()
                for b in range(NB):
                    dve.wait_ge(x2_loaded[b], 16)
                b_stats(0)
                b_norm1(0, first=True)
                b_lengths(0)
                b_body(0, behind=False)
                start = own.base + own.n
                K = 2 + STATS + (5 + 2) + (3 + STATS + 2) + 2
                with dve.Fori(1, NB - 1) as b:
                    own.loop(b - 1, K, start)
                    b_body(b)
                own.leave(NB - 2, K, start)
                b_body(NB - 1, ahead=False)
                for h in range(2):
                    b_final(NB - 1, h)
                dve.wait_ge(V["x3_half"], 2 * NB + 1)
            if "G" in phases:
                gate_loop(1)
                route(1)
                experts(1)

        @block.scalar
        def _(act):
            own = Chain(act, act_own)

            def setup_act():
                act.wait_ge(w_loaded, W_FIRST)
                nc.scalar.activation(decay[:], col["time_decay"][:], ACT.Exp).then_inc(act_setup, 1)

            def setup_act2():
                act.wait_ge(w_loaded2, W_SECOND)
                for ap in (dl[:, 0], dl[:, 1], dcol[:, 0:1], cst[:, 4:5]):
                    nc.scalar.activation(ap, ap, ACT.Tanh, scale=0.5).then_inc(act_setup, 1)
                act.wait_ge(proj_turned, 1)
                nc.scalar.activation(projT[:], ps[2][:, 0:P], ACT.Copy, scale=col["norm1_w"][:]).then_inc(proj_ready, 1)

            def a_front(b):
                act.wait_ge(A["t0_psum"], b + 1 + 1)
                for h in range(2):
                    ins = nc.scalar.activation(xa[:, 1 + 512 * h:513 + 512 * h], ps[h][:], ACT.Identity, bias=col["ln0_b"][:], scale=col["ln0_g"][:])
                ins.then_inc(A["xa_ready"], 1)

            def a_v(b):
                for h in range(2):
                    act.wait_ge(A["v_psum"], 2 * b + h + 1)
                    ins = nc.scalar.copy(vs[:, 512 * h:512 * h + 512], ps[4 + h][:])
                ins.then_inc(A["v_copied"], 1)

            def a_r(b):
                for h in range(2):
                    act.wait_ge(A["r_psum"], 2 * b + h + 1)
                    ins = nc.scalar.activation(th[:, 512 * h:512 * h + 512], ps[h][:], ACT.Tanh, scale=0.5)
                ins.then_inc(A["r_tanh"], 1)

            def a_exps(b, h):
                c = slice(512 * h, 512 * h + 512)
                act.wait_ge(A["d12_ready"], 2 * b + h + 1)
                nc.scalar.activation(E1[:, c], E1[:, c], ACT.Exp)
                nc.scalar.activation(E2[:, c], E2[:, c], ACT.Exp).then_inc(A["e12_ready"], 1)
                act.wait_ge(A["s_ready"], 2 * b + h + 1)
                own(nc.scalar.activation(E4[:, c], E3[:, c], ACT.Relu, scale=-1.0))
                own(nc.scalar.activation(E3[:, c], E3[:, c], ACT.Relu))
                nc.scalar.activation(E4[:, c], E4[:, c], ACT.Exp, scale=-1.0)
                nc.scalar.activation(E3[:, c], E3[:, c], ACT.Exp, scale=-1.0).then_inc(A["e34_ready"], 1)

            def a_guess(b):
                act.wait_ge(A["den_ready"], 2 * b + 2)
                own(nc.scalar.activation(y0, den, ACT.Ln))
                nc.scalar.activation(y0, y0, ACT.Exp, scale=-1.0).then_inc(A["y0_ready"], 1)
            A_WKV = 5

            def a_norm1(b):
                act.wait_ge(A["t1_psum"], b + 1)
                for h in range(2):
                    ins = nc.scalar.activation(xc[:, 1 + 512 * h:513 + 512 * h], ps[h][:], ACT.Identity, bias=col["ln1_b"][:], scale=col["ln1_g"][:])
                ins.then_inc(A["xc_ready"], 1)
                for h in range(2):
                    ins = nc.scalar.activation(ca[:, 512 * h:512 * h + 512], ps[h][:], ACT.Identity, bias=cb[:], scale=cg[:])
                ins.then_inc(A["ca_ready"], 1)

            def a_hidden(b, half):
                act.wait_ge(A["cv_psum"], 2 * b + half + 1)
                for k in range(HC):
                    n = b * (2 * HC) + half * HC + k
                    act.wait_ge(A["ck_psum"], n + 1 + 2)
                    act.wait_ge(A["kk_ready"], n + 1)
                    nc.scalar.activation(kkr[k % 2], ps[4 + k % 2][:], ACT.Relu).then_inc(A["relu_ready"], 1)
                    act.wait_ge(A["relu_ready"], n + 1 + 2)
                    nc.scalar.activation(kk2[:, half, k, :], kkr[k % 2], ACT.Square).then_inc(A["kk_ready"], 1)

            def a_gate(b):
                for h in range(2):
                    act.wait_ge(A["cr_psum"], 2 * b + h + 1)
                    ins = nc.scalar.activation(th2[:, 512 * h:512 * h + 512], ps[6 + h][:], ACT.Tanh, scale=0.5)
                ins.then_inc(A["th2_ready"], 1)

            setup_act()
            if "A" in phases:
                act.wait_ge(tables, 1)

                def a_body(b, behind=True):
                    a_front(b)
                    a_exps(b, 0)
                    a_v(b)
                    a_exps(b, 1)
                    a_r(b)
                    if behind:
                        a_norm1(b - 1)
                    a_guess(b)
                    if behind:
                        a_gate(b - 1)
                        a_hidden(b - 1, 0)
                        a_hidden(b - 1, 1)

                a_body(0, behind=False)
                start = own.base + own.n
                with act.Fori(1, NB) as b:
                    own.loop(b - 1, A_WKV, start)
                    a_body(b)
                own.leave(NB - 1, A_WKV, start)
                a_norm1(NB - 1)
                a_gate(NB - 1)
                a_hidden(NB - 1, 0)
                a_hidden(NB - 1, 1)

            def ffn_act(f):
                s_ = S[f]
                with act.Fori(0, NB) as b:
                    act.wait_ge(s_["zt_psum"], b + 1 + 1)
                    act.wait_ge(s_["logits_done"], b + 1)
                    nc.scalar.copy(z8T[:, 0:512], ps[0][:]).then_inc(s_["zt_copied"], 1)
                    nc.scalar.copy(z8T[:, 512:1024], ps[1][:]).then_inc(s_["zt_copied"], 1)
                act.wait_ge(s_["pos_ready"], 2)
                if f == 0 and "B" in phases:
                    setup_act2()
                nc.scalar.activation(gelu_dummy[:], bg[0:1, 0:1], ACT.Gelu)

                with act.Fori(0, NS // U) as i:
                    for u in range(U):
                        g = i * U + u
                        e = act.value_load(texp[f][0:1, bass.ds(g, 1)], min_val=0, max_val=NE - 1)
                        act.wait_ge(s_["h_psum"], g + 1 + U)
                        act.wait_ge(s_["y_psum"], g + 1)
                        for k in range(HC):
                            b1 = W1[:, bass.ds(e, 1), HC * P + k:HC * P + k + 1].rearrange("p a c -> p (a c)")
                            ins = nc.scalar.activation(hT[u][:, k, :], ps[3 + u][:, k * P:(k + 1) * P], ACT.Gelu, bias=b1)
                        ins.then_inc(s_["h_ready"], 1)

            def b_qk(b):
                act.wait_ge(V["t1_psum"], b + 1)
                for h in range(2):
                    ins = nc.scalar.copy(hnT[:, 512 * h:512 * h + 512], ps[h][:])
                ins.then_inc(V["hnT_ready"], 1)
                act.wait_ge(V["qk_psum"], b + 1)
                nc.scalar.copy(qks.rearrange("p t s r -> p (t s r)"), ps[3][:, 0:TB * 2 * R]).then_inc(V["qk_copied"], 1)

            def b_turned(b):
                act.wait_ge(V["t2_psum"], b + 1)
                for h in range(2):
                    nc.scalar.copy(kT[:, 512 * h:512 * h + 512], ps[h][0:64, :])
                    ins = nc.scalar.copy(qT[:, 512 * h:512 * h + 512], ps[h][64:128, :])
                ins.then_inc(V["kqT_ready"], 1)

            def b_out(b):
                for h in range(2):
                    act.wait_ge(V["o_psum"], 2 * b + h + 1 + 1)
                    nc.scalar.copy(oT[:, 512 * h:512 * h + 512], ps[h][:]).then_inc(V["oT_ready"], 1)

            def b_h2T(b):
                act.wait_ge(V["t3_psum"], b + 1 + 1)
                for h in range(2):
                    ins = nc.scalar.copy(h2T[:, 512 * h:512 * h + 512], ps[h][:])
                ins.then_inc(V["h2T_ready"], 1)

            def b_mlp(b):
                for h in range(2):
                    act.wait_ge(V["down_psum"], 2 * b + h + 1)
                    for k in range(HC):
                        act.wait_ge(V["up_psum"], 2 * HC * b + HC * h + k + 1)
                        nc.scalar.activation(hmT[:, h, k, :], ps[5 + k % 2][:], ACT.Gelu_apprx_tanh, bias=mb1[:, k:k + 1]).then_inc(V["hm_ready"], 1)

            if phases == "B":
                setup_act2()
            if "F" in phases:
                ffn_act(0)
            if "B" in phases:
                def b_body(b, behind=True, ahead=True):
                    act.wait_ge(V["hn_ready"], b + 1)
                    act.wait_ge(V["t3_psum"], b + 1)
                    nc.scalar.copy(hn.rearrange("p t c -> p (t c)"), hna.rearrange("p t c -> p (t c)")).then_inc(V["hn_held"], 1)
                    b_turned(b)
                    if behind:
                        b_mlp(b - 1)
                    b_out(b)
                    if ahead:
                        b_qk(b + 1)
                    b_h2T(b)

                b_qk(0)
                b_body(0, behind=False)
                nc.scalar.activation(gelu_dummy[:], mb1[0:1, 0:1], ACT.Gelu_apprx_tanh)
                with act.Fori(1, NB - 1) as b:
                    b_body(b)
                b_body(NB - 1, ahead=False)
                b_mlp(NB - 1)
            if "G" in phases:
                ffn_act(1)

        @block.tensor
        def _(pe):
            def tiles_turned(src, n=TB):
                for t in range(n):
                    ins = nc.tensor.transpose(ps[t // 4][:, (t % 4) * P:(t % 4 + 1) * P], src[:, t, :], ident[:])
                return ins

            def a_wo(b):
                pe.wait_ge(A["rw_ready"], b + 1)
                pe.wait_ge(A["th2_ready"], b + 1)
                for h in range(2):
                    for t in range(4):
                        at = (4 * h + t) * P
                        ins = nc.tensor.matmul(ps[6 + h][:, t * P:(t + 1) * P], rw[:, at:at + P], Wo[:], start=True, stop=True)
                    ins.then_inc(A["wo_psum"], 1)

            def a_turn0(b):
                pe.wait_ge(A["a8_ready"], b + 1)
                tiles_turned(a8).then_inc(A["t0_psum"], 1)

            def a_kvr(b, first=False):
                pe.wait_ge(A["xa_ready"], b + 1)
                if not first:
                    pe.wait_ge(A["x1_done"], b)
                for n, bank, done in (("k", 2, A["k_psum"]), ("v", 4, A["v_psum"]), ("r", 0, A["r_psum"])):
                    if n == "v" and not first:
                        pe.wait_ge(A["relu_ready"], 2 * HC * (b - 1) + 2)
                    for h in range(2):
                        nc.tensor.matmul(ps[bank + h][:], W_now[n][:], xa[:, 1 + 512 * h:513 + 512 * h], start=True, stop=False)
                        nc.tensor.matmul(ps[bank + h][:], W_shift[n][:], xa[:, 512 * h:512 + 512 * h], start=False, stop=True).then_inc(done, 1)

            def a_back(b, started):
                pe.wait_ge(A["r_tanh"], started)
                pe.wait_ge(A["x1n_ready"], b + 1)
                tiles_turned(x1n).then_inc(A["t1_psum"], 1)
                pe.wait_ge(A["xc_ready"], b + 1)
                for h in range(2):
                    for t in range(4):
                        at = (4 * h + t) * P
                        nc.tensor.matmul(ps[6 + h][:, t * P:(t + 1) * P], xc[:, 1 + at:1 + at + P], W_now["cr"][:], start=True, stop=False)
                        ins = nc.tensor.matmul(ps[6 + h][:, t * P:(t + 1) * P], xc[:, at:at + P], W_shift["cr"][:], start=False, stop=True)
                    ins.then_inc(A["cr_psum"], 1)
                pe.wait_ge(A["v_copied"], started)
                pe.wait_ge(A["mk_ready"], b + 1)
                for h in range(2):
                    for k in range(HC):
                        n = 2 * HC * b + HC * h + k
                        pe.wait_ge(A["relu_ready"], n + 1)
                        nc.tensor.matmul(ps[4 + k % 2][:], Wck[:, k * P:(k + 1) * P], mk[:, 512 * h:512 * h + 512], start=True, stop=True).then_inc(A["ck_psum"], 1)
                pe.wait_ge(A["s_ready"], 2 * started)
                for h in range(2):
                    pe.wait_ge(A["kk_ready"], 2 * HC * b + HC * h + HC + 2)
                    for t in range(4):
                        for k in range(HC):
                            ins = nc.tensor.matmul(ps[2 + h][:, t * P:(t + 1) * P], kk2[:, h, k, t * P:(t + 1) * P], Wcv[:, k, :], start=(k == 0), stop=(k == HC - 1))
                    ins.then_inc(A["cv_psum"], 1)

            def turn_projection():
                pe.wait_ge(w_loaded2, W_SECOND)
                nc.tensor.transpose(ps[2][:, 0:P], proj_in, ident[:]).then_inc(proj_turned, 1)
                pe.wait_ge(proj_ready, 1)

            def ffn_pe(f):
                s_ = S[f]
                with pe.Fori(0, NB) as b:
                    pe.wait_ge(s_["z_ready"], b + 1)
                    pe.wait_ge(s_["zt_copied"], 2 * b + 2)
                    tiles_turned(z8).then_inc(s_["zt_psum"], 1)
                    pe.wait_ge(s_["zt_copied"], 2 * b + 2 + 2)
                    for t in range(TB):
                        ins = nc.tensor.matmul(ps[2][:, bass.ds(b * (TB * NE) + t * NE, NE)], z8T[:, t * P:(t + 1) * P], Wg[:], start=True, stop=True)
                    ins.then_inc(s_["logits_done"], 1)
                pe.wait_ge(s_["onehot_ready"], 1)
                nc.tensor.matmul(ps[3][:, 0:NE * NT], before[:], oh.rearrange("p e t -> p (e t)"), start=True, stop=True)
                nc.tensor.matmul(ps[4][:, 0:NE * NT], ones[:], oh.rearrange("p e t -> p (e t)"), start=True, stop=True).then_inc(s_["ranks_done"], 1)
                pe.wait_ge(s_["pos_ready"], 2)
                if f == 0 and "B" in phases:
                    turn_projection()

                def turn_z(u, g):
                    pe.wait_ge(s_["zs_ready"], g + 1)
                    nc.tensor.transpose(ps[u][:, 0:P], zs[u], ident[:]).then_inc(s_["zsT_psum"], 1)

                def up(u, g, i):
                    pe.wait_ge(s_["zsT_ready"], g + 1)
                    pe.wait_ge(w_loads[f][u], 16 * i + 16)
                    pe.wait_ge(s_["h_ready"], g + 1)
                    for k in range(HC):
                        ins = nc.tensor.matmul(ps[3 + u][:, k * P:(k + 1) * P], w1cur[u][:, k * P:(k + 1) * P], zsT[u], start=True, stop=True)
                    ins.then_inc(s_["h_psum"], 1)

                def down(u, g):
                    e = pe.value_load(texp[f][0:1, bass.ds(g, 1)], min_val=0, max_val=NE - 1)
                    pe.wait_ge(s_["h_ready"], g + 1 + U)
                    pe.wait_ge(s_["y_ready"], g + (2 if u == 0 else 1))
                    nc.tensor.matmul(ps[Y_BANK[u]][:, 0:P], ones[0:1, :], B2[:, bass.ds(e, 1), :].rearrange("p a c -> p (a c)"), start=True, stop=False)
                    for k in range(HC):
                        ins = nc.tensor.matmul(ps[Y_BANK[u]][:, 0:P], hT[u][:, k, :],
                                               W2[:, bass.ds(e, 1), k, :].rearrange("p a c -> p (a c)"), start=False, stop=(k == HC - 1))
                    ins.then_inc(s_["y_psum"], 1)

                def turn(i, first):
                    for u in range(U):
                        g = i * U + u
                        turn_z(u, g)
                        if not (first and u < 1):
                            up((u - 1) % U, g - 1, i - (u == 0))
                        if not (first and u < 2):
                            down((u - 2) % U, g - 2)

                turn(0, True)
                with pe.Fori(1, NS // U) as i:
                    turn(i, False)
                up(U - 1, NS - 1, NS // U - 1)
                down(U - 2, NS - 2)
                down(U - 1, NS - 1)

            def b_turn1(b):
                pe.wait_ge(V["hn_ready"], b + 1)
                tiles_turned(hna).then_inc(V["t1_psum"], 1)

            def b_qk(b):
                pe.wait_ge(V["hnT_ready"], b + 1)
                for t in range(TB):
                    ins = nc.tensor.matmul(ps[3][:, t * 2 * R:(t + 1) * 2 * R], hnT[:, t * P:(t + 1) * P], uv[:], start=True, stop=True)
                ins.then_inc(V["qk_psum"], 1)

            def b_keys(b, first):
                pe.wait_ge(V["kq_ready"], b + 1)
                if not first:
                    pe.wait_ge(V["h2T_ready"], b)
                tiles_turned(KQ).then_inc(V["t2_psum"], 1)
                pe.wait_ge(V["hn_held"], b + 1)
                for t in range(TB - 1):
                    ins = nc.tensor.matmul(ps[3 + t // 4][0:64, (t % 4) * P:(t % 4 + 1) * P], kd[:, t, :], hn[:, t, :], start=True, stop=True)
                    if t % 4 == 3 or t == TB - 2:
                        ins.then_inc(V["u_psum"], 1)

            def b_scores(b):
                pe.wait_ge(V["kqT_ready"], b + 1)
                for h in range(2):
                    if h == 1:
                        pe.wait_ge(V["state_ready"], 2 * b + 1)
                    for t in range(4):
                        at = slice((4 * h + t) * P, (4 * h + t + 1) * P)
                        ins = nc.tensor.matmul(ps[2 + h][:, t * P:(t + 1) * P], kT[:, at], qT[:, at], start=True, stop=True)
                    ins.then_inc(V["at_psum"], 1)

            def b_out(b):
                pe.wait_ge(V["state_ready"], 2 * b + 2)
                for h in range(2):
                    pe.wait_ge(V["at_ready"], 2 * b + h + 1)
                    for t in range(4):
                        c = 4 * h + t
                        o = ps[h][:, t * P:(t + 1) * P]
                        ins = nc.tensor.matmul(o, hn[:, c, :], AT[:, c, :], start=True, stop=(c == 0))
                        if c:
                            nc.tensor.matmul(ps[h][:, t * P:t * P + 4], hn[:, c - 1, :], conv_prev[:], start=False, stop=False)
                            ins = nc.tensor.matmul(o, state[:, c, :], qT[:, c * P:(c + 1) * P], start=False, stop=True)
                    ins.then_inc(V["o_psum"], 1)

            def b_proj(b):
                for h in range(2):
                    pe.wait_ge(V["oT_ready"], 2 * b + h + 1)
                    for t in range(4):
                        at = (4 * h + t) * P
                        ins = nc.tensor.matmul(ps[4 if h == 0 else 2][:, t * P:(t + 1) * P], oT[:, at:at + P], projT[:], start=True, stop=True)
                    ins.then_inc(V["proj_psum"], 1)

            def b_turn3(b):
                pe.wait_ge(V["h2n_ready"], b + 1)
                tiles_turned(h2n).then_inc(V["t3_psum"], 1)

            def b_up(b, h):
                pe.wait_ge(V["h2T_ready"], b + 1)
                for k in range(HC):
                    pe.wait_ge(V["hm_ready"], 2 * HC * b + HC * h + k + 1)
                    nc.tensor.matmul(ps[5 + k % 2][:], M1[:, k * P:(k + 1) * P], h2T[:, 512 * h:512 * h + 512], start=True, stop=True).then_inc(V["up_psum"], 1)

            def b_down(b, h):
                pe.wait_ge(V["hm_ready"], 2 * HC * b + HC * h + HC + 2)
                pe.wait_ge(V["x3_half"], 2 * b + h + 1)
                for t in range(4):
                    for k in range(HC):
                        ins = nc.tensor.matmul(ps[7][:, t * P:(t + 1) * P], hmT[:, h, k, t * P:(t + 1) * P], M2[:, k, :], start=(k == 0), stop=(k == HC - 1))
                ins.then_inc(V["down_psum"], 1)

            def b_body(b, behind=True, ahead=True):
                b_keys(b, first=not behind)
                if behind:
                    b_up(b - 1, 0)
                b_scores(b)
                if behind:
                    b_up(b - 1, 1)
                b_out(b)
                b_proj(b)
                if ahead:
                    b_turn1(b + 1)
                if behind:
                    b_down(b - 1, 0)
                if ahead:
                    b_qk(b + 1)
                if behind:
                    b_down(b - 1, 1)
                b_turn3(b)

            pe.wait_ge(consts, 3)
            if "A" in phases:
                pe.wait_ge(tables, 1)
                a_turn0(0)
                a_kvr(0, first=True)
                with pe.Fori(1, NB) as b:
                    pe.wait_ge(A["r_tanh"], b)
                    a_turn0(b)
                    a_wo(b - 1)
                    a_kvr(b)
                    a_back(b - 1, b + 1)
                a_wo(NB - 1)
                a_back(NB - 1, NB)
            if phases == "B":
                turn_projection()
            if "F" in phases:
                pe.wait_ge(w_loaded2, W_SECOND)
                ffn_pe(0)
            if "B" in phases:
                b_turn1(0)
                b_qk(0)
                b_body(0, behind=False)
                with pe.Fori(1, NB - 1) as b:
                    b_body(b)
                b_body(NB - 1, ahead=False)
                for h in range(2):
                    b_up(NB - 1, h)
                for h in range(2):
                    b_down(NB - 1, h)
            if "G" in phases:
                ffn_pe(1)


_INS = [
    'L0_attn_a_x', 'L0_attn_a_ln0_g', 'L0_attn_a_ln0_b', 'L0_attn_a_ln1_g', 'L0_attn_a_ln1_b', 'L0_attn_a_time_decay',
    'L0_attn_a_time_first', 'L0_attn_a_tm_k', 'L0_attn_a_tm_v', 'L0_attn_a_tm_r', 'L0_attn_a_Wk', 'L0_attn_a_Wv',
    'L0_attn_a_Wr', 'L0_attn_a_Wo', 'L0_attn_a_cm_k', 'L0_attn_a_cm_r', 'L0_attn_a_Wck', 'L0_attn_a_Wcv',
    'L0_attn_a_Wcr', 'L0_attn_b_u', 'L0_attn_b_v', 'L0_attn_b_decay_logit', 'L0_attn_b_alpha_logit',
    'L0_attn_b_k_base_gate_logit', 'L0_attn_b_k_base_kernel', 'L0_attn_b_proj_w', 'L0_attn_b_proj_b',
    'L0_attn_b_norm1_w', 'L0_attn_b_norm2_w', 'L0_attn_b_mlp_w1', 'L0_attn_b_mlp_b1', 'L0_attn_b_mlp_w2',
    'L0_attn_b_mlp_b2', 'L0_ffn_Wg', 'L0_ffn_bg', 'L0_ffn_W1', 'L0_ffn_b1', 'L0_ffn_W2', 'L0_ffn_b2',
]
PHASES = "AFBG"


def kernel(**inputs):
    import numpy as _np
    import concourse.bacc as _bacc
    from concourse import mybir as _mybir
    from concourse.bass_utils import run_bass_kernel_spmd as _run

    nc = _bacc.Bacc("TRN2", target_bir_lowering=False, num_devices=1)
    arrays, aps = {}, {}
    for name in _INS:
        arr = _np.ascontiguousarray(inputs[name])
        shape = arr.shape if arr.ndim and inputs[name].ndim else (1,)
        arrays[f"in_{name}_dram"] = arr.reshape(shape)
        aps[name[3:]] = nc.dram_tensor(f"in_{name}_dram", shape, _mybir.dt.from_np(arr.dtype), kind="ExternalInput").ap()
    out = nc.dram_tensor("out_0_dram", (NT * P, P), F32, kind="ExternalOutput").ap()
    build(nc, aps, out, PHASES)
    r = _run(nc, [arrays], core_ids=[0])
    return r.results[0]["out_0_dram"].reshape(NB, TB * P, P)
```

```python
from contextlib import ExitStack

import concourse.bass as bass
from concourse import mybir

ALU = mybir.AluOpType
ACT = mybir.ActivationFunctionType
AX_X = mybir.AxisListType.X
F32 = mybir.dt.float32
I32 = mybir.dt.int32
U32 = mybir.dt.uint32

P = 128
ROW = P + 4
MEAN, RSTD, ID = P, P + 1, P + 2
NB = 4
TB = 8
NT = NB * TB
NE = 8
HC = 4
EPS = 1e-5
NS = (NT * P + NE * (P - 1)) // P
U = 3
assert NS % U == 0
REGION = NT * P + P
SPARE = NE * REGION


class Chain:

    def __init__(self, engine, sem):
        self.engine, self.sem, self.base, self.n = engine, sem, 0, 0

    def __call__(self, ins):
        self.n += 1
        ins.then_inc(self.sem, 1)
        self.engine.wait_ge(self.sem, self.base + self.n)

    def loop(self, i, per_turn, start):
        self.base, self.n = start + i * per_turn, 0

    def leave(self, turns, per_turn, start):
        assert self.n == per_turn, (self.n, per_turn)
        self.base, self.n = start + turns * per_turn, 0


def build(nc, D, out):
    with ExitStack() as ctx:
        def sb(name, shape, dt=F32):
            return ctx.enter_context(nc.sbuf_tensor(name, shape, dt))

        credits = []

        def sem(name, credit=0):
            handle = ctx.enter_context(nc.semaphore(name))
            if credit:
                credits.append((handle, credit))
            return handle

        sorted_rows = [nc.dram_tensor(f"sorted_rows{f}", [SPARE + P, ROW], F32, kind="Internal").ap() for f in range(2)]
        x2_rows = nc.dram_tensor("x2_rows", [NT * P, P], F32, kind="Internal").ap()

        W1 = sb("W1", [P, NE, HC * P + HC])
        W2 = sb("W2", [P, NE, HC, P])
        B2 = sb("B2", [1, NE, P])
        Wg = sb("Wg", [P, NE])
        bg = sb("bg", [P, NE])
        ident = sb("ident", [P, P])
        ones = sb("ones", [P, P])
        before = sb("before", [P, P])
        expert_m8 = sb("expert_m8", [P, NE])
        slot_no = sb("slot_no", [P, NS])
        region = sb("region", [P, NE])
        not_first = sb("not_first", [P, NE, TB])
        minus_half = sb("minus_half", [P, 2 * TB])
        fill = sb("fill", [P, ROW])
        col = {n: sb("c_" + n, [P, 1]) for n in (
            "ln0_g", "ln0_b", "ln1_g", "ln1_b", "time_decay", "time_first", "tm_k", "tm_v", "tm_r", "cm_k", "cm_r",
            "norm1_w", "norm2_w")}
        rest = {n: sb("r_" + n, [P, 1]) for n in ("tm_k", "tm_v", "tm_r", "cm_k", "cm_r")}
        gelu_dummy = sb("gelu_dummy", [1, 1])
        decay = sb("decay", [P, 1])
        cg = sb("cg", [P, 1])
        cb = sb("cb", [P, 1])
        W_now = {n: sb("now_" + n, [P, P]) for n in ("k", "v", "r", "cr")}
        W_shift = {n: sb("shift_" + n, [P, P]) for n in ("k", "v", "r", "cr")}
        Wo = sb("Wo", [P, P])
        Wck = sb("Wck", [P, HC * P])
        Wcv = sb("Wcv", [P, HC, P])
        R = 16
        BLK = 32
        NBLK = P // BLK
        uv = sb("uv", [P, 2 * R])
        projT = sb("projT", [P, P])
        pb = sb("pb", [P, P])
        M1 = sb("M1", [P, HC * P])
        M2 = sb("M2", [P, HC, P])
        mb1 = sb("mb1", [P, HC])
        mb2 = sb("mb2", [P, P])
        g128 = sb("g128", [64, 1])
        G = sb("G", [P, 3, NBLK, R])
        causal = sb("causal", [P, P])
        conv = sb("conv", [P, P])
        conv_prev = sb("conv_prev", [P, 4])

        Xrow = sb("Xrow", [P, NT, ROW])
        posi = [sb(f"posi{f}", [P, NT], U32) for f in range(2)]
        texp = [sb(f"texp{f}", [P, NS], I32) for f in range(2)]
        trow = [sb(f"trow{f}", [P, NS], I32) for f in range(2)]
        tokens = [sb(f"tokens{f}", [P, NE], I32) for f in range(2)]

        ARENA = 32540
        arena = sb("arena", [P, ARENA])

        class Scratch:
            def __init__(self, name):
                self.name, self.at = name, 0

            def __call__(self, *dims, parts=P):
                n = 1
                for d in dims:
                    n *= d
                ap = arena[0:parts, self.at:self.at + n]
                self.at += n
                assert self.at <= ARENA, (self.name, self.at)
                if len(dims) > 1:
                    names = ["a", "b", "c", "d"][:len(dims)]
                    ap = ap.rearrange(f"p ({' '.join(names)}) -> p {' '.join(names)}", **dict(zip(names, dims)))
                return ap

        fs = Scratch("ffn")
        z8 = fs(TB, P)
        z8T = fs(TB * P)
        bst = fs(TB, 6)
        sm = fs(12, TB)
        lg = fs(TB, NE)
        eq = fs(TB, NE)
        top = fs(TB)
        oh = fs(NE, TB)
        run = fs(NE, TB)
        pos3 = fs(NE, TB)
        base = fs(NE)
        nti = fs(NE).bitcast(I32)
        ntf = fs(NE)
        endt = fs(NE)
        posf = fs(TB)
        cmp_ = fs(NS, NE)
        texf = fs(NS)
        gate_end = fs.at
        x_rows = fs(NS, ROW)
        y_rows = fs(NS, P)
        zs = [fs(P) for u in range(U)]
        zsT = [fs(P) for u in range(U)]
        w1cur = [fs(HC * P) for u in range(U)]
        hT = [fs(HC, P) for u in range(U)]

        bs = Scratch("attn_b")
        bs.at = gate_end
        setup = sb("setup", [P, 1500])
        setup_at = [0]

        def su(*dims, parts=P):
            n = 1
            for d in dims:
                n *= d
            ap = setup[0:parts, setup_at[0]:setup_at[0] + n]
            setup_at[0] += n
            if len(dims) > 1:
                names = ["a", "b", "c"][:len(dims)]
                ap = ap.rearrange(f"p ({' '.join(names)}) -> p {' '.join(names)}", **dict(zip(names, dims)))
            return ap

        proj_in = su(P)
        dl = su(3, R)
        dcol = su(2, parts=64)
        cst = su(8)
        hundred28 = su(1, parts=64)
        expo = su(3, NBLK, R)
        gmask = su(3, NBLK, R)
        dist = su(P)
        ctmp = su(P)
        gam = su(3, NBLK, R)
        hna = bs(TB, P)
        hn = bs(TB, P)
        hnT = bs(TB * P)
        qks = bs(TB, 2, R)
        sq = bs(TB, 2, R)
        n2 = bs(TB, 2)
        rn = bs(TB, 2)
        KQ = bs(TB, 2 * NBLK * R)
        kd = bs(TB, NBLK * R)
        kT = bs(TB * P, parts=64)
        qT = bs(TB * P, parts=64)
        AT = bs(TB, P)
        state = bs(TB, P, parts=64)
        oT = bs(TB * P)
        h2 = bs(TB, P)
        h2n = bs(TB, P)
        xh = bs(TB, P)
        h2T = bs(TB * P)
        hmT = bs(2, HC, 4 * P)
        bstb = bs(TB, 6)
        smb = bs(14, TB)
        smc = bs(14, TB)

        as_ = Scratch("attn_a")
        L = TB * P
        wraw = as_(4, P)
        a8 = as_(TB, P)
        Y = as_(NT, P)
        assert gate_end <= as_.at - TB * P
        xa = as_(1 + L)
        p_ = as_(1 + L)
        aa = as_(1 + L)
        bb = as_(1 + L)
        E1 = as_(L)
        E2 = as_(L)
        E3 = as_(L)
        E4 = as_(L)
        vs = as_(L)
        av = as_(L)
        num = as_(L)
        den = as_(L)
        y0 = as_(L)
        th = as_(L)
        rw = as_(L)
        x1 = as_(TB, P)
        x1n = as_(TB, P)
        xc = as_(1 + L)
        ca = as_(L)
        mk = as_(L)
        kkr = [as_(512) for _ in range(2)]
        kk2 = as_(2, HC, 512)
        th2 = as_(L)
        bsta = as_(TB, 6)
        sma = as_(14, TB)
        smx = as_(14, TB)

        ps = [ctx.enter_context(nc.psum_tensor(f"ps{i}", [P, 512], F32)) for i in range(8)]

        w_loaded = sem("w_loaded")
        w_loaded2 = sem("w_loaded2")
        x_loaded = [sem(f"x_loaded{b}") for b in range(NB)]
        consts = sem("consts")
        pool_own = sem("pool_own")
        tables = sem("tables")
        filled = sem("filled")
        padded = [sem(f"padded{f}") for f in range(2)]
        credit = sem("credit")
        dve_own = sem("dve_own")
        act_own = sem("act_own")
        act_setup = sem("act_setup")
        gpow = sem("gpow")
        gexp = sem("gexp")
        proj_turned = sem("proj_turned")
        proj_ready = sem("proj_ready")
        CR = {"h_psum": U, "zsT_psum": U, "h_ready": U, "y_psum": U, "y_ready": 2}
        S = [{n: sem(f"{n}{f}", CR.get(n, 0)) for n in (
            "ve_ready", "rstd_ready", "z_ready", "zt_psum", "zt_copied", "logits_done",
            "onehot_ready", "ranks_done", "pos_ready", "counts_ready", "tiles_ready", "rows_scattered", "zs_ready", "zsT_psum",
            "zsT_ready", "h_psum", "h_ready", "y_psum", "y_ready",
            "y_scattered")} for f in range(2)]
        V = {n: sem(n + "_b", c) for n, c in (
            ("var_ready", 0), ("scale_ready", 0), ("back_ready", 0), ("hn_ready", 0), ("hn_held", 0), ("t1_psum", 0), ("hnT_ready", 0),
            ("qk_psum", 0), ("qk_copied", 0), ("n2_ready", 0), ("rn_ready", 0), ("kq_ready", 0),
            ("t2_psum", 0), ("kqT_ready", 0), ("u_psum", 0), ("state_ready", 0), ("at_psum", 0), ("at_ready", 0),
            ("o_psum", 1), ("oT_ready", 0), ("proj_psum", 0), ("ms_ready", 0), ("s2_ready", 0),
            ("h2n_ready", 0), ("t3_psum", 1), ("h2T_ready", 0), ("xh_ready", 0),
            ("up_psum", 0), ("hm_ready", 2), ("down_psum", 2), ("x3_half", 1))}
        x2_loaded = [sem(f"x2_loaded{b}") for b in range(NB)]
        A = {n: sem(n + "_a", c) for n, c in (
            ("var0_ready", 0), ("scale0_ready", 0), ("rstd0_ready", 0), ("a8_ready", 0), ("t0_psum", 1), ("xa_ready", 0),
            ("k_psum", 0), ("v_psum", 0), ("r_psum", 0), ("v_copied", 0), ("r_tanh", 0),
            ("d12_ready", 0), ("s_ready", 0), ("e12_ready", 0), ("e34_ready", 0), ("av_ready", 0),
            ("scan_ready", 0), ("den_ready", 0), ("y0_ready", 0), ("qt_ready", 0), ("rw_ready", 0),
            ("wo_psum", 1), ("var1_ready", 0), ("scale1_ready", 0), ("x1n_ready", 0),
            ("t1_psum", 0), ("xc_ready", 0), ("ca_ready", 0), ("mk_ready", 0), ("cr_psum", 0), ("ck_psum", 2), ("relu_ready", 2),
            ("kk_ready", 2), ("cv_psum", 2), ("th2_ready", 1), ("xx_ready", 0), ("x1_done", 1))}
        w_loads = [[sem(f"tile_weights{f}_{u}") for u in range(U)] for f in range(2)]
        loads = [sem(f"rows_loaded{f}") for f in range(2)]

        block = ctx.enter_context(nc.Block())

        vec = "(p a) -> p a"
        first_loads = [(col[n][:], D["attn_a_" + n].rearrange(vec, a=1)) for n in (
            "ln0_g", "ln0_b", "ln1_g", "ln1_b", "time_decay", "time_first", "tm_k", "tm_v", "tm_r", "cm_k", "cm_r")]
        first_loads += [(wraw[:, j, :], D["attn_a_" + n]) for j, n in enumerate(("Wk", "Wv", "Wr", "Wcr"))]
        first_loads += [
            (Wo[:], D["attn_a_Wo"]),
            (Wck[:], D["attn_a_Wck"]),
            (Wcv[:], D["attn_a_Wcv"].rearrange("(k p) c -> p k c", p=P)),
        ]
        second_loads = [(col[n][:], D["attn_b_" + n].rearrange(vec, a=1)) for n in ("norm1_w", "norm2_w")]
        second_loads += [
            (uv[:, 0:R], D["attn_b_u"]),
            (uv[:, R:2 * R], D["attn_b_v"]),
            (proj_in, D["attn_b_proj_w"]),
            (pb[:], D["attn_b_proj_b"].partition_broadcast(P)),
            (M1[:], D["attn_b_mlp_w1"]),
            (M2[:], D["attn_b_mlp_w2"].rearrange("(k p) c -> p k c", p=P)),
            (mb1[:], D["attn_b_mlp_b1"].rearrange("(k p) -> p k", p=P)),
            (mb2[:], D["attn_b_mlp_b2"].partition_broadcast(P)),
            (dl[:, 0, :], D["attn_b_decay_logit"].partition_broadcast(P)),
            (dl[:, 1, :], D["attn_b_alpha_logit"].partition_broadcast(P)),
            (cst[:, 0:4], D["attn_b_k_base_kernel"].partition_broadcast(P)),
            (cst[:, 4:5], D["attn_b_k_base_gate_logit"].partition_broadcast(P)),
        ]
        second_loads += [(dcol[R * g:R * g + R, 0:1], D["attn_b_decay_logit"].rearrange(vec, a=1)) for g in range(NBLK)]
        second_loads += [
            (Wg[:], D["ffn_Wg"]),
            (bg[:], D["ffn_bg"].partition_broadcast(P)),
            *((W1[:, e, HC * P:], D["ffn_b1"][e].rearrange("(k p) -> p k", p=P)) for e in range(NE)),
            (B2[:], D["ffn_b2"].unsqueeze(0)),
            (W1[:, :, 0:HC * P], D["ffn_W1"].rearrange("e c h -> c e h")),
            (W2[:], D["ffn_W2"].rearrange("e (k p) d -> p e k d", p=P)),
        ]
        W_FIRST, W_SECOND = 16 * len(first_loads), 16 * len(second_loads)

        Y_BANK = [6, 7, 6]

        def gate_bank(f, b):
            return ps[3 if f else 6 if b else 1]


        @block.sync
        def _(sp):
            for handle, count in credits:
                sp.sem_inc(handle, count)
            x_view = D["attn_a_x"].rearrange("b (t p) c -> b p t c", p=P)
            with nc.allow_non_contiguous_dma(reason="vectors onto partitions"):
                sp.dma_start(Xrow[:, 0:TB, 0:P], x_view[0]).then_inc(x_loaded[0], 16)
                for dst, src in first_loads:
                    sp.dma_start(dst, src).then_inc(w_loaded, 16)
                for b in range(1, NB):
                    sp.dma_start(Xrow[:, b * TB:(b + 1) * TB, 0:P], x_view[b]).then_inc(x_loaded[b], 16)
                for dst, src in second_loads:
                    sp.dma_start(dst, src).then_inc(w_loaded2, 16)
            sp.wait_ge(consts, 1)
            for f in range(2):
                sp.dma_start(sorted_rows[f][SPARE:SPARE + P, :], fill[:]).then_inc(filled, 16)

            def slot_loads(f):
                def values(ap, top):
                    return nc.values_load_multi_w_load_instructions(ap, engines=[mybir.EngineType.SP], min_val=0, max_val=top)[1]

                def rows_of(i):
                    return values(trow[f][0:1, bass.ds(i * U, U)], SPARE)

                def rows(i, firsts):
                    for u, row in enumerate(firsts):
                        sp.dma_start(x_rows[:, bass.ds(i * U + u, 1), :],
                                     sorted_rows[f][bass.ds(row, P), :].unsqueeze(1)).then_inc(loads[f], 16)

                def weights(i):
                    for u, e in enumerate(values(texp[f][0:1, bass.ds(i * U, U)], NE - 1)):
                        sp.wait_ge(S[f]["h_psum"], i * U + u + 1)
                        sp.dma_start(w1cur[u], W1[:, bass.ds(e, 1), 0:HC * P].rearrange("p a c -> p (a c)")).then_inc(w_loads[f][u], 16)

                sp.wait_ge(S[f]["tiles_ready"], 1)
                weights(0)
                sp.wait_ge(padded[f], 16 * NE)
                sp.wait_ge(filled, 32)
                sp.wait_ge(S[f]["rows_scattered"], 16 * NT)
                rows(0, rows_of(0))
                sp.wait_ge(loads[f], 16 * U)
                rows(1, rows_of(1))
                with sp.Fori(1, NS // U - 1) as i:
                    firsts = rows_of(i + 1)
                    sp.wait_ge(loads[f], 16 * U * i + 16 * U)
                    rows(i + 1, firsts)
                    weights(i)
                weights(NS // U - 1)

            slot_loads(0)
            sp.wait_ge(S[0]["y_scattered"], 16 * NS)
            for b in range(NB):
                sp.wait_ge(x_loaded[b], 16)
                sp.dma_start(Xrow[:, b * TB:(b + 1) * TB, 0:P],
                             x2_rows.rearrange("(b t p) c -> b p t c", p=P, t=TB)[b]).then_inc(x2_loaded[b], 16)
            slot_loads(1)
            sp.wait_ge(S[1]["y_scattered"], 16 * NS)

        @block.gpsimd
        def _(pool):
            own = Chain(pool, pool_own)
            nc.gpsimd.memset(ident[:], 0.0)
            nc.gpsimd.memset(ones[:], 1.0)
            nc.gpsimd.memset(minus_half[:], -0.5)
            nc.gpsimd.memset(not_first[:], 1.0)
            nc.gpsimd.memset(hundred28[:], float(P))
            own(nc.gpsimd.memset(fill[:], 0.0))
            nc.gpsimd.memset(fill[:, ID:ID + 1].bitcast(I32), NT * P).then_inc(consts, 1)
            nc.gpsimd.affine_select(out=ident[:], in_=ident[:], compare_op=ALU.not_equal, fill=1.0, base=0,
                                    pattern=[[-1, P]], channel_multiplier=1).then_inc(consts, 1)
            for line in (xa, p_, aa, bb, xc):
                nc.gpsimd.memset(line[:, 0:1], -1e38 if line is p_ else 0.0)
            nc.gpsimd.affine_select(out=before[:], in_=ones[:], compare_op=ALU.is_gt, fill=0.0, base=0,
                                    pattern=[[1, P]], channel_multiplier=-1)
            nc.gpsimd.affine_select(out=causal[:], in_=ones[:], compare_op=ALU.is_ge, fill=0.0, base=0,
                                    pattern=[[1, P]], channel_multiplier=-1)
            nc.gpsimd.iota(expert_m8[:], [[1, NE]], base=-NE, channel_multiplier=0, allow_small_or_imprecise_dtypes=True)
            nc.gpsimd.iota(region[:], [[REGION, NE]], base=0, channel_multiplier=0, allow_small_or_imprecise_dtypes=True)
            nc.gpsimd.iota(slot_no[:], [[1, NS]], base=0, channel_multiplier=0, allow_small_or_imprecise_dtypes=True)
            nc.gpsimd.iota(dist, [[1, P]], base=0, channel_multiplier=-1, allow_small_or_imprecise_dtypes=True)
            nc.gpsimd.iota(expo[:, 0], [[BLK, NBLK], [0, R]], base=0, channel_multiplier=-1, allow_small_or_imprecise_dtypes=True)
            nc.gpsimd.iota(expo[:, 1], [[-BLK, NBLK], [0, R]], base=0, channel_multiplier=1, allow_small_or_imprecise_dtypes=True)
            nc.gpsimd.iota(expo[:, 2], [[BLK, NBLK], [0, R]], base=P, channel_multiplier=-1, allow_small_or_imprecise_dtypes=True)
            nc.gpsimd.iota(Xrow[:, :, ID:ID + 1].rearrange("p t w -> p (t w)").bitcast(I32), [[P, NT]], base=0, channel_multiplier=1)
            nc.gpsimd.memset(Xrow[:, :, ID + 1:ROW], 0.0)
            nc.gpsimd.memset(not_first[:, :, 0:1], 0.0).then_inc(consts, 1)

            def power(out, base):
                return nc.gpsimd.tensor_tensor(out, base, minus_half[:, 0:TB], ALU.pow)

            def gate_scale(f, b):
                pool.wait_ge(S[f]["ve_ready"], b + 1)
                nc.gpsimd.tensor_tensor(Xrow[:, bass.ts(b, TB), RSTD:RSTD + 1].rearrange("p t w -> p (t w)"), sm[:, 7, :], minus_half[:, 0:TB], ALU.pow).then_inc(S[f]["rstd_ready"], 1)

            def gate_scatter(f, b):
                pool.wait_ge(S[f]["pos_ready"], b + 1)
                for t in range(b * TB, (b + 1) * TB):
                    nc.gpsimd.indirect_dma_start(
                        out=sorted_rows[f], out_offset=bass.IndirectOffsetOnAxis(posi[f][:, t:t + 1], 0),
                        in_=Xrow[:, t, :], in_offset=None).then_inc(S[f]["rows_scattered"], 16)

            def a_products(b, h):
                c = slice(512 * h, 512 * h + 512)
                pool.wait_ge(A["e12_ready"], 2 * b + h + 1)
                pool.wait_ge(A["v_copied"], b + 1)
                nc.gpsimd.tensor_tensor(av[:, c], E2[:, c], vs[:, c], ALU.mult).then_inc(A["av_ready"], 1)
                pool.wait_ge(A["e34_ready"], 2 * b + h + 1)
                own(nc.gpsimd.tensor_tensor(num[:, c], E4[:, c], vs[:, c], ALU.mult))

            def a_numerator(b, h):
                c = slice(512 * h, 512 * h + 512)
                pool.wait_ge(A["scan_ready"], 2 * b + h + 1)
                own(nc.gpsimd.tensor_tensor(av[:, c], E3[:, c], aa[:, c], ALU.mult))
                own(nc.gpsimd.tensor_tensor(num[:, c], num[:, c], av[:, c], ALU.add))

            def a_quotient(b):
                pool.wait_ge(A["y0_ready"], b + 1)
                nc.gpsimd.tensor_tensor(num, num, y0, ALU.mult)
                nc.gpsimd.tensor_tensor(den, den, y0, ALU.mult).then_inc(A["qt_ready"], 1)

            def a_streams(b):
                nc.gpsimd.tensor_tensor(x1, Xrow[:, bass.ts(b, TB), 0:P], x1, ALU.add).then_inc(A["xx_ready"], 1)

            def rstd0(b):
                pool.wait_ge(A["var0_ready"], b + 1)
                power(sma[:, 6, :], sma[:, 8, :]).then_inc(A["scale0_ready"], 1)
                power(sma[:, 5, :], sma[:, 7, :]).then_inc(A["rstd0_ready"], 1)

            def rstd1(b):
                pool.wait_ge(A["var1_ready"], b + 1)
                power(smx[:, 5, :], smx[:, 7, :]).then_inc(A["scale1_ready"], 1)

            def a_body(b, behind=True, ahead=True):
                if behind:
                    rstd1(b - 1)
                if ahead:
                    rstd0(b + 1)
                a_products(b, 0)
                a_products(b, 1)
                if behind:
                    pool.wait_ge(A["x1n_ready"], b)
                a_numerator(b, 0)
                a_numerator(b, 1)
                if behind:
                    a_streams(b - 1)
                a_quotient(b)
                if not ahead:
                    gate_scale(0, 0)

            rstd0(0)
            a_body(0, behind=False)
            start = own.base + own.n
            K = 2 * 3
            with pool.Fori(1, NB - 1) as b:
                own.loop(b - 1, K, start)
                a_body(b)
            own.leave(NB - 2, K, start)
            a_body(NB - 1, ahead=False)
            rstd1(NB - 1)
            gate_scale(0, 1)
            pool.wait_ge(A["x1n_ready"], NB)
            a_streams(NB - 1)

            def b_tables():
                pool.wait_ge(gexp, 1)
                nc.gpsimd.tensor_tensor(G[:].rearrange("p a b r -> p (a b r)"), gam.rearrange("p a b r -> p (a b r)"), expo.rearrange("p a b r -> p (a b r)"), ALU.pow)
                nc.gpsimd.tensor_tensor(g128[:], dcol[:, 1:2], hundred28, ALU.pow).then_inc(gpow, 1)

            def ffn_pool(f, target):
                s_ = S[f]
                gate_scatter(f, 0)
                gate_scale(f, 2)
                gate_scatter(f, 1)
                gate_scale(f, 3)
                gate_scatter(f, 2)
                gate_scatter(f, 3)

                if f == 0:
                    b_tables()
                for s in range(NS):
                    pool.wait_ge(s_["y_ready"], s + 1 + 2)
                    nc.gpsimd.indirect_dma_start(
                        out=target, out_offset=bass.IndirectOffsetOnAxis(x_rows[:, s, ID:ID + 1].bitcast(U32), 0),
                        in_=y_rows[:, s, :], in_offset=None, bounds_check=NT * P - 1,
                        oob_is_err=False).then_inc(s_["y_scattered"], 16)
                pool.wait_ge(s_["y_scattered"], 16 * NS)

            def b_rstd(b):
                pool.wait_ge(V["var_ready"], b + 1)
                power(smb[:, 6, :], smb[:, 8, :]).then_inc(V["scale_ready"], 1)
                own(power(smb[:, 5, :], smb[:, 7, :]))
                pool.wait_ge(V["scale_ready"], b + 1)
                own(nc.gpsimd.tensor_tensor(smb[:, 9, :], smb[:, 8, :], smb[:, 6, :], ALU.mult))
                nc.gpsimd.tensor_tensor(smb[:, 10, :], smb[:, 9, :], smb[:, 5, :], ALU.mult).then_inc(V["back_ready"], 1)

            def b_unit(b):
                pool.wait_ge(V["n2_ready"], b + 1)
                nc.gpsimd.tensor_tensor(rn.rearrange("p t s -> p (t s)"), n2.rearrange("p t s -> p (t s)"), minus_half[:], ALU.pow).then_inc(V["rn_ready"], 1)

            def b_norm2(b):
                pool.wait_ge(V["ms_ready"], b + 1)
                nc.gpsimd.tensor_tensor(smc[:, 12, :], smc[:, 11, :], minus_half[:, 0:TB], ALU.pow).then_inc(V["s2_ready"], 1)

            def b_residual(b):
                pool.wait_ge(V["x3_half"], 2 * b + 1)
                own(nc.gpsimd.tensor_tensor(xh, Xrow[:, bass.ts(b, TB), 0:P], h2, ALU.add))
                nc.gpsimd.tensor_tensor(xh, xh, mb2[:].unsqueeze(1).to_broadcast([P, TB, P]), ALU.add).then_inc(V["xh_ready"], 1)

            def b_body(b, ahead=True):
                if ahead:
                    b_rstd(b + 1)
                else:
                    gate_scale(1, 0)
                b_norm2(b)
                if ahead:
                    b_unit(b + 1)
                else:
                    gate_scale(1, 1)
                b_residual(b)

            ffn_pool(0, x2_rows)
            b_rstd(0)
            b_unit(0)
            b_body(0)
            start = own.base + own.n
            with pool.Fori(1, NB - 1) as b:
                own.loop(b - 1, 3, start)
                b_body(b)
            own.leave(NB - 2, 3, start)
            b_body(NB - 1, ahead=False)
            ffn_pool(1, out)

        @block.vector
        def _(dve):
            own = Chain(dve, dve_own)

            def stats(src, bst, sm, twice=None):
                for t in range(TB):
                    ins = nc.vector.bn_stats(bst[:, t, :], src(t))
                own(ins)

                def part(k):
                    return bst[:, :, k:k + 1].rearrange("p t w -> p (t w)")
                nc.vector.tensor_tensor(sm[:, 1, :], part(1), part(4), ALU.add)
                nc.vector.tensor_tensor(sm[:, 2, :], part(4), part(1), ALU.subtract)
                own(nc.vector.tensor_tensor(sm[:, 3, :], part(2), part(5), ALU.add))
                nc.vector.tensor_scalar(sm[:, 0, :], sm[:, 1, :], 0.5, None, ALU.mult)
                own(nc.vector.scalar_tensor_tensor(sm[:, 2, :], sm[:, 2, :], 0.25 * P, sm[:, 2, :], ALU.mult, ALU.mult))
                own(nc.vector.tensor_tensor(sm[:, 3, :], sm[:, 2, :], sm[:, 3, :], ALU.add))
                nc.vector.tensor_scalar(sm[:, 7, :], sm[:, 3, :], 1.0 / P, EPS, ALU.mult, ALU.add)
                if twice is not None:
                    nc.vector.tensor_scalar(sm[:, 8, :], sm[:, 3, :], (1.0 + twice) / P, twice * EPS, ALU.mult, ALU.add)
                return nc.vector.tensor_scalar(sm[:, 4, :], sm[:, 3, :], 1.0 / P, None, ALU.mult)
            STATS = 4

            def x_tile(b, t, width=P):
                return Xrow[:, bass.ds(b * TB + t, 1), 0:width].rearrange("p a c -> p (a c)")

            def a_tables():
                dve.wait_ge(w_loaded, W_FIRST)
                for n in rest:
                    ins = nc.vector.tensor_scalar(rest[n][:], col[n][:], -1.0, 1.0, ALU.mult, ALU.add)
                own(ins)
                for j, (n, m) in enumerate((("k", "tm_k"), ("v", "tm_v"), ("r", "tm_r"), ("cr", "cm_r"))):
                    nc.vector.tensor_scalar(W_now[n][:], wraw[:, j, :], col[m][:], None, ALU.mult)
                    nc.vector.tensor_scalar(W_shift[n][:], wraw[:, j, :], rest[m][:], None, ALU.mult)
                nc.vector.tensor_scalar(Wo[:], Wo[:], -0.5, None, ALU.mult)
                nc.vector.tensor_tensor(cg[:], col["cm_k"][:], col["ln1_g"][:], ALU.mult)
                nc.vector.tensor_tensor(cb[:], col["cm_k"][:], col["ln1_b"][:], ALU.mult)
                dve.wait_ge(act_setup, 1)
                nc.vector.tensor_scalar(decay[:], decay[:], -1.0, None, ALU.mult).then_inc(tables, 1)
                dve.wait_ge(tables, 1)

            def a_stats(b):
                stats(lambda t: x_tile(b, t), bsta, sma, EPS).then_inc(A["var0_ready"], 1)

            def a_norm0(b):
                dve.wait_ge(A["scale0_ready"], b + 1)
                dve.wait_ge(A["t0_psum"], b + 1)
                for t in range(TB):
                    ins = nc.vector.tensor_scalar(a8[:, t, :], x_tile(b, t), sma[:, 0, t:t + 1], sma[:, 6, t:t + 1], ALU.subtract, ALU.mult)
                ins.then_inc(A["a8_ready"], 1)

            def a_residual(b):
                dve.wait_ge(A["rstd0_ready"], b + 1)
                for t in range(TB):
                    ins = nc.vector.tensor_scalar(Y[:, bass.ds(b * TB + t, 1), :].rearrange("p a c -> p (a c)"), x_tile(b, t), sma[:, 0, t:t + 1], sma[:, 5, t:t + 1], ALU.subtract, ALU.mult)
                own(ins)

            def a_exponents(b):
                for h in range(2):
                    c, c1 = slice(512 * h, 512 * h + 512), slice(512 * h + 1, 512 * h + 513)
                    kp = ps[2 + h][:]
                    dve.wait_ge(A["k_psum"], 2 * b + h + 1)
                    own(nc.vector.tensor_tensor_scan(p_[:, c1], decay[:].to_broadcast([P, 512]), kp, p_[:, 512 * h:512 * h + 1], ALU.add, ALU.max))
                    nc.vector.tensor_tensor(E2[:, c], kp, p_[:, c1], ALU.subtract)
                    nc.vector.scalar_tensor_tensor(E1[:, c], p_[:, c], decay[:], p_[:, c1], ALU.add, ALU.subtract).then_inc(A["d12_ready"], 1)
                    nc.vector.scalar_tensor_tensor(E3[:, c], kp, col["time_first"][:], p_[:, c], ALU.add, ALU.subtract).then_inc(A["s_ready"], 1)

            def a_scans(b, h):
                c, c1 = slice(512 * h, 512 * h + 512), slice(512 * h + 1, 512 * h + 513)
                dve.wait_ge(A["e12_ready"], 2 * b + h + 1)
                nc.vector.tensor_tensor_scan(bb[:, c1], E1[:, c], E2[:, c], bb[:, 512 * h:512 * h + 1] if h else 0.0, ALU.mult, ALU.add)
                dve.wait_ge(A["av_ready"], 2 * b + h + 1)
                nc.vector.tensor_tensor_scan(aa[:, c1], E1[:, c], av[:, c], aa[:, 512 * h:512 * h + 1] if h else 0.0, ALU.mult, ALU.add).then_inc(A["scan_ready"], 1)
                dve.wait_ge(A["scan_ready"], 2 * b + h + 1)
                dve.wait_ge(A["e34_ready"], 2 * b + h + 1)
                own(nc.vector.tensor_tensor(den[:, c], E3[:, c], bb[:, c], ALU.mult))
                nc.vector.tensor_tensor(den[:, c], den[:, c], E4[:, c], ALU.add).then_inc(A["den_ready"], 1)

            def a_rw(b):
                dve.wait_ge(A["qt_ready"], b + 1)
                dve.wait_ge(A["r_tanh"], b + 1)
                own(nc.vector.scalar_tensor_tensor(th, th, 1.0, num, ALU.add, ALU.mult))
                nc.vector.scalar_tensor_tensor(rw, den, -2.0, th, ALU.add, ALU.mult).then_inc(A["rw_ready"], 1)

            def a_x1(b):
                dve.wait_ge(A["x1_done"], b + 1)
                for h in range(2):
                    dve.wait_ge(A["wo_psum"], 2 * b + h + 1 + 1)
                    ins = nc.vector.tensor_tensor(x1[:, 4 * h:4 * h + 4, :], ps[6 + h][:].rearrange("p (t c) -> p t c", c=P),
                                                  Y[:, bass.ds(b * TB + 4 * h, 4), :], ALU.add)
                own(ins)
                stats(lambda t: x1[:, t, :], bsta, smx).then_inc(A["var1_ready"], 1)

            def a_norm1(b):
                dve.wait_ge(A["scale1_ready"], b + 1)
                for t in range(TB):
                    ins = nc.vector.tensor_scalar(x1n[:, t, :], x1[:, t, :], smx[:, 0, t:t + 1], smx[:, 5, t:t + 1], ALU.subtract, ALU.mult)
                ins.then_inc(A["x1n_ready"], 1)

            def a_mix(b):
                dve.wait_ge(A["ca_ready"], b + 1)
                nc.vector.scalar_tensor_tensor(mk, xc[:, 0:L], rest["cm_k"][:], ca, ALU.mult, ALU.add).then_inc(A["mk_ready"], 1)

            def a_final(b):
                dve.wait_ge(A["th2_ready"], b + 2)
                dve.wait_ge(A["xx_ready"], b + 1)
                for h in range(2):
                    dve.wait_ge(A["cv_psum"], 2 * b + h + 1 + 2)
                    t4 = th2[:, 512 * h:512 * h + 512]
                    own(nc.vector.scalar_tensor_tensor(t4, t4, 1.0, ps[2 + h][:], ALU.add, ALU.mult))
                    ins = nc.vector.scalar_tensor_tensor(Xrow[:, bass.ds(b * TB + 4 * h, 4), 0:P], t4.rearrange("p (t c) -> p t c", c=P), 0.5, x1[:, 4 * h:4 * h + 4, :], ALU.mult, ALU.add)
                ins.then_inc(A["x1_done"], 1)

            def a_body(b, behind=True, ahead=True):
                if behind:
                    a_x1(b - 1)
                if ahead:
                    a_stats(b + 1)
                a_exponents(b)
                if behind:
                    a_norm1(b - 1)
                a_scans(b, 0)
                a_scans(b, 1)
                if behind:
                    a_mix(b - 1)
                gate = not ahead
                if ahead:
                    a_norm0(b + 1)
                    a_residual(b + 1)
                if gate:
                    dve.wait_ge(w_loaded2, W_SECOND)
                    dve.wait_ge(A["t0_psum"], NB + 1)
                    gate_stats(0, 0)
                    gate_norm(0, 0)
                a_rw(b)
                if gate:
                    gate_pick(0, 0)
                if behind:
                    a_final(b - 1)
                if gate:
                    gate_slots(0, 0)

            def attn_a():
                dve.wait_ge(x_loaded[0], 16)
                a_stats(0)
                a_norm0(0)
                a_tables()
                a_residual(0)
                for b in range(1, NB):
                    dve.wait_ge(x_loaded[b], 16)
                a_body(0, behind=False)
                start = own.base + own.n
                K = 1 + 2 * STATS + 2 + 2 + 1 + 1 + 2
                with dve.Fori(1, NB - 1) as b:
                    own.loop(b - 1, K, start)
                    a_body(b)
                own.leave(NB - 2, K, start)
                a_body(NB - 1, ahead=False)
                a_x1(NB - 1)
                gate_stats(0, 1)
                a_norm1(NB - 1)
                gate_norm(0, 1)
                a_mix(NB - 1)
                gate_stats(0, 2)
                gate_pick(0, 1)
                gate_slots(0, 1)
                gate_norm(0, 2)
                a_final(NB - 1)
                dve.wait_ge(A["x1_done"], NB + 1)
                gate_stats(0, 3)
                gate_pick(0, 2)
                gate_norm(0, 3)
                gate_slots(0, 2)
                gate_pick(0, 3)
                gate_slots(0, 3)
                gate_tiles(0)

            def gate_stats(f, b):
                s_ = S[f]
                own(stats(lambda t: x_tile(b, t), bst, sm))
                nc.vector.tensor_copy(Xrow[:, bass.ts(b, TB), MEAN:MEAN + 1].rearrange("p t w -> p (t w)"), sm[:, 0, :]).then_inc(s_["ve_ready"], 1)

            def gate_norm(f, b):
                s_ = S[f]
                dve.wait_ge(s_["rstd_ready"], b + 1)
                if b:
                    dve.wait_ge(s_["zt_psum"], b)
                for t in range(TB):
                    row = x_tile(b, t, ROW)
                    ins = nc.vector.tensor_scalar(z8[:, t, :], row[:, 0:P], row[:, MEAN:MEAN + 1], row[:, RSTD:RSTD + 1], ALU.subtract, ALU.mult)
                ins.then_inc(s_["z_ready"], 1)

            def flat(ap):
                return ap.rearrange("p e t -> p (e t)")

            def gate_pick(f, b):
                s_ = S[f]
                bank = gate_bank(f, b)
                dve.wait_ge(s_["logits_done"], b + 1)
                own(nc.vector.tensor_tensor(lg, bank[:, 0:TB * NE].rearrange("p (t e) -> p t e", e=NE), bg[:].unsqueeze(1).to_broadcast([P, TB, NE]), ALU.add))
                own(nc.vector.tensor_reduce(top, lg, AX_X, ALU.max))
                own(nc.vector.tensor_tensor(eq, lg, top.unsqueeze(2).to_broadcast([P, TB, NE]), ALU.is_ge))
                own(nc.vector.tensor_tensor(eq, eq, expert_m8[:].unsqueeze(1).to_broadcast([P, TB, NE]), ALU.mult))
                own(nc.vector.tensor_reduce(top, eq, AX_X, ALU.min))
                if b == 0:
                    nc.vector.tensor_copy(base, region[:])
                nc.vector.tensor_tensor(oh, expert_m8[:].unsqueeze(2).to_broadcast([P, NE, TB]), top.unsqueeze(1).to_broadcast([P, NE, TB]), ALU.is_equal).then_inc(s_["onehot_ready"], 1)

            def gate_slots(f, b):
                s_ = S[f]
                tot = gate_bank(f, b)[:, 2 * NE * TB:3 * NE * TB]
                dve.wait_ge(s_["ranks_done"], b + 1)
                own(nc.vector.tensor_tensor_scan(flat(run), flat(not_first[:]), tot, 0.0, ALU.mult, ALU.add))
                own(nc.vector.tensor_tensor(flat(pos3), flat(run), tot, ALU.subtract))
                own(nc.vector.tensor_tensor(flat(pos3), flat(pos3), gate_bank(f, b)[:, NE * TB:2 * NE * TB], ALU.add))
                own(nc.vector.tensor_tensor(pos3, pos3, base.unsqueeze(2).to_broadcast([P, NE, TB]), ALU.add))
                own(nc.vector.tensor_tensor(pos3, pos3, oh, ALU.mult))
                own(nc.vector.tensor_tensor(base, base, flat(run[:, :, TB - 1:TB]), ALU.add))
                own(nc.vector.tensor_reduce(posf, pos3.rearrange("p e t -> p t e"), AX_X, ALU.add))
                nc.vector.tensor_copy(posi[f][:, b * TB:(b + 1) * TB], posf).then_inc(s_["pos_ready"], 1)

            def gate_tiles(f):
                s_ = S[f]
                own(nc.vector.tensor_tensor(endt, base, region[:], ALU.subtract))
                nc.vector.tensor_copy(tokens[f][:], endt).then_inc(s_["counts_ready"], 1)
                own(nc.vector.tensor_scalar(ntf, endt, float(P - 1), None, ALU.add))
                own(nc.vector.tensor_copy(nti, ntf))
                own(nc.vector.tensor_scalar(nti, nti, 7, None, ALU.arith_shift_right))
                own(nc.vector.tensor_copy(ntf, nti))
                own(nc.vector.tensor_tensor_scan(endt, ones[:, 0:NE], ntf, 0.0, ALU.mult, ALU.add))
                own(nc.vector.tensor_tensor(cmp_, endt.unsqueeze(1).to_broadcast([P, NS, NE]), slot_no[:].unsqueeze(2).to_broadcast([P, NS, NE]), ALU.is_le))
                own(nc.vector.tensor_reduce(texf, cmp_, AX_X, ALU.add))
                own(nc.vector.tensor_scalar(texf, texf, float(NE - 1), None, ALU.min))
                own(nc.vector.tensor_copy(texp[f][:], texf))
                own(nc.vector.tensor_scalar(ntf, ntf, float(-P), float(REGION), ALU.mult, ALU.add))
                own(nc.vector.tensor_tensor(cmp_, cmp_, ntf.unsqueeze(1).to_broadcast([P, NS, NE]), ALU.mult))
                own(nc.vector.tensor_reduce(texf, cmp_, AX_X, ALU.add))
                own(nc.vector.scalar_tensor_tensor(texf, slot_no[:], float(P), texf, ALU.mult, ALU.add))
                own(nc.vector.tensor_scalar(texf, texf, float(SPARE), None, ALU.min))
                nc.vector.tensor_copy(trow[f][:], texf).then_inc(s_["tiles_ready"], 1)
                dve.wait_ge(s_["tiles_ready"], 1)

            def experts(f):
                s_ = S[f]

                def finish(u, g):
                    y = y_rows[:, bass.ds(g, 1), :].rearrange("p a c -> p (a c)")
                    x = x_rows[:, bass.ds(g, 1), 0:P].rearrange("p a c -> p (a c)")
                    dve.wait_ge(s_["y_psum"], g + 1 + U)
                    nc.vector.tensor_tensor(y, ps[Y_BANK[u]][:, 0:P], x, ALU.add).then_inc(s_["y_ready"], 1)

                def turn(i, first):
                    for u in range(U):
                        g = i * U + u
                        if u == 0:
                            dve.wait_ge(loads[f], 16 * U * i + 16 * U)
                        dve.wait_ge(s_["zsT_psum"], g + 1)
                        row = x_rows[:, bass.ds(g, 1), :].rearrange("p a c -> p (a c)")
                        nc.vector.tensor_scalar(zs[u], row[:, 0:P], row[:, MEAN:MEAN + 1], row[:, RSTD:RSTD + 1], ALU.subtract, ALU.mult).then_inc(s_["zs_ready"], 1)
                        dve.wait_ge(s_["h_psum"], g + 1)
                        dve.wait_ge(s_["zsT_psum"], g + 1 + U)
                        nc.vector.tensor_copy(zsT[u], ps[u][:, 0:P]).then_inc(s_["zsT_ready"], 1)
                        if not first:
                            finish(u, g - U)

                turn(0, True)
                with dve.Fori(1, NS // U) as i:
                    turn(i, False)
                for u in range(U):
                    finish(u, NS - U + u)
                own(nc.vector.tensor_copy(posf[:, 0:1], posf[:, 1:2]))

            def b_tables():
                dve.wait_ge(w_loaded2, W_SECOND)
                nc.vector.tensor_scalar(uv[:], uv[:], col["norm1_w"][:], None, ALU.mult)
                nc.vector.tensor_scalar(M1[:], M1[:], col["norm2_w"][:], None, ALU.mult)
                dve.wait_ge(act_setup, 5)
                nc.vector.tensor_scalar(cst[:, 4:5], cst[:, 4:5], 0.5, 0.5, ALU.mult, ALU.add)
                nc.vector.tensor_scalar(dcol[:, 0:1], dcol[:, 0:1], 0.5, 0.5, ALU.mult, ALU.add)
                own(nc.vector.tensor_scalar(dl[:, 0:2], dl[:, 0:2], 0.5, 0.5, ALU.mult, ALU.add))
                nc.vector.tensor_scalar(dcol[:, 1:2], dcol[:, 0:1], 0.15, 1.0, ALU.max, ALU.min)
                nc.vector.tensor_scalar(cst[:, 0:4], cst[:, 0:4], cst[:, 4:5], None, ALU.mult)
                own(nc.vector.tensor_scalar(dl[:, 2], dl[:, 0], 0.15, 1.0, ALU.max, ALU.min))
                g2 = dl[:, 2].unsqueeze(1).to_broadcast([P, 3 * NBLK, R])
                own(nc.vector.tensor_copy(gam.rearrange("p a b r -> p (a b) r"), g2))
                nc.vector.tensor_scalar(gmask[:, 0], expo[:, 0], 0.5 - BLK, None, ALU.is_gt)
                nc.vector.tensor_scalar(gmask[:, 2], expo[:, 1], BLK - 0.5, None, ALU.is_lt)
                own(nc.vector.tensor_scalar(gmask[:, 1], expo[:, 1], -0.5, None, ALU.is_gt))
                own(nc.vector.tensor_tensor(gmask[:, 1], gmask[:, 1], gmask[:, 2], ALU.mult))
                own(nc.vector.tensor_tensor(gmask[:, 1], gmask[:, 1], dl[:, 1].unsqueeze(1).to_broadcast([P, NBLK, R]), ALU.mult))
                nc.vector.tensor_scalar(expo[:, 0], expo[:, 0], float(-BLK), None, ALU.max)
                nc.vector.tensor_scalar(expo[:, 1], expo[:, 1], 0.0, None, ALU.max).then_inc(gexp, 1)
                nc.vector.tensor_scalar(conv[:], dist, 0.0, cst[:, 0:1], ALU.is_equal, ALU.mult)
                own(nc.vector.tensor_scalar(conv_prev[:], dist[:, 0:4], float(1 - P), cst[:, 1:2], ALU.is_equal, ALU.mult))
                for m in range(1, 4):
                    own(nc.vector.tensor_scalar(ctmp, dist, float(m), cst[:, m:m + 1], ALU.is_equal, ALU.mult))
                    own(nc.vector.tensor_tensor(conv[:], conv[:], ctmp, ALU.add))
                    if m > 1:
                        own(nc.vector.tensor_scalar(ctmp[:, 0:4], dist[:, 0:4], float(m - P), cst[:, m:m + 1], ALU.is_equal, ALU.mult))
                        own(nc.vector.tensor_tensor(conv_prev[:], conv_prev[:], ctmp[:, 0:4], ALU.add))

            def b_masks():
                dve.wait_ge(gpow, 1)
                own(nc.vector.tensor_tensor(G[:, 0:2].rearrange("p a b r -> p (a b r)"), G[:, 0:2].rearrange("p a b r -> p (a b r)"), gmask[:, 0:2].rearrange("p a b r -> p (a b r)"), ALU.mult))

            def b_stats(b):
                stats(lambda t: x_tile(b, t), bstb, smb, 1e-6).then_inc(V["var_ready"], 1)

            def b_norm1(b, first=False):
                dve.wait_ge(V["scale_ready"], b + 1)
                if not first:
                    dve.wait_ge(V["hn_held"], b)
                for t in range(TB):
                    ins = nc.vector.tensor_scalar(hna[:, t, :], x_tile(b, t), smb[:, 0, t:t + 1], smb[:, 6, t:t + 1], ALU.subtract, ALU.mult)
                ins.then_inc(V["hn_ready"], 1)

            def b_lengths(b):
                dve.wait_ge(V["qk_copied"], b + 1)
                own(nc.vector.tensor_tensor(sq, qks, qks, ALU.mult))
                own(nc.vector.tensor_reduce(n2, sq, AX_X, ALU.add))
                nc.vector.tensor_scalar(n2, n2, 1e-16, None, ALU.max).then_inc(V["n2_ready"], 1)

            def b_decayed(b):
                dve.wait_ge(V["rn_ready"], b + 1)
                own(nc.vector.tensor_tensor(sq, qks, rn.unsqueeze(3).to_broadcast([P, TB, 2, R]), ALU.mult))
                for dst, qk, table in ((KQ[:, :, 0:64], 1, 0), (KQ[:, :, 64:128], 0, 1), (kd, 1, 2)):
                    ins = nc.vector.tensor_tensor(dst.rearrange("p t (b r) -> p t b r", r=R),
                                                  sq[:, :, qk, :].unsqueeze(2).to_broadcast([P, TB, NBLK, R]),
                                                  G[:, table].unsqueeze(1).to_broadcast([P, TB, NBLK, R]), ALU.mult)
                ins.then_inc(V["kq_ready"], 1)
                dve.wait_ge(V["back_ready"], b + 1)
                own(nc.vector.tensor_copy(smc[:, 13, :], smb[:, 10, :]))

            def b_scores(b):
                for t in range(TB - 1):
                    src = ps[3 + t // 4][0:64, (t % 4) * P:(t % 4 + 1) * P]
                    if t % 4 == 0:
                        dve.wait_ge(V["u_psum"], 2 * b + t // 4 + 1)
                    if t == 0:
                        ins = nc.vector.tensor_copy(state[:, 1, :], src)
                    else:
                        ins = nc.vector.scalar_tensor_tensor(state[:, t + 1, :], state[:, t, :], g128[:], src, ALU.mult, ALU.add)
                    if t == 3 or t == TB - 2:
                        ins.then_inc(V["state_ready"], 1)
                        dve.wait_ge(V["state_ready"], 2 * b + (1 if t == 3 else 2))
                    else:
                        own(ins)
                for h in range(2):
                    dve.wait_ge(V["at_psum"], 2 * b + h + 1)
                    at = AT[:, 4 * h:4 * h + 4, :]
                    own(nc.vector.tensor_tensor(at, ps[2 + h][:].rearrange("p (t c) -> p t c", c=P), causal[:].unsqueeze(1).to_broadcast([P, 4, P]), ALU.mult))
                    nc.vector.tensor_tensor(at, at, conv[:].unsqueeze(1).to_broadcast([P, 4, P]), ALU.add).then_inc(V["at_ready"], 1)

            def b_h2(b, first):
                if not first:
                    dve.wait_ge(V["xh_ready"], b)
                for h in range(2):
                    dve.wait_ge(V["proj_psum"], 2 * b + h + 1)
                    hh = h2[:, 4 * h:4 * h + 4, :]
                    own(nc.vector.tensor_tensor(hh, ps[4 if h == 0 else 2][:].rearrange("p (t c) -> p t c", c=P), pb[:].unsqueeze(1).to_broadcast([P, 4, P]), ALU.add))
                    for t in range(4 * h, 4 * h + 4):
                        ins = nc.vector.scalar_tensor_tensor(h2[:, t, :], hn[:, t, :], smc[:, 13, t:t + 1], h2[:, t, :], ALU.mult, ALU.add)
                own(ins)
                own(stats(lambda t: h2[:, t, :], bstb, smc))
                own(nc.vector.tensor_tensor(smc[:, 10, :], smc[:, 0, :], smc[:, 0, :], ALU.mult))
                nc.vector.scalar_tensor_tensor(smc[:, 11, :], smc[:, 4, :], 1e-6, smc[:, 10, :], ALU.add, ALU.add).then_inc(V["ms_ready"], 1)

            def b_norm2(b):
                dve.wait_ge(V["s2_ready"], b + 1)
                dve.wait_ge(V["t3_psum"], b + 1)
                for t in range(TB):
                    ins = nc.vector.tensor_scalar(h2n[:, t, :], h2[:, t, :], smc[:, 12, t:t + 1], None, ALU.mult)
                ins.then_inc(V["h2n_ready"], 1)

            def b_final(b, h):
                if h == 0:
                    dve.wait_ge(V["xh_ready"], b + 1)
                dve.wait_ge(V["down_psum"], 2 * b + h + 1 + 2)
                x = Xrow[:, bass.ds(b * TB + 4 * h, 4), 0:P]
                ins = nc.vector.tensor_tensor(x, ps[7][:].rearrange("p (t c) -> p t c", c=P), xh[:, 4 * h:4 * h + 4, :], ALU.add)
                ins.then_inc(V["x3_half"], 1)

            def b_body(b, behind=True, ahead=True):
                gate = not ahead
                b_decayed(b)
                if ahead:
                    b_stats(b + 1)
                if gate:
                    dve.wait_ge(V["x3_half"], 2 * 2 + 1)
                    gate_stats(1, 0)
                b_scores(b)
                if ahead:
                    b_norm1(b + 1)
                if gate:
                    gate_norm(1, 0)
                b_h2(b, first=not behind)
                if behind:
                    b_final(b - 1, 0)
                if ahead:
                    b_lengths(b + 1)
                if gate:
                    gate_pick(1, 0)
                    gate_stats(1, 1)
                b_norm2(b)
                if behind:
                    b_final(b - 1, 1)

            dve.wait_ge(consts, 3)
            attn_a()
            dve.wait_ge(w_loaded2, W_SECOND)
            b_tables()
            experts(0)
            b_masks()
            dve.wait_ge(x2_loaded[0], 16)
            b_stats(0)
            b_norm1(0, first=True)
            b_lengths(0)
            for b in range(1, NB):
                dve.wait_ge(x2_loaded[b], 16)
            b_body(0, behind=False)
            start = own.base + own.n
            K = 2 + STATS + (5 + 2) + (3 + STATS + 2) + 2
            with dve.Fori(1, NB - 1) as b:
                own.loop(b - 1, K, start)
                b_body(b)
            own.leave(NB - 2, K, start)
            b_body(NB - 1, ahead=False)
            gate_slots(1, 0)
            gate_norm(1, 1)
            dve.wait_ge(V["x3_half"], 2 * 3 + 1)
            gate_stats(1, 2)
            gate_pick(1, 1)
            b_final(NB - 1, 0)
            gate_slots(1, 1)
            gate_norm(1, 2)
            b_final(NB - 1, 1)
            dve.wait_ge(V["x3_half"], 2 * NB + 1)
            gate_stats(1, 3)
            gate_pick(1, 2)
            gate_norm(1, 3)
            gate_slots(1, 2)
            gate_pick(1, 3)
            gate_slots(1, 3)
            gate_tiles(1)
            dve.wait_ge(V["x3_half"], 2 * NB + 1)
            experts(1)

        @block.scalar
        def _(act):
            own = Chain(act, act_own)

            def gate_turned(f, b):
                s_ = S[f]
                act.wait_ge(s_["zt_psum"], b + 1)
                if b:
                    act.wait_ge(s_["logits_done"], b)
                nc.scalar.copy(z8T[:, 0:512], ps[0][:])
                nc.scalar.copy(z8T[:, 512:1024], ps[1][:]).then_inc(s_["zt_copied"], 1)

            turned = {0: 2, 1: 3}

            def setup_act():
                act.wait_ge(w_loaded, W_FIRST)
                nc.scalar.activation(decay[:], col["time_decay"][:], ACT.Exp).then_inc(act_setup, 1)

            def setup_act2():
                act.wait_ge(w_loaded2, W_SECOND)
                for ap in (dl[:, 0], dl[:, 1], dcol[:, 0:1], cst[:, 4:5]):
                    nc.scalar.activation(ap, ap, ACT.Tanh, scale=0.5).then_inc(act_setup, 1)
                act.wait_ge(proj_turned, 1)
                nc.scalar.activation(projT[:], ps[2][:, 0:P], ACT.Copy, scale=col["norm1_w"][:]).then_inc(proj_ready, 1)

            def a_front(b):
                act.wait_ge(A["t0_psum"], b + 1 + 1)
                for h in range(2):
                    ins = nc.scalar.activation(xa[:, 1 + 512 * h:513 + 512 * h], ps[h][:], ACT.Identity, bias=col["ln0_b"][:], scale=col["ln0_g"][:])
                ins.then_inc(A["xa_ready"], 1)

            def a_v(b):
                for h in range(2):
                    act.wait_ge(A["v_psum"], 2 * b + h + 1)
                    ins = nc.scalar.copy(vs[:, 512 * h:512 * h + 512], ps[4 + h][:])
                ins.then_inc(A["v_copied"], 1)

            def a_r(b):
                for h in range(2):
                    act.wait_ge(A["r_psum"], 2 * b + h + 1)
                    ins = nc.scalar.activation(th[:, 512 * h:512 * h + 512], ps[h][:], ACT.Tanh, scale=0.5)
                ins.then_inc(A["r_tanh"], 1)

            def a_exps(b, h):
                c = slice(512 * h, 512 * h + 512)
                act.wait_ge(A["d12_ready"], 2 * b + h + 1)
                nc.scalar.activation(E1[:, c], E1[:, c], ACT.Exp)
                nc.scalar.activation(E2[:, c], E2[:, c], ACT.Exp).then_inc(A["e12_ready"], 1)
                act.wait_ge(A["s_ready"], 2 * b + h + 1)
                own(nc.scalar.activation(E4[:, c], E3[:, c], ACT.Relu, scale=-1.0))
                own(nc.scalar.activation(E3[:, c], E3[:, c], ACT.Relu))
                nc.scalar.activation(E4[:, c], E4[:, c], ACT.Exp, scale=-1.0)
                nc.scalar.activation(E3[:, c], E3[:, c], ACT.Exp, scale=-1.0).then_inc(A["e34_ready"], 1)

            def a_guess(b):
                act.wait_ge(A["den_ready"], 2 * b + 2)
                own(nc.scalar.activation(y0, den, ACT.Ln))
                nc.scalar.activation(y0, y0, ACT.Exp, scale=-1.0).then_inc(A["y0_ready"], 1)
            A_WKV = 5

            def a_norm1(b):
                act.wait_ge(A["t1_psum"], b + 1)
                for h in range(2):
                    ins = nc.scalar.activation(xc[:, 1 + 512 * h:513 + 512 * h], ps[h][:], ACT.Identity, bias=col["ln1_b"][:], scale=col["ln1_g"][:])
                ins.then_inc(A["xc_ready"], 1)
                for h in range(2):
                    ins = nc.scalar.activation(ca[:, 512 * h:512 * h + 512], ps[h][:], ACT.Identity, bias=cb[:], scale=cg[:])
                ins.then_inc(A["ca_ready"], 1)

            def a_hidden(b, half):
                act.wait_ge(A["cv_psum"], 2 * b + half + 1)
                for k in range(HC):
                    n = b * (2 * HC) + half * HC + k
                    act.wait_ge(A["ck_psum"], n + 1 + 2)
                    act.wait_ge(A["kk_ready"], n + 1)
                    nc.scalar.activation(kkr[k % 2], ps[4 + k % 2][:], ACT.Relu).then_inc(A["relu_ready"], 1)
                    act.wait_ge(A["relu_ready"], n + 1 + 2)
                    nc.scalar.activation(kk2[:, half, k, :], kkr[k % 2], ACT.Square).then_inc(A["kk_ready"], 1)

            def a_gate(b):
                for h in range(2):
                    act.wait_ge(A["cr_psum"], 2 * b + h + 1)
                    ins = nc.scalar.activation(th2[:, 512 * h:512 * h + 512], ps[6 + h][:], ACT.Tanh, scale=0.5)
                ins.then_inc(A["th2_ready"], 1)

            setup_act()
            act.wait_ge(tables, 1)

            def a_body(b, behind=True):
                a_front(b)
                a_exps(b, 0)
                a_v(b)
                a_exps(b, 1)
                a_r(b)
                if behind:
                    a_norm1(b - 1)
                a_guess(b)
                if behind:
                    a_gate(b - 1)
                    a_hidden(b - 1, 0)
                    a_hidden(b - 1, 1)

            a_body(0, behind=False)
            start = own.base + own.n
            with act.Fori(1, NB - 1) as b:
                own.loop(b - 1, A_WKV, start)
                a_body(b)
            own.leave(NB - 2, A_WKV, start)
            a_body(NB - 1)
            gate_turned(0, 0)
            a_norm1(NB - 1)
            a_gate(NB - 1)
            a_hidden(NB - 1, 0)
            gate_turned(0, 1)
            a_hidden(NB - 1, 1)

            def ffn_act(f):
                s_ = S[f]
                for b in range(turned[f], NB):
                    gate_turned(f, b)
                act.wait_ge(s_["counts_ready"], 1)
                for e, n in enumerate(nc.values_load_multi_w_load_instructions(tokens[f][0:1, :], engines=[mybir.EngineType.Activation], min_val=0, max_val=NT * P)[1]):
                    act.dma_start(sorted_rows[f][bass.ds(n + e * REGION, P), :], fill[:]).then_inc(padded[f], 16)
                act.wait_ge(s_["tiles_ready"], 1)
                if f == 0:
                    setup_act2()
                nc.scalar.activation(gelu_dummy[:], bg[0:1, 0:1], ACT.Gelu)

                with act.Fori(0, NS // U) as i:
                    for u in range(U):
                        g = i * U + u
                        e = act.value_load(texp[f][0:1, bass.ds(g, 1)], min_val=0, max_val=NE - 1)
                        act.wait_ge(s_["h_psum"], g + 1 + U)
                        act.wait_ge(s_["y_psum"], g + 1)
                        for k in range(HC):
                            b1 = W1[:, bass.ds(e, 1), HC * P + k:HC * P + k + 1].rearrange("p a c -> p (a c)")
                            ins = nc.scalar.activation(hT[u][:, k, :], ps[3 + u][:, k * P:(k + 1) * P], ACT.Gelu, bias=b1)
                        ins.then_inc(s_["h_ready"], 1)

            def b_qk(b):
                act.wait_ge(V["t1_psum"], b + 1)
                for h in range(2):
                    ins = nc.scalar.copy(hnT[:, 512 * h:512 * h + 512], ps[h][:])
                ins.then_inc(V["hnT_ready"], 1)
                act.wait_ge(V["qk_psum"], b + 1)
                nc.scalar.copy(qks.rearrange("p t s r -> p (t s r)"), ps[3][:, 0:TB * 2 * R]).then_inc(V["qk_copied"], 1)

            def b_turned(b):
                act.wait_ge(V["t2_psum"], b + 1)
                for h in range(2):
                    nc.scalar.copy(kT[:, 512 * h:512 * h + 512], ps[h][0:64, :])
                    ins = nc.scalar.copy(qT[:, 512 * h:512 * h + 512], ps[h][64:128, :])
                ins.then_inc(V["kqT_ready"], 1)

            def b_out(b):
                for h in range(2):
                    act.wait_ge(V["o_psum"], 2 * b + h + 1 + 1)
                    nc.scalar.copy(oT[:, 512 * h:512 * h + 512], ps[h][:]).then_inc(V["oT_ready"], 1)

            def b_h2T(b):
                act.wait_ge(V["t3_psum"], b + 1 + 1)
                for h in range(2):
                    ins = nc.scalar.copy(h2T[:, 512 * h:512 * h + 512], ps[h][:])
                ins.then_inc(V["h2T_ready"], 1)

            def b_mlp(b, h):
                act.wait_ge(V["down_psum"], 2 * b + h + 1)
                for k in range(HC):
                    act.wait_ge(V["up_psum"], 2 * HC * b + HC * h + k + 1)
                    nc.scalar.activation(hmT[:, h, k, :], ps[5 + k % 2][:], ACT.Gelu_apprx_tanh, bias=mb1[:, k:k + 1]).then_inc(V["hm_ready"], 1)

            ffn_act(0)
            def b_body(b, behind=True, ahead=True):
                act.wait_ge(V["hn_ready"], b + 1)
                act.wait_ge(V["t3_psum"], b + 1)
                nc.scalar.copy(hn.rearrange("p t c -> p (t c)"), hna.rearrange("p t c -> p (t c)")).then_inc(V["hn_held"], 1)
                b_turned(b)
                if behind:
                    for h in range(2):
                        b_mlp(b - 1, h)
                b_out(b)
                if ahead:
                    b_qk(b + 1)
                else:
                    gate_turned(1, 0)
                b_h2T(b)

            b_qk(0)
            b_body(0, behind=False)
            nc.scalar.activation(gelu_dummy[:], mb1[0:1, 0:1], ACT.Gelu_apprx_tanh)
            with act.Fori(1, NB - 1) as b:
                b_body(b)
            b_body(NB - 1, ahead=False)
            b_mlp(NB - 1, 0)
            gate_turned(1, 1)
            b_mlp(NB - 1, 1)
            gate_turned(1, 2)
            ffn_act(1)

        @block.tensor
        def _(pe):
            def tiles_turned(src, n=TB):
                for t in range(n):
                    ins = nc.tensor.transpose(ps[t // 4][:, (t % 4) * P:(t % 4 + 1) * P], src[:, t, :], ident[:])
                return ins

            def gate_turn(f, b):
                pe.wait_ge(S[f]["z_ready"], b + 1)
                if b:
                    pe.wait_ge(S[f]["zt_copied"], b)
                tiles_turned(z8).then_inc(S[f]["zt_psum"], 1)

            def gate_logits(f, b):
                pe.wait_ge(S[f]["zt_copied"], b + 1)
                if b:
                    pe.wait_ge(S[f]["pos_ready"], b)
                for t in range(TB):
                    ins = nc.tensor.matmul(gate_bank(f, b)[:, t * NE:(t + 1) * NE], z8T[:, t * P:(t + 1) * P], Wg[:], start=True, stop=True)
                ins.then_inc(S[f]["logits_done"], 1)

            def gate_ranks(f, b):
                pe.wait_ge(S[f]["onehot_ready"], b + 1)
                bank = gate_bank(f, b)
                n = NE * TB
                nc.tensor.matmul(bank[:, n:2 * n], before[:], oh.rearrange("p e t -> p (e t)"), start=True, stop=True)
                nc.tensor.matmul(bank[:, 2 * n:3 * n], ones[:], oh.rearrange("p e t -> p (e t)"), start=True, stop=True).then_inc(S[f]["ranks_done"], 1)

            def a_wo(b):
                pe.wait_ge(A["rw_ready"], b + 1)
                pe.wait_ge(A["th2_ready"], b + 1)
                for h in range(2):
                    for t in range(4):
                        at = (4 * h + t) * P
                        ins = nc.tensor.matmul(ps[6 + h][:, t * P:(t + 1) * P], rw[:, at:at + P], Wo[:], start=True, stop=True)
                    ins.then_inc(A["wo_psum"], 1)

            def a_turn0(b):
                pe.wait_ge(A["a8_ready"], b + 1)
                tiles_turned(a8).then_inc(A["t0_psum"], 1)

            def a_kvr(b, first=False):
                pe.wait_ge(A["xa_ready"], b + 1)
                if not first:
                    pe.wait_ge(A["x1_done"], b)
                for n, bank, done in (("k", 2, A["k_psum"]), ("v", 4, A["v_psum"]), ("r", 0, A["r_psum"])):
                    if n == "v" and not first:
                        pe.wait_ge(A["relu_ready"], 2 * HC * (b - 1) + 2)
                    for h in range(2):
                        nc.tensor.matmul(ps[bank + h][:], W_now[n][:], xa[:, 1 + 512 * h:513 + 512 * h], start=True, stop=False)
                        nc.tensor.matmul(ps[bank + h][:], W_shift[n][:], xa[:, 512 * h:512 + 512 * h], start=False, stop=True).then_inc(done, 1)

            def a_back(b, started, first_gate=False, gate=False):
                pe.wait_ge(A["r_tanh"], started)
                pe.wait_ge(A["x1n_ready"], b + 1)
                if gate:
                    pe.wait_ge(S[0]["pos_ready"], 1)
                tiles_turned(x1n).then_inc(A["t1_psum"], 1)
                pe.wait_ge(A["xc_ready"], b + 1)
                for h in range(2):
                    for t in range(4):
                        at = (4 * h + t) * P
                        nc.tensor.matmul(ps[6 + h][:, t * P:(t + 1) * P], xc[:, 1 + at:1 + at + P], W_now["cr"][:], start=True, stop=False)
                        ins = nc.tensor.matmul(ps[6 + h][:, t * P:(t + 1) * P], xc[:, at:at + P], W_shift["cr"][:], start=False, stop=True)
                    ins.then_inc(A["cr_psum"], 1)
                pe.wait_ge(A["v_copied"], started)
                pe.wait_ge(A["mk_ready"], b + 1)
                for h in range(2):
                    if gate and h == 1:
                        gate_turn(0, 1)
                    for k in range(HC):
                        n = 2 * HC * b + HC * h + k
                        pe.wait_ge(A["relu_ready"], n + 1)
                        nc.tensor.matmul(ps[4 + k % 2][:], Wck[:, k * P:(k + 1) * P], mk[:, 512 * h:512 * h + 512], start=True, stop=True).then_inc(A["ck_psum"], 1)
                pe.wait_ge(A["s_ready"], 2 * started)
                if first_gate:
                    gate_turn(0, 0)
                if gate:
                    pe.wait_ge(A["th2_ready"], NB + 1)
                    gate_logits(0, 1)
                for h in range(2):
                    if first_gate and h == 1:
                        gate_logits(0, 0)
                    if gate and h == 1:
                        gate_ranks(0, 1)
                    pe.wait_ge(A["kk_ready"], 2 * HC * b + HC * h + HC + 2)
                    for t in range(4):
                        for k in range(HC):
                            ins = nc.tensor.matmul(ps[2 + h][:, t * P:(t + 1) * P], kk2[:, h, k, t * P:(t + 1) * P], Wcv[:, k, :], start=(k == 0), stop=(k == HC - 1))
                    ins.then_inc(A["cv_psum"], 1)

            def turn_projection():
                pe.wait_ge(w_loaded2, W_SECOND)
                nc.tensor.transpose(ps[2][:, 0:P], proj_in, ident[:]).then_inc(proj_turned, 1)
                pe.wait_ge(proj_ready, 1)

            def ffn_pe(f):
                s_ = S[f]
                pe.wait_ge(s_["tiles_ready"], 1)
                if f == 0:
                    turn_projection()

                def turn_z(u, g):
                    pe.wait_ge(s_["zs_ready"], g + 1)
                    nc.tensor.transpose(ps[u][:, 0:P], zs[u], ident[:]).then_inc(s_["zsT_psum"], 1)

                def up(u, g, i):
                    pe.wait_ge(s_["zsT_ready"], g + 1)
                    pe.wait_ge(w_loads[f][u], 16 * i + 16)
                    pe.wait_ge(s_["h_ready"], g + 1)
                    for k in range(HC):
                        ins = nc.tensor.matmul(ps[3 + u][:, k * P:(k + 1) * P], w1cur[u][:, k * P:(k + 1) * P], zsT[u], start=True, stop=True)
                    ins.then_inc(s_["h_psum"], 1)

                def down(u, g):
                    e = pe.value_load(texp[f][0:1, bass.ds(g, 1)], min_val=0, max_val=NE - 1)
                    pe.wait_ge(s_["h_ready"], g + 1 + U)
                    pe.wait_ge(s_["y_ready"], g + (2 if u == 0 else 1))
                    nc.tensor.matmul(ps[Y_BANK[u]][:, 0:P], ones[0:1, :], B2[:, bass.ds(e, 1), :].rearrange("p a c -> p (a c)"), start=True, stop=False)
                    for k in range(HC):
                        ins = nc.tensor.matmul(ps[Y_BANK[u]][:, 0:P], hT[u][:, k, :],
                                               W2[:, bass.ds(e, 1), k, :].rearrange("p a c -> p (a c)"), start=False, stop=(k == HC - 1))
                    ins.then_inc(s_["y_psum"], 1)

                def turn(i, first):
                    for u in range(U):
                        g = i * U + u
                        turn_z(u, g)
                        if not (first and u < 1):
                            up((u - 1) % U, g - 1, i - (u == 0))
                        if not (first and u < 2):
                            down((u - 2) % U, g - 2)

                turn(0, True)
                with pe.Fori(1, NS // U) as i:
                    turn(i, False)
                up(U - 1, NS - 1, NS // U - 1)
                down(U - 2, NS - 2)
                down(U - 1, NS - 1)

            def b_turn1(b):
                pe.wait_ge(V["hn_ready"], b + 1)
                tiles_turned(hna).then_inc(V["t1_psum"], 1)

            def b_qk(b):
                pe.wait_ge(V["hnT_ready"], b + 1)
                for t in range(TB):
                    ins = nc.tensor.matmul(ps[3][:, t * 2 * R:(t + 1) * 2 * R], hnT[:, t * P:(t + 1) * P], uv[:], start=True, stop=True)
                ins.then_inc(V["qk_psum"], 1)

            def b_keys(b, first):
                pe.wait_ge(V["kq_ready"], b + 1)
                if not first:
                    pe.wait_ge(V["h2T_ready"], b)
                tiles_turned(KQ).then_inc(V["t2_psum"], 1)
                pe.wait_ge(V["hn_held"], b + 1)
                for t in range(TB - 1):
                    ins = nc.tensor.matmul(ps[3 + t // 4][0:64, (t % 4) * P:(t % 4 + 1) * P], kd[:, t, :], hn[:, t, :], start=True, stop=True)
                    if t % 4 == 3 or t == TB - 2:
                        ins.then_inc(V["u_psum"], 1)

            def b_scores(b):
                pe.wait_ge(V["kqT_ready"], b + 1)
                for h in range(2):
                    if h == 1:
                        pe.wait_ge(V["state_ready"], 2 * b + 1)
                    for t in range(4):
                        at = slice((4 * h + t) * P, (4 * h + t + 1) * P)
                        ins = nc.tensor.matmul(ps[2 + h][:, t * P:(t + 1) * P], kT[:, at], qT[:, at], start=True, stop=True)
                    ins.then_inc(V["at_psum"], 1)

            def b_out(b):
                pe.wait_ge(V["state_ready"], 2 * b + 2)
                for h in range(2):
                    pe.wait_ge(V["at_ready"], 2 * b + h + 1)
                    for t in range(4):
                        c = 4 * h + t
                        o = ps[h][:, t * P:(t + 1) * P]
                        ins = nc.tensor.matmul(o, hn[:, c, :], AT[:, c, :], start=True, stop=(c == 0))
                        if c:
                            nc.tensor.matmul(ps[h][:, t * P:t * P + 4], hn[:, c - 1, :], conv_prev[:], start=False, stop=False)
                            ins = nc.tensor.matmul(o, state[:, c, :], qT[:, c * P:(c + 1) * P], start=False, stop=True)
                    ins.then_inc(V["o_psum"], 1)

            def b_proj(b):
                for h in range(2):
                    pe.wait_ge(V["oT_ready"], 2 * b + h + 1)
                    for t in range(4):
                        at = (4 * h + t) * P
                        ins = nc.tensor.matmul(ps[4 if h == 0 else 2][:, t * P:(t + 1) * P], oT[:, at:at + P], projT[:], start=True, stop=True)
                    ins.then_inc(V["proj_psum"], 1)

            def b_turn3(b):
                pe.wait_ge(V["h2n_ready"], b + 1)
                tiles_turned(h2n).then_inc(V["t3_psum"], 1)

            def b_up(b, h):
                pe.wait_ge(V["h2T_ready"], b + 1)
                for k in range(HC):
                    pe.wait_ge(V["hm_ready"], 2 * HC * b + HC * h + k + 1)
                    nc.tensor.matmul(ps[5 + k % 2][:], M1[:, k * P:(k + 1) * P], h2T[:, 512 * h:512 * h + 512], start=True, stop=True).then_inc(V["up_psum"], 1)

            def b_down(b, h):
                pe.wait_ge(V["hm_ready"], 2 * HC * b + HC * h + HC + 2)
                pe.wait_ge(V["x3_half"], 2 * b + h + 1)
                for t in range(4):
                    for k in range(HC):
                        ins = nc.tensor.matmul(ps[7][:, t * P:(t + 1) * P], hmT[:, h, k, t * P:(t + 1) * P], M2[:, k, :], start=(k == 0), stop=(k == HC - 1))
                ins.then_inc(V["down_psum"], 1)

            def b_body(b, behind=True, ahead=True):
                b_keys(b, first=not behind)
                if behind:
                    b_up(b - 1, 0)
                b_scores(b)
                if behind:
                    b_up(b - 1, 1)
                b_out(b)
                b_proj(b)
                gate = not ahead
                if ahead:
                    b_turn1(b + 1)
                if gate:
                    gate_turn(1, 0)
                if behind:
                    b_down(b - 1, 0)
                if ahead:
                    b_qk(b + 1)
                if gate:
                    gate_logits(1, 0)
                if behind:
                    b_down(b - 1, 1)
                if gate:
                    gate_ranks(1, 0)
                b_turn3(b)

            pe.wait_ge(consts, 3)
            a_turn0(0)
            pe.wait_ge(tables, 1)
            a_kvr(0, first=True)

            def a_body(b, first_gate=False):
                pe.wait_ge(A["r_tanh"], b)
                a_turn0(b)
                a_wo(b - 1)
                a_kvr(b)
                a_back(b - 1, b + 1, first_gate)

            with pe.Fori(1, NB - 1) as b:
                a_body(b)
            a_body(NB - 1, first_gate=True)
            gate_ranks(0, 0)
            a_wo(NB - 1)
            a_back(NB - 1, NB, gate=True)
            for b in range(2, NB):
                gate_turn(0, b)
                gate_logits(0, b)
                gate_ranks(0, b)
            pe.wait_ge(w_loaded2, W_SECOND)
            ffn_pe(0)
            b_turn1(0)
            b_qk(0)
            b_body(0, behind=False)
            with pe.Fori(1, NB - 1) as b:
                b_body(b)
            b_body(NB - 1, ahead=False)
            b_up(NB - 1, 0)
            gate_turn(1, 1)
            b_up(NB - 1, 1)
            gate_logits(1, 1)
            b_down(NB - 1, 0)
            gate_ranks(1, 1)
            b_down(NB - 1, 1)
            gate_turn(1, 2)
            gate_logits(1, 2)
            gate_ranks(1, 2)
            gate_turn(1, 3)
            gate_logits(1, 3)
            gate_ranks(1, 3)
            ffn_pe(1)


_INS = [
    'L0_attn_a_x', 'L0_attn_a_ln0_g', 'L0_attn_a_ln0_b', 'L0_attn_a_ln1_g', 'L0_attn_a_ln1_b', 'L0_attn_a_time_decay',
    'L0_attn_a_time_first', 'L0_attn_a_tm_k', 'L0_attn_a_tm_v', 'L0_attn_a_tm_r', 'L0_attn_a_Wk', 'L0_attn_a_Wv',
    'L0_attn_a_Wr', 'L0_attn_a_Wo', 'L0_attn_a_cm_k', 'L0_attn_a_cm_r', 'L0_attn_a_Wck', 'L0_attn_a_Wcv',
    'L0_attn_a_Wcr', 'L0_attn_b_u', 'L0_attn_b_v', 'L0_attn_b_decay_logit', 'L0_attn_b_alpha_logit',
    'L0_attn_b_k_base_gate_logit', 'L0_attn_b_k_base_kernel', 'L0_attn_b_proj_w', 'L0_attn_b_proj_b',
    'L0_attn_b_norm1_w', 'L0_attn_b_norm2_w', 'L0_attn_b_mlp_w1', 'L0_attn_b_mlp_b1', 'L0_attn_b_mlp_w2',
    'L0_attn_b_mlp_b2', 'L0_ffn_Wg', 'L0_ffn_bg', 'L0_ffn_W1', 'L0_ffn_b1', 'L0_ffn_W2', 'L0_ffn_b2',
]


def kernel(**inputs):
    import numpy as _np
    import concourse.bacc as _bacc
    from concourse import mybir as _mybir
    from concourse.bass_utils import run_bass_kernel_spmd as _run

    nc = _bacc.Bacc("TRN2", target_bir_lowering=False, num_devices=1)
    arrays, aps = {}, {}
    for name in _INS:
        arr = _np.ascontiguousarray(inputs[name])
        shape = arr.shape if arr.ndim and inputs[name].ndim else (1,)
        arrays[f"in_{name}_dram"] = arr.reshape(shape)
        aps[name[3:]] = nc.dram_tensor(f"in_{name}_dram", shape, _mybir.dt.from_np(arr.dtype), kind="ExternalInput").ap()
    out = nc.dram_tensor("out_0_dram", (NT * P, P), F32, kind="ExternalOutput").ap()
    build(nc, aps, out)
    r = _run(nc, [arrays], core_ids=[0])
    return r.results[0]["out_0_dram"].reshape(NB, TB * P, P)
```
